# Optimizing a Trainium2 kernel written in Bass

```python
import numpy as np
import jax
import jax.numpy as jnp

def _softmax(x, axis=-1):
    return jax.nn.softmax(x, axis=axis)

def _gelu(x):
    return jax.nn.gelu(x, approximate=True)

def _silu(x):
    return jax.nn.silu(x)

def _sigmoid(x):
    return jax.nn.sigmoid(x)

def _layernorm(x, axis=-1, eps=1e-05):
    m = jnp.mean(x, axis=axis, keepdims=True)
    v = jnp.var(x, axis=axis, keepdims=True)
    return (x - m) / jnp.sqrt(v + eps)

def _scatter_add(tgt, idx, src, axis=0):
    return tgt.at[idx].add(src)

def _segment_sum(src, seg, n):
    return jax.ops.segment_sum(src, seg, n)
kernel_name = 'mk_seq_postln_d1_jaxref_r8_7585a3'

def setup_inputs(seed: int=0):
    np.random.seed(seed)
    _w = jnp.asarray

    def _L0_attn_setup():
        import jax, jax.numpy as jnp
        import numpy as np
        B, T, D = (2, 256, 256)
        H, G = (32, 8)
        HD = D // H
        GROUP = H // G
        ROPE_BASE = 10000.0

        def _apply_rope(x):
            t = x.shape[2]
            half = HD // 2
            inv_freq = 1.0 / ROPE_BASE ** (jnp.arange(half, dtype=jnp.float32) * 2.0 / HD)
            ang = jnp.arange(t, dtype=jnp.float32)[:, None] * inv_freq[None, :]
            cos, sin = (jnp.cos(ang), jnp.sin(ang))
            x1, x2 = (x[..., :half], x[..., half:])
            out = jnp.concatenate([x1 * cos - x2 * sin, x2 * cos + x1 * sin], axis=-1)
            return out.astype(x.dtype)
        key = jax.random.key(seed)
        kx, kq, kk, kv, ko = jax.random.split(key, 5)
        scale = 0.02
        x = jax.random.normal(kx, (B, T, D), dtype=jnp.float32)
        Wq = jax.random.normal(kq, (D, D), dtype=jnp.float32) * scale
        Wk = jax.random.normal(kk, (D, G * HD), dtype=jnp.float32) * scale
        Wv = jax.random.normal(kv, (D, G * HD), dtype=jnp.float32) * scale
        Wo = jax.random.normal(ko, (D, D), dtype=jnp.float32) * scale
        return {'x': x, 'Wq': Wq, 'Wk': Wk, 'Wv': Wv, 'Wo': Wo}
    _L0_attn_in = _L0_attn_setup()

    def _L0_ffn_setup():
        import jax, jax.numpy as jnp
        import numpy as np
        N_GROUPS = 4
        TOPK_GROUPS = 2
        TOPK = 4
        ROUTE_SCALE = 1.0

        def _gate(xt, gate_w):
            T = xt.shape[0]
            E = gate_w.shape[0]
            scores = jax.nn.sigmoid(xt @ gate_w.T)
            original_scores = scores
            sg = scores.reshape(T, N_GROUPS, E // N_GROUPS)
            group_scores = sg.max(axis=-1)
            _, gidx = jax.lax.top_k(group_scores, TOPK_GROUPS)
            gmask = jax.nn.one_hot(gidx, N_GROUPS, dtype=scores.dtype).sum(axis=1)
            masked = (sg * gmask[:, :, None]).reshape(T, E)
            _, idx = jax.lax.top_k(masked, TOPK)
            w = jnp.take_along_axis(original_scores, idx, axis=-1)
            w = w / w.sum(axis=-1, keepdims=True) * ROUTE_SCALE
            return (w, idx)
        key = jax.random.key(seed)
        ks = jax.random.split(key, 8)
        B, S, D = (1, 256, 256)
        E, I = (16, 176)
        SH = 2 * I
        s = 0.02
        return {'x': jax.random.normal(ks[0], (B, S, D), dtype=jnp.float32), 'gate_w': jax.random.normal(ks[1], (E, D), dtype=jnp.float32) * s, 'W1': jax.random.normal(ks[2], (E, I, D), dtype=jnp.float32) * s, 'W2': jax.random.normal(ks[3], (E, D, I), dtype=jnp.float32) * s, 'W3': jax.random.normal(ks[4], (E, I, D), dtype=jnp.float32) * s, 'Ws1': jax.random.normal(ks[5], (SH, D), dtype=jnp.float32) * s, 'Ws2': jax.random.normal(ks[6], (D, SH), dtype=jnp.float32) * s, 'Ws3': jax.random.normal(ks[7], (SH, D), dtype=jnp.float32) * s}
    _L0_ffn_in = _L0_ffn_setup()
    _d = {'L0_attn_x': _L0_attn_in['x'], 'L0_attn_Wq': _L0_attn_in['Wq'], 'L0_attn_Wk': _L0_attn_in['Wk'], 'L0_attn_Wv': _L0_attn_in['Wv'], 'L0_attn_Wo': _L0_attn_in['Wo'], 'L0_ffn_gate_w': _L0_ffn_in['gate_w'], 'L0_ffn_W1': _L0_ffn_in['W1'], 'L0_ffn_W2': _L0_ffn_in['W2'], 'L0_ffn_W3': _L0_ffn_in['W3'], 'L0_ffn_Ws1': _L0_ffn_in['Ws1'], 'L0_ffn_Ws2': _L0_ffn_in['Ws2'], 'L0_ffn_Ws3': _L0_ffn_in['Ws3']}
    _x0 = _d['L0_attn_x']
    _d['L0_attn_x'] = jax.random.normal(jax.random.fold_in(jax.random.key(seed), 1), (4, 512, 256), dtype=_x0.dtype)
    del _x0
    return _d

def reference(L0_attn_x, L0_attn_Wq, L0_attn_Wk, L0_attn_Wv, L0_attn_Wo, L0_ffn_gate_w, L0_ffn_W1, L0_ffn_W2, L0_ffn_W3, L0_ffn_Ws1, L0_ffn_Ws2, L0_ffn_Ws3):

    def _L0_attn_ref(x, Wq, Wk, Wv, Wo):
        import jax, jax.numpy as jnp
        import numpy as np
        B, T, D = (2, 256, 256)
        H, G = (32, 8)
        HD = D // H
        GROUP = H // G
        ROPE_BASE = 10000.0

        def _apply_rope(x):
            t = x.shape[2]
            half = HD // 2
            inv_freq = 1.0 / ROPE_BASE ** (jnp.arange(half, dtype=jnp.float32) * 2.0 / HD)
            ang = jnp.arange(t, dtype=jnp.float32)[:, None] * inv_freq[None, :]
            cos, sin = (jnp.cos(ang), jnp.sin(ang))
            x1, x2 = (x[..., :half], x[..., half:])
            out = jnp.concatenate([x1 * cos - x2 * sin, x2 * cos + x1 * sin], axis=-1)
            return out.astype(x.dtype)
        b, t, _ = x.shape
        q = (x @ Wq).reshape(b, t, H, HD).transpose(0, 2, 1, 3)
        k = (x @ Wk).reshape(b, t, G, HD).transpose(0, 2, 1, 3)
        v = (x @ Wv).reshape(b, t, G, HD).transpose(0, 2, 1, 3)
        q = _apply_rope(q)
        k = _apply_rope(k)
        k = jnp.repeat(k, GROUP, axis=1)
        v = jnp.repeat(v, GROUP, axis=1)
        scores = jnp.einsum('bhqd,bhkd->bhqk', q, k)
        causal = jnp.triu(jnp.ones((t, t), dtype=bool), k=1)
        scores = jnp.where(causal, -jnp.inf, scores)
        attn = jax.nn.softmax(scores / jnp.sqrt(jnp.float32(HD)), axis=-1)
        ctx = jnp.einsum('bhqk,bhkd->bhqd', attn, v)
        ctx = jnp.swapaxes(ctx, -2, -1).reshape(b, t, D)
        return ctx @ Wo

    def _L0_ffn_ref(x, gate_w, W1, W2, W3, Ws1, Ws2, Ws3):
        import jax, jax.numpy as jnp
        import numpy as np
        N_GROUPS = 4
        TOPK_GROUPS = 2
        TOPK = 4
        ROUTE_SCALE = 1.0

        def _gate(xt, gate_w):
            T = xt.shape[0]
            E = gate_w.shape[0]
            scores = jax.nn.sigmoid(xt @ gate_w.T)
            original_scores = scores
            sg = scores.reshape(T, N_GROUPS, E // N_GROUPS)
            group_scores = sg.max(axis=-1)
            _, gidx = jax.lax.top_k(group_scores, TOPK_GROUPS)
            gmask = jax.nn.one_hot(gidx, N_GROUPS, dtype=scores.dtype).sum(axis=1)
            masked = (sg * gmask[:, :, None]).reshape(T, E)
            _, idx = jax.lax.top_k(masked, TOPK)
            w = jnp.take_along_axis(original_scores, idx, axis=-1)
            w = w / w.sum(axis=-1, keepdims=True) * ROUTE_SCALE
            return (w, idx)
        shape = x.shape
        D = shape[-1]
        xt = x.reshape(-1, D)
        E = W1.shape[0]
        weights, indices = _gate(xt, gate_w)
        combine = jnp.einsum('tk,tke->te', weights, jax.nn.one_hot(indices, E, dtype=weights.dtype))
        h1 = jnp.einsum('td,eid->tei', xt, W1)
        h3 = jnp.einsum('td,eid->tei', xt, W3)
        g = jax.nn.silu(h1) * h3 * combine[:, :, None]
        y = jnp.einsum('tei,edi->td', g, W2)
        z = jax.nn.silu(xt @ Ws1.T) * (xt @ Ws3.T) @ Ws2.T
        return (y + z).reshape(shape)
    x = L0_attn_x
    x = _layernorm(x + _L0_attn_ref(x, L0_attn_Wq, L0_attn_Wk, L0_attn_Wv, L0_attn_Wo), axis=-1)
    x = _layernorm(x + _L0_ffn_ref(x, L0_ffn_gate_w, L0_ffn_W1, L0_ffn_W2, L0_ffn_W3, L0_ffn_Ws1, L0_ffn_Ws2, L0_ffn_Ws3), axis=-1)
    return x

_drawn_inputs = setup_inputs


def setup_inputs(seed=0):
    import zlib

    import numpy as np

    out = dict(_drawn_inputs(seed))
    spreads = {}
    factors = {'L0_attn_Wq': 8.0,
     'L0_attn_Wk': 8.0,
     'L0_attn_Wv': 4.57,
     'L0_attn_Wo': 4.854,
     'L0_ffn_gate_w': 8.0,
     'L0_ffn_W1': 8.0,
     'L0_ffn_W2': 8.0,
     'L0_ffn_W3': 8.0,
     'L0_ffn_Ws1': 2.893,
     'L0_ffn_Ws2': 2.869,
     'L0_ffn_Ws3': 2.863}
    for name, (base, spread) in spreads.items():
        noise = np.random.default_rng([zlib.crc32(name.encode()), seed]).standard_normal(out[name].shape)
        drawn = base * np.exp(spread * noise) if base else spread * noise
        out[name] = jnp.asarray(drawn.astype(out[name].dtype))
    for name, factor in factors.items():
        out[name] = (out[name] * factor).astype(out[name].dtype)
    return out
```

```python
from contextlib import ExitStack

import concourse.bass as bass
from concourse import mybir

F32 = mybir.dt.float32
BF16 = mybir.dt.bfloat16
U32 = mybir.dt.uint32
ALU = mybir.AluOpType
ACT = mybir.ActivationFunctionType
AXX = mybir.AxisListType.X
ds = bass.ds

P = 128
NB, T, D = 4, 512, 256
H, G, HD = 32, 8, 8
GH = H // G
QT = T // P
KC = D // P
NT = NB * T // P
E, I = 16, 176
NE = E + 2
IH = I // 2
PARTS = 3
ROWS = PARTS * PARTS * HD
KROWS = ROWS + PARTS
SLOTS = 2 * G
NEG = -3.0e38
EPS = 1e-5
SCALE = float(HD) ** -0.5
TOPK = 4
TJ = NT * TOPK
TOKENS = NB * T
TILES = (TOKENS * TOPK + E * (P - 1)) // P
HI = TILES + 1
PAD = TOKENS
UNITS = 2 * NT
CH = 4

S1_TILES = 12
S2_TILES = 6
S1 = [(0, 0, 2), (0, 2, 2), (1, 0, 2), (1, 2, 2)] + [(q, h, 1) for q in (2, 3) for h in range(GH)]
S2 = [(0, 0, 2), (0, 2, 2), (1, 0, 2), (1, 2, 2), (2, 0, 4), (3, 0, 4)]


def program(nc, x, xT, wqkv, wo, cos, sin, gateT, w13, w2, out):
    q_scr = nc.dram_tensor("q_parts", (NB, PARTS, HD, H, T), BF16, kind="Internal").ap()
    k_scr = nc.dram_tensor("k_parts", (NB, PARTS, HD, G, T), BF16, kind="Internal").ap()
    x1_scr = nc.dram_tensor("x1_rows", (TOKENS + P, D), F32, kind="Internal").ap()
    acc = [nc.dram_tensor(f"acc{i}", (TOKENS + P, D), F32, kind="Internal").ap() for i in range(2)]
    with ExitStack() as ctx:
        def sb(name, shape, dt=F32):
            return ctx.enter_context(nc.sbuf_tensor(name, shape, dt))

        def psum(name, shape):
            return ctx.enter_context(nc.psum_tensor(name, shape, F32))

        def sem(name):
            return ctx.enter_context(nc.semaphore(name))

        EARLY = sb("EARLY", [P, KC * TOKENS])
        WQ = EARLY[:, 0:KC * 704].rearrange("p (c n) -> p c n", c=KC)
        COS = EARLY[:, KC * 704:KC * 704 + T]
        SIN = EARLY[:, KC * 704 + T:KC * 704 + 2 * T]
        x1T = EARLY[:, :].rearrange("p (c t) -> p c t", c=KC)
        WO = sb("WO", [P, KC, D])
        GT = sb("GT", [P, KC, E])
        XT = sb("XT", [P, KC * NB * T])
        xT_sb = XT[:, :].rearrange("p (c t) -> p c t", c=KC)
        X1 = XT[:, :].rearrange("p (n d) -> p n d", n=NT)
        QS = sb("QS", [P, SLOTS * GH * T // 2])
        qs = QS[:, :].bitcast(BF16).rearrange("p (s h t) -> p s h t", s=SLOTS, h=GH)
        w2_sb = QS[0:IH, 0:E * 2 * D].rearrange("p (e c d) -> p e c d", e=E, c=2)
        KS = sb("KS", [P, SLOTS, T], BF16)
        w2s_sb = KS[0:IH, 0:G // 2, :].rearrange("p s t -> p (s t)").bitcast(F32).rearrange(
            "p (e c d) -> p e c d", e=2, c=2)
        W13 = sb("W13", [P, KC * NE * 2 * I])
        w13_sb = W13[:, :].rearrange("p (c e n) -> p c e n", c=KC, e=NE)
        rope_t = W13[:, 0:2 * 4 * T].rearrange("p (u k t) -> p u k t", u=2, k=4)
        parts = W13[:, 2 * 4 * T:2 * 4 * T + 2 * PARTS * T // 2].bitcast(BF16).rearrange(
            "p (u a t) -> p u a t", u=2, a=PARTS)
        VA = sb("VA", [P, NT, G * HD])
        VC = sb("VC", [P, QT, 32])
        ATT = sb("ATT", [P, GH * sum(T - P * k for k in range(QT))])
        PT, at = [], 0
        for k in range(QT):
            PT.append(ATT[:, at:at + GH * (T - P * k)].rearrange("p (h t) -> p h t", h=GH))
            at += GH * (T - P * k)
        PVS = sb("PVS", [P, T])
        RC = sb("RC", [P, QT, GH])
        CTX = sb("CTX", [P, QT, D])
        NM = sb("NM", [P, QT, H])
        NR = sb("NR", [P, 2, QT, H])
        NS = sb("NS", [P, QT, PARTS, H], BF16)
        MR = sb("MR", [PARTS * H, T], BF16)
        IDF = sb("IDF", [P, P])
        IDB = sb("IDB", [P, P], BF16)
        MQ = sb("MQ", [P, GH, P], BF16)
        MK = sb("MK", [P, GH, P], BF16)
        EPSC = sb("EPSC", [P, 1])
        ST = sb("ST", [P, QT, 6])
        MV = sb("MV", [P, NT, 2])
        SD = sb("SD", [P, NT])
        RSTD = sb("RSTD", [P, NT])
        def taker(region):
            at = [0]

            def take(*shape, dt=F32, rows=P):
                n = 1
                for d in shape:
                    n *= d
                view = region[0:rows, at[0]:at[0] + n]
                at[0] += n
                names = [f"x{i}" for i in range(len(shape))]
                if len(shape) > 1:
                    view = view.rearrange(f"p ({' '.join(names)}) -> p {' '.join(names)}",
                                          **{m: d for m, d in zip(names[1:], shape[1:])})
                return view if dt == F32 else view.bitcast(dt)
            return take

        in_att = taker(ATT)
        XS = [in_att(D) for _ in range(4)]
        YS = [in_att(D) for _ in range(4)]
        GG = [in_att(I) for _ in range(2)]
        SILU = [in_att(I) for _ in range(2)]
        GTS = [in_att(2, P, rows=IH) for _ in range(2)]
        XTS = [in_att(KC, P) for _ in range(2)]
        SC = in_att(NT, E)
        MSK = in_att(NT, E)
        GS = in_att(NT, 4)
        GR = in_att(NT, 4)
        GA = in_att(NT, 4, 4)
        GB = in_att(NT, 4, 4)
        in_qs = taker(QS[:, SLOTS * GH * T // 4:SLOTS * GH * T // 2])
        OHJ = in_qs(NT, TOPK, E)
        TMJ = in_qs(NT, TOPK, E)
        OHLO = in_qs(CH * TOPK, P)
        OHHI = in_qs(CH * TOPK, HI)
        RH = in_qs(CH * TOPK, 2 * HI)
        POS = in_qs(NT, E)
        in_ctx = taker(CTX[:, :, :].rearrange("p q d -> p (q d)"))
        TOP = in_ctx(NT, 8)
        TOPI = in_ctx(NT, 8, dt=U32)
        TOPF = in_ctx(NT, 8)
        WJ = in_ctx(NT, TOPK)
        WSUM = in_ctx(NT)
        WREC = in_ctx(NT)
        PJ = in_ctx(TJ)
        PU = in_ctx(TJ, dt=U32)
        HU = in_ctx(TJ, dt=U32)
        LU = in_ctx(TJ, dt=U32)
        HF = in_ctx(TJ)
        LF = in_ctx(TJ)
        NEXP = in_ctx(E)
        KEXP = in_ctx(E)
        BASE = in_ctx(E)
        ENDS = in_ctx(E)
        in_pvs = taker(PVS)
        IDXF = in_pvs(HI)
        EMPTY = in_pvs(HI)
        IDX = sb("IDX", [P, HI], U32)
        WT = sb("WT", [P, HI])
        EOTF = sb("EOTF", [P, HI])
        EOT = sb("EOT", [P, HI], U32)
        MB = sb("MB", [P, NT, E], BF16)
        LOWER = sb("LOWER", [P, 4, 4])
        LOWER16 = sb("LOWER16", [P, E, E])
        IOTA = sb("IOTA", [P, P])
        TID1 = sb("TID1", [P, NT, TOPK])
        PADROW = sb("PADROW", [P, 1])
        UPPER = sb("UPPER", [P, P], BF16)
        ONES = sb("ONES", [P, P], BF16)

        S1P = [psum(f"S1P{i}", [P, T]) for i in range(2)]
        S2P = [psum(f"S2P{i}", [P, 2, T]) for i in range(2)]
        PVP = psum("PVP", [P, T])
        MIS = psum("MIS", [P, T])
        HP = [S2P[0][:, i, :] for i in range(2)]
        TGP = [S2P[1][:, i, :] for i in range(2)]
        YP = [S1P[i] for i in range(2)]
        TXP = [PVP, MIS]

        ld_x = sem("ld_x"); ld_w = sem("ld_w"); ld_tab = sem("ld_tab")
        ld_res = sem("ld_res"); ld_w13 = sem("ld_w13"); ld_w2 = sem("ld_w2")
        consts_ready = sem("consts_ready")
        ones_ready = sem("ones_ready")
        proj_ready = sem("proj_ready")
        proj_used = sem("proj_used")
        v_ready = sem("v_ready"); v_used = sem("v_used")
        rot_ready = sem("rot_ready")
        hi_ready = sem("hi_ready")
        rest1_ready = sem("rest1_ready")
        mid_ready = sem("mid_ready")
        lo_ready = sem("lo_ready")
        scr_done = [sem("scr_done0"), sem("scr_done1")]
        stack = [[sem(f"stack{p}{h}") for h in range(2)] for p in range(2)]
        s1_ready = sem("s1_ready"); s1_free = sem("s1_free")
        s2_ready = sem("s2_ready"); exp_done = sem("exp_done")
        vc_ready = sem("vc_ready"); vc_init = sem("vc_init")
        pv_done = sem("pv_done"); pvs_ready = sem("pvs_ready")
        ctxT_ready = sem("ctxT_ready"); norm_done = sem("norm_done")
        dve_step = sem("dve_step")
        ns_ready = sem("ns_ready"); mrT_ready = sem("mrT_ready"); mr_ready = sem("mr_ready")
        mrow = [sem("mrow0"), sem("mrow1")]
        oproj_ready = sem("oproj_ready"); oproj_used = sem("oproj_used")
        var_ready = sem("var_ready"); std_ready = sem("std_ready")
        x1_ready = sem("x1_ready")
        zero_ready = sem("zero_ready"); zeroed = sem("zeroed")
        x1T_ready = sem("x1T_ready"); x1T_copied = sem("x1T_copied")
        x1_out = [sem(f"x1_out{b}") for b in range(NB)]; res_out = sem("res_out")
        logits_ready = sem("logits_ready"); score_ready = sem("score_ready")
        mb_ready = sem("mb_ready"); pre_ready = sem("pre_ready")
        onehot_ready = sem("onehot_ready"); tab_used = sem("tab_used"); tab_ready = sem("tab_ready")
        wprod_ready = sem("wprod_ready"); hi_made = sem("hi_made")
        idx_ready = sem("idx_ready")
        sh_h = sem("sh_h"); sh_silu = sem("sh_silu"); sh_g = sem("sh_g")
        sh_gT = sem("sh_gT"); sh_gts = sem("sh_gts"); sh_y = sem("sh_y"); sh_yused = sem("sh_yused")
        xs_in = [sem(f"xs_in{i}") for i in range(4)]
        xT_ready = sem("xT_ready"); xts_ready = sem("xts_ready")
        h_ready = sem("h_ready"); silu_ready = sem("silu_ready"); g_ready = sem("g_ready")
        gT_ready = sem("gT_ready"); gts_ready = sem("gts_ready")
        y_ready = sem("y_ready"); ys_ready = sem("ys_ready")
        acc_done = [sem(f"acc_done{i}") for i in range(2)]
        acc_in = [sem(f"acc_in{i}") for i in range(4)]
        out_ready = sem("out_ready"); out_done = sem("out_done")

        FIN = [W13[:, i * NT * D:(i + 1) * NT * D].rearrange("p (n d) -> p n d", n=NT) for i in range(2)]

        block = ctx.enter_context(nc.Block())

        x_tiles = x.rearrange("(n p q) d -> p n (q d)", p=P, q=2)
        out_tiles = out.rearrange("(n p q) d -> p n q d", p=P, q=2)

        def load_stacks(eng, b, half):
            p, g0, n = b % 2, half * 4, 4
            s0 = p * G + g0
            for a in range(PARTS):
                src = q_scr[b, a].rearrange("d h t -> d (h t)")[:, g0 * GH * T:(g0 + n) * GH * T]
                src = bass.AP(tensor=src.tensor, offset=src.offset, ap=[[0, PARTS]] + list(src.ap))
                dst = qs[a * 24:(a + 1) * 24, s0:s0 + n, :, :].rearrange("p s h t -> p (s h t)")
                eng.dma_start(dst, src).then_inc(stack[p][half], 16)
            src = k_scr[b].rearrange("c d g t -> (c d) (g t)")[:, g0 * T:(g0 + n) * T]
            src = bass.AP(tensor=src.tensor, offset=src.offset, ap=[[0, PARTS]] + list(src.ap))
            eng.dma_start(KS[0:ROWS, s0:s0 + n, :].rearrange("p s t -> p (s t)"), src).then_inc(
                stack[p][half], 16)

        def stacks_here(eng, b, half):
            eng.wait_ge(stack[b % 2][half], 64 * (b // 2 + 1))

        @block.sync
        def _(sp):
            sp.dma_start(WQ, wqkv.rearrange("(c p) n -> p c n", p=P)).then_inc(ld_w, 16)
            sp.dma_start(xT_sb, xT.rearrange("(c p) t -> p c t", p=P)).then_inc(ld_x, 16)
            sp.dma_start(COS, cos).then_inc(ld_tab, 16)
            sp.dma_start(SIN, sin).then_inc(ld_tab, 16)
            sp.dma_start(WO[:, :, :], wo.rearrange("(c p) n -> p c n", p=P)).then_inc(ld_w, 16)
            sp.dma_start(GT[:, :, :], gateT.rearrange("(c p) n -> p c n", p=P)).then_inc(ld_w, 16)
            sp.wait_ge(zero_ready, 1)
            ctx0 = CTX[:, 0, :]
            zero = bass.AP(tensor=ctx0.tensor, offset=ctx0.offset, ap=[ctx0.ap[0], [0, NT + 1], ctx0.ap[1]])
            sp.dma_start(acc[1].rearrange("(t p) d -> p t d", p=P), zero).then_inc(zeroed, 16)
            for rows in (acc[0], x1_scr):
                sp.dma_start(rows[PAD:PAD + P, :], CTX[:, 0, :]).then_inc(zeroed, 16)
            for b in range(NB):
                for m in range(3):
                    u = 3 * b + m
                    sp.wait_ge(lo_ready, u + 1)
                    for a in range(PARTS):
                        if m < 2:
                            sp.dma_start(q_scr[b, a, :, m * 16:(m + 1) * 16, :].rearrange("d h t -> h d t"),
                                         parts[:, u % 2, a, :]).then_inc(scr_done[u % 2], 16)
                        else:
                            sp.dma_start(k_scr[b, a].rearrange("d h t -> h d t"),
                                         parts[0:64, u % 2, a, :]).then_inc(scr_done[u % 2], 16)
                if b == 0:
                    sp.wait_ge(ones_ready, 1)
                if b < 2:
                    for par in range(2):
                        sp.wait_ge(scr_done[par], 48 * len([u for u in range(3 * b + 3) if u % 2 == par]))
                    load_stacks(sp, b, 0)
                    load_stacks(sp, b, 1)
            for par in range(2):
                sp.wait_ge(scr_done[par], 48 * 6)
            sp.wait_ge(v_ready, NB)
            sp.dma_start(XT[:, :].rearrange("p (n d) -> p n d", n=NT // 2), x_tiles).then_inc(ld_res, 16)
            sp.dma_start(w13_sb, w13.rearrange("(c p) e n -> p c e n", p=P)).then_inc(ld_w13, 16)
            for b in range(NB):
                sp.wait_ge(mr_ready, b + 1)
                for a in range(PARTS):
                    sp.dma_start(qs[ROWS + a:ROWS + a + 1, (b % 2) * G:(b % 2 + 1) * G, :, :].rearrange(
                        "p s h t -> p (s h) t"), MR[a * H:(a + 1) * H, :]).then_inc(mrow[b % 2], 16)
                if b >= 1:
                    sp.wait_ge(x1_ready, b)
                    sp.dma_start(x1_scr[(b - 1) * T:b * T, :].rearrange("(t p) d -> p t d", p=P),
                                 X1[:, 4 * b - 4:4 * b, :]).then_inc(x1_out[b - 1], 16)
                if b < 2:
                    for half in range(2):
                        sp.wait_ge(s2_ready, S2_TILES * (8 * b + 4 * (half + 1)))
                        load_stacks(sp, b + 2, half)
                if b == 2:
                    sp.wait_ge(s2_ready, S2_TILES * 3 * G)
                    sp.dma_start(w2_sb, w2[:, 0:E, :, :]).then_inc(ld_w2, 16)
                    sp.dma_start(w2s_sb, w2[:, E:NE, :, :]).then_inc(ld_w2, 16)
            sp.wait_ge(x1_ready, NB)
            sp.dma_start(x1_scr[3 * T:4 * T, :].rearrange("(t p) d -> p t d", p=P),
                         X1[:, 12:16, :]).then_inc(x1_out[3], 16)
            sp.wait_ge(sh_yused, NT)
            sp.dma_start(acc[0][0:TOKENS, :].rearrange("(t p) d -> p t d", p=P), X1[:, :, :]).then_inc(
                res_out, 16)
            sp.wait_ge(acc_done[0], 16 * ((TILES + 1) // 2))
            sp.wait_ge(acc_done[1], 16 * (TILES // 2))
            sp.wait_ge(res_out, 16)
            for q in range(4):
                for a in range(2):
                    sp.dma_start(FIN[a][:, 4 * q:4 * q + 4, :],
                                 acc[a][q * T:(q + 1) * T, :].rearrange("(t p) d -> p t d", p=P)).then_inc(
                                     acc_in[q], 16)
            for b in range(NB):
                sp.wait_ge(out_ready, b + 1)
                for q in range(2):
                    sp.dma_start(out_tiles[:, 2 * b:2 * b + 2, q, :], X1[:, 4 * b + q:4 * b + 4:2, :]).then_inc(
                        out_done, 16)
            sp.wait_ge(out_done, 16 * 2 * NB)

        @block.gpsimd
        def _(pool):
            nc.gpsimd.memset(IDF[:, :], 0.0).then_inc(consts_ready, 1)
            nc.gpsimd.memset(IDB[:, :], 0.0).then_inc(consts_ready, 1)
            nc.gpsimd.memset(MQ[:, :, :], 0.0).then_inc(consts_ready, 1)
            nc.gpsimd.memset(MK[:, :, :], 0.0).then_inc(consts_ready, 1)
            nc.gpsimd.memset(EPSC[:, :], EPS).then_inc(consts_ready, 1)
            nc.gpsimd.memset(LOWER[:, :, :], 0.0).then_inc(consts_ready, 1)
            nc.gpsimd.iota(IOTA[:, :], pattern=[[1, P]], base=0, channel_multiplier=0,
                           allow_small_or_imprecise_dtypes=True).then_inc(consts_ready, 1)
            nc.gpsimd.iota(TID1[:, :, :], pattern=[[P, NT], [0, TOPK]], base=1, channel_multiplier=1,
                           allow_small_or_imprecise_dtypes=True).then_inc(consts_ready, 1)
            nc.gpsimd.iota(PADROW[:, :], pattern=[[0, 1]], base=PAD + 1, channel_multiplier=1,
                           allow_small_or_imprecise_dtypes=True).then_inc(consts_ready, 1)
            nc.gpsimd.memset(LOWER16[:, :, :], 0.0).then_inc(consts_ready, 1)
            nc.gpsimd.memset(UPPER[:, :], 0.0).then_inc(consts_ready, 1)
            nc.gpsimd.memset(ONES[:, :], 1.0).then_inc(consts_ready, 1)
            nc.gpsimd.memset(VC[:, :, HD + 1:32], 0.0).then_inc(vc_init, 1)
            nc.gpsimd.memset(VC[:, :, HD:HD + 1], 1.0).then_inc(vc_init, 1)
            pool.wait_ge(consts_ready, 12)
            for m in (IDF, IDB):
                nc.gpsimd.affine_select(out=m[:, :], in_=m[:, :], compare_op=ALU.not_equal, fill=1.0, base=0,
                                        pattern=[[-1, P]], channel_multiplier=1).then_inc(consts_ready, 1)
            nc.gpsimd.affine_select(out=MQ[:, :, :], in_=MQ[:, :, :], compare_op=ALU.is_ge, fill=NEG, base=0,
                                    pattern=[[0, GH], [-1, P]], channel_multiplier=1).then_inc(consts_ready, 1)
            nc.gpsimd.affine_select(out=MK[:, :, :], in_=MK[:, :, :], compare_op=ALU.is_ge, fill=NEG, base=0,
                                    pattern=[[0, GH], [1, P]], channel_multiplier=-1).then_inc(consts_ready, 1)
            nc.gpsimd.affine_select(out=LOWER[:, :, :], in_=LOWER[:, :, :], compare_op=ALU.is_ge, fill=1.0,
                                    base=0, pattern=[[-1, 4], [1, 4]], channel_multiplier=0).then_inc(
                                        consts_ready, 1)
            nc.gpsimd.affine_select(out=LOWER16[:, :, :], in_=LOWER16[:, :, :], compare_op=ALU.is_ge, fill=1.0,
                                    base=0, pattern=[[-1, E], [1, E]], channel_multiplier=0).then_inc(
                                        consts_ready, 1)
            nc.gpsimd.affine_select(out=UPPER[:, :], in_=UPPER[:, :], compare_op=ALU.is_ge, fill=1.0, base=0,
                                    pattern=[[-1, P]], channel_multiplier=1).then_inc(consts_ready, 1)
            pool.wait_ge(consts_ready, 19)
            nc.gpsimd.memset(KS[64:96, :, :], 1.0).then_inc(ones_ready, 1)
            pool.wait_ge(ones_ready, 1)
            for u in range(3 * NB):
                n = P if u % 3 < 2 else 64
                pool.wait_ge(mid_ready, u + 1)
                nc.gpsimd.tensor_tensor(parts[0:n, u % 2, 2, :], rope_t[0:n, u % 2, 3, :],
                                        parts[0:n, u % 2, 1, :], ALU.subtract).then_inc(lo_ready, 1)
            pool.wait_ge(vc_init, 2)
            for b in range(NB):
                pool.wait_ge(v_used, b + 1)
                with pool.Fori(0, G) as g:
                    pool.wait_ge(pv_done, (g + 8 * b) * 4 + 4)
                    nc.gpsimd.tensor_copy(VC[:, :, 0:HD],
                                          VA[:, b * QT:(b + 1) * QT, ds(g * HD, HD)]).then_inc(vc_ready, 1)
            for c in range(NT // CH):
                pool.wait_ge(hi_made, c + 1)
                nc.gpsimd.tensor_tensor(RH[:, :, HI:2 * HI], OHHI,
                                        WJ.rearrange("p t j -> p (t j)")[:, c * CH * TOPK:(c + 1) * CH * TOPK]
                                        .unsqueeze(2).broadcast_to([P, CH * TOPK, HI]),
                                        ALU.mult).then_inc(wprod_ready, 1)
            pool.wait_ge(idx_ready, 1)
            for b in range(NB):
                pool.wait_ge(x1_out[b], 16)
            pool.wait_ge(res_out, 16)
            pool.wait_ge(zeroed, 48)
            AHEAD = 5
            for n in range(TILES + AHEAD):
                if n < TILES:
                    if n >= 4:
                        pool.wait_ge(xT_ready, n - 3)
                    nc.gpsimd.indirect_dma_start(XS[n % 4], None, x1_scr,
                                                 bass.IndirectOffsetOnAxis(IDX[:, n:n + 1], 0)).then_inc(
                                                     xs_in[n % 4], 16)
                m = n - AHEAD
                if m >= 0:
                    if m >= 2:
                        pool.wait_ge(acc_done[m % 2], 16 * (m // 2))
                    pool.wait_ge(ys_ready, m + 3)
                    nc.gpsimd.indirect_dma_start(acc[m % 2], bass.IndirectOffsetOnAxis(IDX[:, m:m + 1], 0),
                                                 YS[m % 4], None, compute_op=ALU.add).then_inc(
                                                     acc_done[m % 2], 16)

        @block.scalar
        def _(act):
            act.sem_inc(exp_done, 2)
            for b in range(NB):
                for m in range(3):
                    u = 3 * b + m
                    n = P if m < 2 else 64
                    act.wait_ge(rot_ready, u + 1)
                    if u >= 2:
                        act.wait_ge(scr_done[u % 2], 48 * (u // 2))
                    nc.scalar.activation(parts[0:n, u % 2, 0, :], rope_t[0:n, u % 2, 2, :], ACT.Copy).then_inc(
                        hi_ready, 1)
                    act.wait_ge(rest1_ready, u + 1)
                    nc.scalar.activation(parts[0:n, u % 2, 1, :], rope_t[0:n, u % 2, 3, :], ACT.Copy).then_inc(
                        mid_ready, 1)
                act.wait_ge(v_ready, b + 1)
                nc.scalar.activation(VA[:, b * QT:(b + 1) * QT, :],
                                     PVP[:, 0:QT * G * HD].rearrange("p (q n) -> p q n", q=QT),
                                     ACT.Copy).then_inc(v_used, 1)

            def maxima_rows(b):
                act.wait_ge(mrT_ready, b + 1)
                if b >= 1:
                    act.wait_ge(mrow[(b - 1) % 2], 48 * ((b - 1) // 2 + 1))
                nc.scalar.activation(MR[:, :], MIS[0:PARTS * H, 0:T // 2].bitcast(BF16), ACT.Copy).then_inc(
                    mr_ready, 1)

            def copy_x1T(b, banks):
                act.wait_ge(x1T_ready, b + 1)
                for i in range(2):
                    t = (4 * b + 2 * i) * P
                    nc.scalar.activation(x1T[:, :, t:t + 2 * P].rearrange("p c (t n) -> p t c n", n=P),
                                         banks[i][:, :].rearrange("p (t c n) -> p t c n", t=2, c=KC),
                                         ACT.Copy).then_inc(x1T_copied, 1)

            maxima_rows(0)
            for b in range(NB):
                with act.Fori(0, G) as g:
                    s = g + 8 * b
                    for k, (kt, h0, nh) in enumerate(S2):
                        act.wait_ge(s2_ready, s * S2_TILES + k + 1)
                        act.wait_ge(pv_done, s * 4 + kt + 1)
                        w = T - P * kt
                        tile = S2P[k % 2][:, :, :]
                        if nh == 2:
                            src = tile[:, :, 0:w]
                            dst = PT[kt][:, h0:h0 + 2, :]
                        else:
                            src = tile.rearrange("p a t -> p (a t)")[:, 0:GH * w]
                            dst = PT[kt].rearrange("p h t -> p (h t)")
                        nc.scalar.activation(dst, src, ACT.Exp, scale=SCALE).then_inc(exp_done, 1)
                    act.wait_ge(pv_done, s * 4 + 8)
                    act.wait_ge(ctxT_ready, s + 1)
                    nc.scalar.activation(PVS[:, :], PVP[:, :], ACT.Copy).then_inc(pvs_ready, 1)
                if b < NB - 1:
                    maxima_rows(b + 1)
                act.wait_ge(var_ready, b + 1)
                nc.scalar.activation(SD[:, 4 * b:4 * b + 4], MV[:, 4 * b:4 * b + 4, 1], ACT.Sqrt,
                                     bias=EPSC[:, 0:1]).then_inc(std_ready, 1)
                if b >= 1:
                    copy_x1T(b - 1, S1P)

            def unit(u):
                act.wait_ge(sh_h, u + 1)
                if u >= 2:
                    act.wait_ge(sh_g, u - 1)
                nc.scalar.activation(SILU[u % 2], HP[u % 2][:, 0:I], ACT.Silu).then_inc(sh_silu, 1)
                if u >= 1:
                    unit_gT(u - 1)

            def unit_gT(u):
                act.wait_ge(sh_gT, u + 1)
                if u >= 2:
                    act.wait_ge(sh_y, u - 1)
                nc.scalar.activation(GTS[u % 2], TGP[u % 2][0:IH, 0:2 * P].rearrange("p (c t) -> p c t", c=2),
                                     ACT.Copy).then_inc(sh_gts, 1)

            for u in range(2):
                unit(u)
            copy_x1T(NB - 1, TXP)
            act.wait_ge(logits_ready, 1)
            nc.scalar.activation(SC, MIS[:, 0:NT * E].rearrange("p (t e) -> p t e", t=NT),
                                 ACT.Sigmoid).then_inc(score_ready, 1)
            for u in range(2, UNITS):
                unit(u)
            unit_gT(UNITS - 1)

            def silu(n, p):
                act.wait_ge(h_ready, n + 3)
                act.wait_ge(g_ready, n + 1)
                nc.scalar.activation(SILU[p], HP[p][:, 0:I], ACT.Silu).then_inc(silu_ready, 1)

            def copy_gT(n, p):
                act.wait_ge(gT_ready, n + 3)
                act.wait_ge(y_ready, n + 1)
                nc.scalar.activation(GTS[p], TGP[p][0:IH, 0:2 * P].rearrange("p (c t) -> p c t", c=2),
                                     ACT.Copy).then_inc(gts_ready, 1)

            act.wait_ge(sh_y, UNITS)
            act.sem_inc(gts_ready, 2)
            silu(0, 0)
            with act.Fori(0, TILES // 2) as i:
                for p in range(2):
                    silu(2 * i + (p + 1), (p + 1) % 2)
                    copy_gT(2 * i + p, p)
            copy_gT(TILES - 1, (TILES - 1) % 2)
            for b in range(NB):
                act.wait_ge(var_ready, NB + b + 1)
                nc.scalar.activation(SD[:, 4 * b:4 * b + 4], MV[:, 4 * b:4 * b + 4, 1], ACT.Sqrt,
                                     bias=EPSC[:, 0:1]).then_inc(std_ready, 1)

        @block.tensor
        def _(pe):
            pe.sem_inc(pv_done, 4)
            pe.sem_inc(ctxT_ready, 1)
            pe.wait_ge(ld_w, 48)
            pe.wait_ge(ld_x, 16)
            for b in range(NB):
                toks = slice(b * T, (b + 1) * T)
                for m in range(3):
                    if b >= 1:
                        pe.wait_ge(proj_used, 3 * (b - 1) + m + 1)
                    outs = ([(S2P[m][:, 0, :], m * P), (S2P[m][:, 1, :], D + m * P)] if m < 2
                            else [(S1P[0][:, :], 2 * D)])
                    for dst, col in outs:
                        for c in range(KC):
                            last = nc.tensor.matmul(dst, WQ[:, c, col:col + P], xT_sb[:, c, toks],
                                                    start=(c == 0), stop=(c == KC - 1))
                    last.then_inc(proj_ready, 1)
                if b >= 1:
                    pe.wait_ge(v_used, b)
                for q in range(QT):
                    for c in range(KC):
                        last = nc.tensor.matmul(PVP[:, q * 64:(q + 1) * 64],
                                                xT_sb[:, c, b * T + q * P:b * T + (q + 1) * P],
                                                WQ[:, c, 640:704], start=(c == 0), stop=(c == KC - 1))
                last.then_inc(v_ready, 1)
            pe.wait_ge(proj_used, 3 * NB)
            pe.wait_ge(v_used, NB)
            pe.wait_ge(consts_ready, 19)
            pe.wait_ge(ones_ready, 1)

            def s1_tile(s, slot, k):
                q, h0, nh = S1[k]
                w = P * (q + 1)
                pe.wait_ge(s1_free, s * S1_TILES + k + 1)
                dst = S1P[k % 2][:, 0:nh * w].rearrange("p (h k) -> p h k", h=nh)
                for h in range(nh):
                    nc.tensor.matmul(dst[:, h, :], qs[0:ROWS, ds(slot, 1), h0 + h, q * P:(q + 1) * P],
                                     KS[0:ROWS, ds(slot, 1), 0:w], start=(h == 0), stop=True,
                                     skip_group_check=True)
                nc.tensor.matmul(dst[:, :, w - P:w], IDB[:, :], MQ[:, 0:nh, :], start=False, stop=True,
                                 skip_group_check=True).then_inc(s1_ready, 1)

            def s2_tile(s, slot, k):
                kt, h0, nh = S2[k]
                w = T - P * kt
                pe.wait_ge(exp_done, s * S2_TILES + k + 1)
                per = T // w if kt >= 2 else 1
                for a in range(max(1, nh // per)):
                    hs = slice(h0 + a * per, h0 + (a + 1) * per)
                    dst = S2P[k % 2][:, a, 0:per * w].rearrange("p (h q) -> p h q", h=per)
                    nc.tensor.matmul(dst, KS[0:KROWS, ds(slot, 1), kt * P:(kt + 1) * P],
                                     qs[0:KROWS, ds(slot, 1), hs, kt * P:T], start=True, stop=True,
                                     skip_group_check=True)
                    last = nc.tensor.matmul(dst[:, :, 0:P], IDB[:, :], MK[:, 0:per, :], start=False, stop=True,
                                            skip_group_check=True)
                last.then_inc(s2_ready, 1)

            def pv(s, kt):
                pe.wait_ge(exp_done, s * S2_TILES + 2 + (2, 4, 5, 6)[kt])
                if kt == 0:
                    pe.wait_ge(vc_ready, s + 1)
                for j in range(GH):
                    last = nc.tensor.matmul(PVP[32 * j:32 * j + 32, kt * P:T], VC[:, kt, :], PT[kt][:, j, :],
                                            start=(kt == 0), stop=(kt == QT - 1))
                last.then_inc(pv_done, 1)

            def group(b, g, with_s1):
                s = g + 8 * b
                slot = g + 8 * (b % 2)
                nxt = g + 8 * ((b + 1) % 2)

                def fill(*ks):
                    if with_s1:
                        for k in ks:
                            s1_tile(s + 8, nxt, k)
                s2_tile(s, slot, 0)
                fill(0)
                s2_tile(s, slot, 1)
                fill(1, 2)
                s2_tile(s, slot, 2)
                fill(3)
                pv(s, 0)
                s2_tile(s, slot, 3)
                fill(4, 5)
                s2_tile(s, slot, 4)
                pv(s, 1)
                fill(6, 7)
                s2_tile(s, slot, 5)
                pv(s, 2)
                fill(8, 9)
                pv(s, 3)
                fill(10, 11)
                pe.wait_ge(pvs_ready, s + 1)
                pe.wait_ge(norm_done, s + 1)
                for q in range(QT):
                    last = nc.tensor.matmul(MIS[:, q * P:(q + 1) * P], PVS[:, q * P:(q + 1) * P], IDF[:, :],
                                            is_transpose=True, start=True, stop=True)
                last.then_inc(ctxT_ready, 1)

            def maxima(b):
                pe.wait_ge(ns_ready, b + 1)
                for q in range(QT):
                    last = nc.tensor.transpose(
                        MIS[0:PARTS * H, q * P // 2:(q + 1) * P // 2].bitcast(BF16),
                        NS[:, q, :, :].rearrange("p a h -> p (a h)"), IDB[:, :])
                last.then_inc(mrT_ready, 1)

            def transpose_x1(b, banks):
                for i in range(2):
                    for t in range(2):
                        for c in range(KC):
                            last = nc.tensor.matmul(banks[i][:, (2 * t + c) * P:(2 * t + c + 1) * P],
                                                    X1[:, 4 * b + 2 * i + t, c * P:(c + 1) * P], IDF[:, :],
                                                    is_transpose=True, start=True, stop=True)
                last.then_inc(x1T_ready, 1)

            for half in range(2):
                stacks_here(pe, 0, half)
                with pe.Fori(4 * half, 4 * half + 4) as g:
                    for k in range(S1_TILES):
                        s1_tile(g, g, k)
            maxima(0)
            pe.wait_ge(mr_ready, 1)
            for b in range(NB):
                pe.wait_ge(mrow[b % 2], 48 * (b // 2 + 1))
                for half in range(2):
                    if b < NB - 1:
                        stacks_here(pe, b + 1, half)
                    with pe.Fori(4 * half, 4 * half + 4) as g:
                        group(b, g, b < NB - 1)
                pe.wait_ge(norm_done, 8 * b + 9)
                for hd in range(KC):
                    pe.wait_ge(oproj_used, 2 * b + hd + 1)
                    for q in range(2):
                        for c in range(KC):
                            last = nc.tensor.matmul(PVP[:, q * D:(q + 1) * D],
                                                    CTX[:, 2 * q + c, hd * P:(hd + 1) * P], WO[:, c, :],
                                                    start=(c == 0), stop=(c == KC - 1))
                    last.then_inc(oproj_ready, 1)
                if b < NB - 1:
                    maxima(b + 1)
                    pe.wait_ge(mr_ready, b + 2)
                pe.wait_ge(oproj_used, 2 * b + 3)
                if b >= 1:
                    pe.wait_ge(s1_free, S1_TILES * G * min(b + 2, NB) + 2)
                    transpose_x1(b - 1, S1P)
                    pe.wait_ge(x1T_copied, 2 * b)

            pe.wait_ge(ld_w13, 16)
            pe.wait_ge(ld_w2, 32)

            def unit_h(u):
                t, e = divmod(u, 2)
                if u >= 2:
                    pe.wait_ge(sh_g, u - 1)
                for c in range(KC):
                    last = nc.tensor.matmul(HP[u % 2][:, 0:2 * I], x1T[:, c, t * P:(t + 1) * P],
                                            w13_sb[:, c, E + e, :], start=(c == 0), stop=(c == KC - 1))
                last.then_inc(sh_h, 1)

            def transpose_g(dst, g, done):
                for c in range(2):
                    last = nc.tensor.matmul(dst[0:IH, c * P:(c + 1) * P], g[:, c * IH:(c + 1) * IH],
                                            IDF[:, :], is_transpose=True, start=True, stop=True)
                last.then_inc(done, 1)

            def unit_y(u):
                t, e = divmod(u, 2)
                pe.wait_ge(sh_gts, u + 1)
                if e == 0 and t >= 2:
                    pe.wait_ge(sh_yused, t - 1)
                for c in range(2):
                    last = nc.tensor.matmul(YP[t % 2][:, 0:D], GTS[u % 2][:, c, :], w2s_sb[:, e, c, :],
                                            start=(e == 0 and c == 0), stop=(e == 1 and c == 1))
                last.then_inc(sh_y, 1)

            def units(u0, u1):
                for u in range(u0, u1):
                    if u + 1 < UNITS:
                        unit_h(u + 1)
                    pe.wait_ge(sh_g, u + 1)
                    if u >= 2:
                        pe.wait_ge(sh_gts, u - 1)
                    transpose_g(TGP[u % 2], GG[u % 2], sh_gT)
                    if u >= 1:
                        unit_y(u - 1)

            unit_h(0)
            units(0, 1)
            pe.wait_ge(x1_ready, NB)
            transpose_x1(NB - 1, TXP)
            units(1, 2)
            pe.wait_ge(x1T_copied, 2 * NB)
            for t in range(NT):
                for c in range(KC):
                    last = nc.tensor.matmul(MIS[:, t * E:(t + 1) * E], x1T[:, c, t * P:(t + 1) * P], GT[:, c, :],
                                            start=(c == 0), stop=(c == KC - 1))
            last.then_inc(logits_ready, 1)
            units(2, 12)
            pe.wait_ge(mb_ready, 1)
            nc.tensor.matmul(MIS[:, 0:NT * E], UPPER[:, :], MB[:, :, :], start=True, stop=True)
            for t in range(NT - 1):
                later = MB[:, t, :].unsqueeze(1).broadcast_to([P, NT - 1 - t, E])
                nc.tensor.matmul(MIS[:, (t + 1) * E:NT * E].rearrange("p (t e) -> p t e", e=E), ONES[:, :],
                                 later, start=False, stop=True, skip_group_check=True)
            for t in range(NT):
                last = nc.tensor.matmul(PVP[:, 0:E], ONES[:, :], MB[:, t, :], start=(t == 0), stop=(t == NT - 1))
            last.then_inc(pre_ready, 1)
            units(12, 22)

            def place_tables(c):
                pe.wait_ge(onehot_ready, c + 1)
                pe.wait_ge(wprod_ready, c + 1)
                for k in range(CH * TOPK):
                    last = nc.tensor.matmul(PVP[:, 0:2 * HI], OHLO[:, k, :], RH[:, k, :],
                                            start=(c == 0 and k == 0),
                                            stop=(c == NT // CH - 1 and k == CH * TOPK - 1))
                last.then_inc(tab_ready, 1)

            for c, (u0, u1) in enumerate(((22, 24), (24, 26), (26, 28), (28, 30))):
                place_tables(c)
                units(u0, u1)
            units(30, UNITS)
            unit_y(UNITS - 1)

            def expert(n):
                return pe.value_load(EOT[0:1, n], min_val=0, max_val=E - 1)

            def tile_x(n, p, k):
                pe.wait_ge(xts_ready, n + 1)
                for c in range(KC):
                    last = nc.tensor.matmul(TXP[p][:, c * P:(c + 1) * P], XS[k][:, c * P:(c + 1) * P], IDF[:, :],
                                            is_transpose=True, start=True, stop=True)
                last.then_inc(xT_ready, 1)

            def tile_h(n, p, e):
                pe.wait_ge(xts_ready, n + 3)
                pe.wait_ge(g_ready, n + 1)
                for c in range(KC):
                    last = nc.tensor.matmul(HP[p][:, 0:2 * I], XTS[p][:, c, :], w13_sb[:, c, ds(e, 1), :],
                                            start=(c == 0), stop=(c == KC - 1))
                last.then_inc(h_ready, 1)

            def tile_g(n, p):
                pe.wait_ge(g_ready, n + 3)
                pe.wait_ge(gts_ready, n + 1)
                transpose_g(TGP[p], GG[p], gT_ready)

            def tile_y(n, p, e):
                pe.wait_ge(gts_ready, n + 3)
                pe.wait_ge(ys_ready, n + 1)
                for c in range(2):
                    last = nc.tensor.matmul(YP[p][:, 0:D], GTS[p][:, c, :], w2_sb[:, ds(e, 1), c, :],
                                            start=(c == 0), stop=(c == 1))
                last.then_inc(y_ready, 1)

            def one(n):
                return slice(n, n + 1)

            pe.wait_ge(idx_ready, 1)
            pe.sem_inc(y_ready, 2)
            pe.sem_inc(h_ready, 2)
            pe.sem_inc(gT_ready, 2)
            for n in range(2):
                pe.wait_ge(xs_in[n], 16)
                tile_x(n, n, n)
            tile_h(0, 0, expert(one(0)))
            tile_h(1, 1, expert(one(1)))
            pe.wait_ge(xs_in[2], 16)
            tile_x(2, 0, 2)
            tile_g(0, 0)
            LOOPED = (TILES - 3) // 4 * 4
            with pe.Fori(0, LOOPED // 4) as i:
                for k in range(4):
                    n = 4 * i + (k + 1)
                    p = (k + 1) % 2
                    tile_h(n + 1, 1 - p, expert(ds(n + 1, 1)))
                    pe.wait_ge(xs_in[(k + 3) % 4], 16 * i + 16 * ((k + 3) // 4 + 1))
                    tile_x(n + 2, p, (k + 3) % 4)
                    tile_g(n, p)
                    tile_y(n - 1, 1 - p, expert(ds(n - 1, 1)))
            for n in range(LOOPED + 1, TILES):
                p = n % 2
                if n + 1 < TILES:
                    tile_h(n + 1, 1 - p, expert(one(n + 1)))
                if n + 2 < TILES:
                    pe.wait_ge(xs_in[(n + 2) % 4], 16 * ((n + 2) // 4 + 1))
                    tile_x(n + 2, p, (n + 2) % 4)
                tile_g(n, p)
                tile_y(n - 1, 1 - p, expert(one(n - 1)))
            tile_y(TILES - 1, (TILES - 1) % 2, expert(one(TILES - 1)))

        @block.vector
        def _(dve):
            steps = [0]

            def link(ins, wait=True):
                steps[0] += 1
                ins.then_inc(dve_step, 1)
                if wait:
                    dve.wait_ge(dve_step, steps[0])

            dve.sem_inc(s1_free, 2)
            dve.sem_inc(norm_done, 1)
            dve.sem_inc(oproj_used, 1)
            nc.vector.memset(CTX[:, 0, :], 0.0).then_inc(zero_ready, 1)
            dve.wait_ge(ld_tab, 32)
            for b in range(NB):
                for m in range(3):
                    u = 3 * b + m
                    dve.wait_ge(proj_ready, u + 1)
                    if u >= 2:
                        dve.wait_ge(lo_ready, u - 1)
                    n = P if m < 2 else 64
                    t1, t2, rot, rest = (rope_t[0:n, u % 2, k, :] for k in range(4))
                    if m < 2:
                        straight, swapped, sn = S2P[m][:, 0, :], S2P[m][:, 1, :], SIN
                    else:
                        straight, swapped, sn = S1P[0][0:64, :], S1P[0][64:128, :], SIN[64:128, :]
                    link(nc.vector.tensor_tensor(t1, straight, COS[0:n, :], ALU.mult), False)
                    link(nc.vector.tensor_tensor(t2, swapped, sn, ALU.mult))
                    dve.sem_inc(proj_used, 1)
                    nc.vector.tensor_tensor(rot, t1, t2, ALU.add).then_inc(rot_ready, 1)
                    dve.wait_ge(hi_ready, u + 1)
                    nc.vector.tensor_tensor(rest, rot, parts[0:n, u % 2, 0, :], ALU.subtract).then_inc(
                        rest1_ready, 1)

            def s1_max(s, g, k):
                q, h0, nh = S1[k]
                w = P * (q + 1)
                dve.wait_ge(s1_ready, s * S1_TILES + k + 1)
                nc.vector.tensor_reduce(NM[:, q, ds(g * GH + h0, nh)],
                                        S1P[k % 2][:, 0:nh * w].rearrange("p (h k) -> p h k", h=nh),
                                        AXX, ALU.max, negate=True).then_inc(s1_free, 1)

            def split_maxima(b):
                dve.wait_ge(s1_free, S1_TILES * 8 * (b + 1) + 2)
                link(nc.vector.tensor_copy(NS[:, :, 0, :], NM[:, :, :]))
                link(nc.vector.tensor_tensor(NR[:, 0, :, :], NM[:, :, :], NS[:, :, 0, :], ALU.subtract))
                link(nc.vector.tensor_copy(NS[:, :, 1, :], NR[:, 0, :, :]))
                link(nc.vector.tensor_tensor(NR[:, 1, :, :], NR[:, 0, :, :], NS[:, :, 1, :], ALU.subtract))
                nc.vector.tensor_copy(NS[:, :, 2, :], NR[:, 1, :, :]).then_inc(ns_ready, 1)

            with dve.Fori(0, G) as g:
                for k in range(S1_TILES):
                    s1_max(g, g, k)
            split_maxima(0)
            dve.wait_ge(ld_res, 16)
            dve.wait_ge(zeroed, 48)
            ctx_v = CTX[:, :, :].rearrange("p q (g j d) -> p q g j d", g=G, j=GH)
            mis_v = MIS[:, :].rearrange("p (q j n) -> p q j n", q=QT, j=GH)
            for b in range(NB):
                rc0 = steps[0]
                with dve.Fori(0, G) as g:
                    s = g + 8 * b
                    if b < NB - 1:
                        for k in range(S1_TILES):
                            s1_max(s + 8, g, k)
                    dve.wait_ge(ctxT_ready, s + 2)
                    nc.vector.reciprocal(RC[:, :, :], mis_v[:, :, :, HD]).then_inc(dve_step, 1)
                    dve.wait_ge(dve_step, g + (rc0 + 1))
                    nc.vector.tensor_tensor(ctx_v[:, :, ds(g, 1), :, :].rearrange("p q g j d -> p q (g j) d"),
                                            mis_v[:, :, :, 0:HD],
                                            RC[:, :, :].unsqueeze(3).broadcast_to([P, QT, GH, HD]),
                                            ALU.mult).then_inc(norm_done, 1)
                steps[0] += G
                if b < NB - 1:
                    split_maxima(b + 1)
                for hd in range(KC):
                    dve.wait_ge(oproj_ready, 2 * b + hd + 1)
                    t = 4 * b + 2 * hd
                    nc.vector.tensor_tensor(X1[:, t:t + 2, :], PVP[:, :].rearrange("p (q d) -> p q d", q=2),
                                            X1[:, t:t + 2, :], ALU.add).then_inc(oproj_used, 1)
                dve.wait_ge(oproj_used, 2 * b + 3)
                for k in range(4):
                    link(nc.vector.bn_stats(ST[:, k, :], X1[:, 4 * b + k, :]), False)
                dve.wait_ge(dve_step, steps[0])
                for k in range(4):
                    link(nc.vector.bn_aggr(MV[:, 4 * b + k, :], ST[:, k, :]), False)
                dve.wait_ge(dve_step, steps[0])
                dve.sem_inc(var_ready, 1)
                dve.wait_ge(std_ready, b + 1)
                link(nc.vector.reciprocal(RSTD[:, 4 * b:4 * b + 4], SD[:, 4 * b:4 * b + 4]))
                for k in range(4):
                    t = 4 * b + k
                    link(nc.vector.tensor_scalar(X1[:, t, :], X1[:, t, :], MV[:, t, 0:1], RSTD[:, t:t + 1],
                                                 ALU.subtract, ALU.mult), False)
                dve.wait_ge(dve_step, steps[0])
                dve.sem_inc(x1_ready, 1)

            def units(u0, u1):
                for u in range(u0, u1):
                    dve.wait_ge(sh_silu, u + 1)
                    if u >= 2:
                        dve.wait_ge(sh_gT, u - 1)
                    nc.vector.tensor_tensor(GG[u % 2], SILU[u % 2], HP[u % 2][:, I:2 * I],
                                            ALU.mult).then_inc(sh_g, 1)
                    if u % 2 and u >= 3:
                        unit_out(u // 2 - 1)

            def unit_out(t):
                dve.wait_ge(sh_y, 2 * t + 2)
                dve.wait_ge(x1_out[t // 4], 16)
                nc.vector.tensor_tensor(X1[:, t, :], YP[t % 2][:, 0:D], X1[:, t, :], ALU.add).then_inc(
                    sh_yused, 1)

            dve.wait_ge(pv_done, 4 * NB * G + 4)
            units(0, 2)
            dve.wait_ge(score_ready, 1)
            dve.wait_ge(consts_ready, 19)
            sg = SC.rearrange("p t (g k) -> p t g k", g=4)
            link(nc.vector.tensor_reduce(GS, sg, AXX, ALU.max))
            other = GS.unsqueeze(2).broadcast_to([P, NT, 4, 4])
            own = GS.unsqueeze(3).broadcast_to([P, NT, 4, 4])
            low = LOWER[:, :, :].unsqueeze(1).broadcast_to([P, NT, 4, 4])
            link(nc.vector.tensor_tensor(GA, other, own, ALU.is_gt), False)
            link(nc.vector.tensor_tensor(GB, other, own, ALU.is_equal))
            link(nc.vector.tensor_tensor(GB, GB, low, ALU.mult))
            link(nc.vector.tensor_tensor(GA, GA, GB, ALU.add))
            link(nc.vector.tensor_reduce(GR, GA, AXX, ALU.add))
            link(nc.vector.tensor_scalar(GR, GR, 2.0, None, ALU.is_lt))
            link(nc.vector.tensor_tensor(MSK.rearrange("p t (g k) -> p t g k", g=4), sg,
                                         GR.unsqueeze(3).broadcast_to([P, NT, 4, 4]), ALU.mult))
            units(2, 4)
            for t in range(NT):
                link(nc.vector.max(TOP[:, t, :], MSK[:, t, :]), False)
            dve.wait_ge(dve_step, steps[0])
            for t in range(NT):
                link(nc.vector.max_index(TOPI[:, t, :], TOP[:, t, :], MSK[:, t, :]), False)
            dve.wait_ge(dve_step, steps[0])
            units(4, 7)
            link(nc.vector.tensor_copy(TOPF, TOPI))
            by_t = [P, NT, TOPK, E]
            link(nc.vector.tensor_tensor(OHJ, TOPF[:, :, 0:TOPK].unsqueeze(3).broadcast_to(by_t),
                                         IOTA[:, 0:E].unsqueeze(1).unsqueeze(1).broadcast_to(by_t),
                                         ALU.is_equal))
            with nc.allow_low_precision("zeros and ones"):
                nc.vector.tensor_reduce(MB[:, :, :], OHJ.rearrange("p t j e -> p t e j"), AXX,
                                        ALU.add).then_inc(mb_ready, 1)
            link(nc.vector.tensor_tensor(TMJ, OHJ, SC.unsqueeze(2).broadcast_to(by_t), ALU.mult))
            link(nc.vector.tensor_reduce(WJ, TMJ, AXX, ALU.add))
            units(7, 9)
            link(nc.vector.tensor_reduce(WSUM, WJ, AXX, ALU.add))
            link(nc.vector.reciprocal(WREC, WSUM))
            link(nc.vector.tensor_tensor(WJ, WJ, WREC.unsqueeze(2).broadcast_to([P, NT, TOPK]), ALU.mult))
            units(9, 12)
            dve.wait_ge(pre_ready, 1)
            sq = [P, E, E]
            cmp = MSK.rearrange("p a b -> p (a b)").rearrange("p (a b) -> p a b", a=E)
            link(nc.vector.tensor_scalar(EMPTY[:, 0:E], IOTA[:, 0:E], float(P), None, ALU.mult), False)
            link(nc.vector.tensor_copy(NEXP, PVP[:, 0:E]))
            link(nc.vector.tensor_tensor(cmp, NEXP.unsqueeze(2).broadcast_to(sq),
                                         EMPTY[:, 0:E].unsqueeze(1).broadcast_to(sq), ALU.is_gt))
            link(nc.vector.tensor_reduce(KEXP, cmp, AXX, ALU.add))
            link(nc.vector.tensor_tensor(cmp, KEXP.unsqueeze(1).broadcast_to(sq), LOWER16[:, :, :], ALU.mult))
            link(nc.vector.tensor_reduce(BASE, cmp, AXX, ALU.add))
            link(nc.vector.tensor_tensor(ENDS, BASE, KEXP, ALU.add), False)
            link(nc.vector.scalar_tensor_tensor(out=POS, in0=BASE.unsqueeze(1).broadcast_to([P, NT, E]),
                                                scalar=float(P),
                                                in1=MIS[:, 0:NT * E].rearrange("p (t e) -> p t e", t=NT),
                                                op0=ALU.mult, op1=ALU.add))
            link(nc.vector.tensor_tensor(TMJ, OHJ, POS.unsqueeze(2).broadcast_to(by_t), ALU.mult))
            link(nc.vector.tensor_reduce(PJ.rearrange("p (t j) -> p t j", j=TOPK), TMJ, AXX, ALU.add))
            units(12, 14)
            link(nc.vector.tensor_copy(PU, PJ))
            link(nc.vector.tensor_scalar(HU, PU, 7, None, ALU.logical_shift_right), False)
            link(nc.vector.tensor_scalar(LU, PU, P - 1, None, ALU.bitwise_and))
            link(nc.vector.tensor_copy(HF, HU), False)
            link(nc.vector.tensor_copy(LF, LU))

            def onehots(c):
                n = CH * TOPK
                ch = slice(c * n, (c + 1) * n)
                if c:
                    dve.wait_ge(tab_ready, c)
                nc.vector.tensor_tensor(OHHI, HF[:, ch].unsqueeze(2).broadcast_to([P, n, HI]),
                                        IOTA[:, 0:HI].unsqueeze(1).broadcast_to([P, n, HI]),
                                        ALU.is_equal).then_inc(hi_made, 1)
                link(nc.vector.tensor_tensor(OHLO, LF[:, ch].unsqueeze(2).broadcast_to([P, n, P]),
                                             IOTA[:, :].unsqueeze(1).broadcast_to([P, n, P]), ALU.is_equal))
                dve.wait_ge(hi_made, c + 1)
                nc.vector.tensor_tensor(RH[:, :, 0:HI], OHHI,
                                        TID1[:, :, :].rearrange("p t j -> p (t j)")[:, ch].unsqueeze(2)
                                        .broadcast_to([P, n, HI]), ALU.mult).then_inc(onehot_ready, 1)

            onehots(0)
            units(14, 22)
            for c, (u0, u1) in enumerate(((22, 24), (24, 26), (26, 28), (28, 30))):
                if c < 3:
                    onehots(c + 1)
                units(u0, u1)
            dve.wait_ge(tab_ready, 4)
            dve.wait_ge(wprod_ready, 4)
            ends = RH.rearrange("p a b -> p (a b)")[:, 0:HI * E].rearrange("p (n e) -> p n e", e=E)
            link(nc.vector.tensor_tensor(ends, ENDS.unsqueeze(1).broadcast_to([P, HI, E]),
                                         IOTA[:, 0:HI].unsqueeze(2).broadcast_to([P, HI, E]), ALU.is_le))
            link(nc.vector.tensor_reduce(EOTF[:, :], ends, AXX, ALU.add))
            link(nc.vector.tensor_scalar(EOTF[:, :], EOTF[:, :], float(E - 1), None, ALU.min))
            link(nc.vector.tensor_copy(EOT[:, :], EOTF[:, :]), False)
            link(nc.vector.tensor_scalar(IDXF, PVP[:, 0:HI], -1.0, None, ALU.add), False)
            link(nc.vector.tensor_scalar(EMPTY, PVP[:, 0:HI], 0.0, PADROW[:, 0:1], ALU.is_equal, ALU.mult), False)
            link(nc.vector.tensor_copy(WT[:, :], PVP[:, HI:2 * HI]))
            link(nc.vector.tensor_tensor(IDXF, IDXF, EMPTY, ALU.add))
            link(nc.vector.tensor_copy(IDX[:, :], IDXF))
            dve.sem_inc(idx_ready, 1)
            units(30, UNITS)
            unit_out(NT - 1)

            dve.wait_ge(sh_yused, NT)
            dve.sem_inc(xts_ready, 2)
            dve.sem_inc(g_ready, 2)
            dve.sem_inc(ys_ready, 2)

            def copy_xT(n, p):
                dve.wait_ge(xT_ready, n + 1)
                dve.wait_ge(h_ready, n + 1)
                nc.vector.tensor_copy(XTS[p], TXP[p][:, 0:D].rearrange("p (c t) -> p c t", c=KC)).then_inc(
                    xts_ready, 1)

            def product(n, p):
                dve.wait_ge(silu_ready, n + 1)
                dve.wait_ge(gT_ready, n + 1)
                weight = WT[:, n:n + 1] if isinstance(n, int) else WT[:, ds(n, 1)]
                nc.vector.scalar_tensor_tensor(out=GG[p], in0=SILU[p], scalar=weight, in1=HP[p][:, I:2 * I],
                                               op0=ALU.mult, op1=ALU.mult).then_inc(g_ready, 1)

            def result(n, k):
                dve.wait_ge(y_ready, n + 3)
                nc.vector.tensor_copy(YS[k], YP[k % 2][:, 0:D]).then_inc(ys_ready, 1)

            def tile(n):
                if n + 2 < TILES:
                    copy_xT(n + 2, n % 2)
                if n + 1 < TILES:
                    product(n + 1, (n + 1) % 2)
                if n >= 1:
                    if n >= 5:
                        dve.wait_ge(acc_done[(n - 1) % 2], 16 * ((n - 1) // 2 - 1))
                    result(n - 1, (n - 1) % 4)

            copy_xT(0, 0)
            copy_xT(1, 1)
            product(0, 0)
            for n in range(5):
                tile(n)
            rounds = (TILES - 2 - 5) // 4
            with dve.Fori(0, rounds) as i:
                for k in range(4):
                    n = 4 * i + (k + 5)
                    copy_xT(n + 2, (k + 1) % 2)
                    product(n + 1, k % 2)
                    dve.wait_ge(acc_done[k % 2], 32 * i + 16 * (1 + k // 2))
                    result(n - 1, k)
            for n in range(5 + 4 * rounds, TILES):
                tile(n)
            dve.wait_ge(acc_done[(TILES - 1) % 2], 16 * ((TILES - 1) // 2 - 1))
            result(TILES - 1, (TILES - 1) % 4)

            for b in range(NB):
                dve.wait_ge(acc_in[b], 32)
                ts = slice(4 * b, 4 * b + 4)
                link(nc.vector.tensor_tensor(X1[:, ts, :], FIN[0][:, ts, :], FIN[1][:, ts, :], ALU.add))
                for k in range(4):
                    link(nc.vector.bn_stats(ST[:, k, :], X1[:, 4 * b + k, :]), False)
                dve.wait_ge(dve_step, steps[0])
                for k in range(4):
                    link(nc.vector.bn_aggr(MV[:, 4 * b + k, :], ST[:, k, :]), False)
                dve.wait_ge(dve_step, steps[0])
                dve.sem_inc(var_ready, 1)
                dve.wait_ge(std_ready, NB + b + 1)
                link(nc.vector.reciprocal(RSTD[:, ts], SD[:, ts]))
                for k in range(4):
                    t = 4 * b + k
                    link(nc.vector.tensor_scalar(X1[:, t, :], X1[:, t, :], MV[:, t, 0:1], RSTD[:, t:t + 1],
                                                 ALU.subtract, ALU.mult), False)
                dve.wait_ge(dve_step, steps[0])
                dve.sem_inc(out_ready, 1)


def tables():
    import numpy as np
    half = HD // 2
    inv = (np.float32(1.0) / np.float32(10000.0) ** (np.arange(half, dtype=np.float32) * np.float32(2.0) /
                                                      np.float32(HD))).astype(np.float32)
    ang = np.arange(T, dtype=np.float32)[:, None] * inv[None, :]
    c, s = np.cos(ang).astype(np.float32).T, np.sin(ang).astype(np.float32).T
    cos = np.tile(np.concatenate([c, c]), (P // HD, 1))
    sin = np.tile(np.concatenate([-s, s]), (P // HD, 1))
    return np.ascontiguousarray(cos), np.ascontiguousarray(sin)


def kernel(L0_attn_x, L0_attn_Wq, L0_attn_Wk, L0_attn_Wv, L0_attn_Wo, L0_ffn_gate_w, L0_ffn_W1, L0_ffn_W2,
           L0_ffn_W3, L0_ffn_Ws1, L0_ffn_Ws2, L0_ffn_Ws3):
    import numpy as np
    import concourse.bacc as bacc
    from concourse.bass_utils import run_bass_kernel_spmd

    def halves_swapped(w):
        return w.reshape(D, -1, 2, HD // 2)[:, :, ::-1].reshape(D, -1)

    x = np.asarray(L0_attn_x).reshape(NB * T, D)
    wq, wk, wv = (np.asarray(w) for w in (L0_attn_Wq, L0_attn_Wk, L0_attn_Wv))
    wqkv = np.concatenate([wq, halves_swapped(wq), wk, halves_swapped(wk), wv], axis=1)
    w1 = np.concatenate([np.asarray(L0_ffn_W1), np.asarray(L0_ffn_Ws1).reshape(2, I, D)])
    w3 = np.concatenate([np.asarray(L0_ffn_W3), np.asarray(L0_ffn_Ws3).reshape(2, I, D)])
    w13 = np.concatenate([w1, w3], axis=1).transpose(2, 0, 1)
    w2 = np.concatenate([np.asarray(L0_ffn_W2), np.asarray(L0_ffn_Ws2).reshape(D, 2, I).transpose(1, 0, 2)])
    w2 = w2.transpose(2, 0, 1).reshape(2, IH, NE, D).transpose(1, 2, 0, 3)
    cos, sin = tables()
    ins = {"x": x, "xT": x.T, "wqkv": wqkv, "wo": np.asarray(L0_attn_Wo), "cos": cos, "sin": sin,
           "gateT": np.asarray(L0_ffn_gate_w).T, "w13": w13, "w2": w2}
    nc = bacc.Bacc("TRN2", target_bir_lowering=False, num_devices=1)
    arrays, args = {}, []
    for name, a in ins.items():
        arrays[f"in_{name}"] = np.ascontiguousarray(a)
        args.append(nc.dram_tensor(f"in_{name}", a.shape, mybir.dt.from_np(a.dtype), kind="ExternalInput").ap())
    args.append(nc.dram_tensor("out_x", (NB * T, D), F32, kind="ExternalOutput").ap())
    program(nc, *args)
    r = run_bass_kernel_spmd(nc, [arrays], core_ids=[0])
    return r.results[0]["out_x"].reshape(NB, T, D)
```

```python
from contextlib import ExitStack

import concourse.bass as bass
from concourse import mybir

F32 = mybir.dt.float32
BF16 = mybir.dt.bfloat16
U32 = mybir.dt.uint32
ALU = mybir.AluOpType
ACT = mybir.ActivationFunctionType
AXX = mybir.AxisListType.X
ds = bass.ds

P = 128
NB, T, D = 4, 512, 256
H, G, HD = 32, 8, 8
GH = H // G
QT = T // P
KC = D // P
NT = NB * T // P
E, I = 16, 176
NE = E + 2
IH = I // 2
PARTS = 3
ROWS = PARTS * PARTS * HD
KROWS = ROWS + PARTS
SLOTS = 2 * G
NEG = -3.0e38
EPS = 1e-5
SCALE = float(HD) ** -0.5
TOPK = 4
TJ = NT * TOPK
TOKENS = NB * T
TILES = (TOKENS * TOPK + E * (P - 1)) // P
HI = TILES + 1
PAD = TOKENS
UNITS = 2 * NT
CH = 4

UB = 4
S1_TILES = 12
S2_TILES = 6
S1 = [(0, 0, 2), (0, 2, 2), (1, 0, 2), (1, 2, 2)] + [(q, h, 1) for q in (2, 3) for h in range(GH)]
EXPS = (2, 4, 5, 6)
S2 = [(0, 0, 2), (0, 2, 2), (1, 0, 2), (1, 2, 2), (2, 0, 4), (3, 0, 4)]


def program(nc, x, xT, wqkv, wo, cos, sin, gateT, w13, w2, out):
    q_scr = nc.dram_tensor("q_parts", (NB, PARTS, HD, H, T), BF16, kind="Internal").ap()
    k_scr = nc.dram_tensor("k_parts", (NB, PARTS, HD, G, T), BF16, kind="Internal").ap()
    x1_scr = nc.dram_tensor("x1_rows", (TOKENS + P, D), F32, kind="Internal").ap()
    acc = [nc.dram_tensor(f"acc{i}", (TOKENS + P, D), F32, kind="Internal").ap() for i in range(2)]
    with ExitStack() as ctx:
        def sb(name, shape, dt=F32):
            return ctx.enter_context(nc.sbuf_tensor(name, shape, dt))

        def psum(name, shape):
            return ctx.enter_context(nc.psum_tensor(name, shape, F32))

        def sem(name):
            return ctx.enter_context(nc.semaphore(name))

        EARLY = sb("EARLY", [P, KC * TOKENS])
        WQ = EARLY[:, 0:KC * 704].rearrange("p (c n) -> p c n", c=KC)
        COS = EARLY[:, KC * 704:KC * 704 + T]
        SIN = EARLY[:, KC * 704 + T:KC * 704 + 2 * T]
        x1T = EARLY[:, :].rearrange("p (c t) -> p c t", c=KC)
        WO = sb("WO", [P, KC, D])
        GT = sb("GT", [P, KC, E])
        XT = sb("XT", [P, KC * NB * T])
        xT_sb = XT[:, :].rearrange("p (c t) -> p c t", c=KC)
        X1 = XT[:, :].rearrange("p (n d) -> p n d", n=NT)
        QS = sb("QS", [P, SLOTS * GH * T // 2])
        qs = QS[:, :].bitcast(BF16).rearrange("p (s h t) -> p s h t", s=SLOTS, h=GH)
        w2_sb = QS[0:IH, 0:E * 2 * D].rearrange("p (e c d) -> p e c d", e=E, c=2)
        KS = sb("KS", [P, SLOTS, T], BF16)
        w2s_sb = KS[0:IH, 0:G // 2, :].rearrange("p s t -> p (s t)").bitcast(F32).rearrange(
            "p (e c d) -> p e c d", e=2, c=2)
        W13 = sb("W13", [P, KC * NE * 2 * I])
        w13_sb = W13[:, :].rearrange("p (c e n) -> p c e n", c=KC, e=NE)
        rope_t = W13[:, 0:UB * 4 * T].rearrange("p (u k t) -> p u k t", u=UB, k=4)
        parts = W13[:, UB * 4 * T:UB * 4 * T + UB * PARTS * T // 2].bitcast(BF16).rearrange(
            "p (u a t) -> p u a t", u=UB, a=PARTS)
        VA = sb("VA", [P, NT, G * HD])
        VC = sb("VC", [P, QT, 32])
        ATT = sb("ATT", [P, GH * sum(T - P * k for k in range(QT))])
        PT, at = [], 0
        for k in range(QT):
            PT.append(ATT[:, at:at + GH * (T - P * k)].rearrange("p (h t) -> p h t", h=GH))
            at += GH * (T - P * k)
        PVS = sb("PVS", [P, T])
        RC = sb("RC", [P, QT, GH])
        CTX = sb("CTX", [P, QT, D])
        NM = sb("NM", [P, QT, H])
        NR = sb("NR", [P, 2, QT, H // 2])
        NS = sb("NS", [P, 2, QT, PARTS, H // 2], BF16)
        MR = sb("MR", [PARTS * H // 2, 2, T], BF16)
        SEL = sb("SEL", [P, GH, HD + 1])
        IDF = sb("IDF", [P, P])
        IDB = sb("IDB", [P, P], BF16)
        MQ = sb("MQ", [P, GH, P], BF16)
        EPSC = sb("EPSC", [P, 1])
        ST = sb("ST", [P, QT, 6])
        MV = sb("MV", [P, NT, 2])
        SD = sb("SD", [P, NT])
        RSTD = sb("RSTD", [P, NT])
        def taker(region):
            at = [0]

            def take(*shape, dt=F32, rows=P):
                n = 1
                for d in shape:
                    n *= d
                view = region[0:rows, at[0]:at[0] + n]
                at[0] += n
                names = [f"x{i}" for i in range(len(shape))]
                if len(shape) > 1:
                    view = view.rearrange(f"p ({' '.join(names)}) -> p {' '.join(names)}",
                                          **{m: d for m, d in zip(names[1:], shape[1:])})
                return view if dt == F32 else view.bitcast(dt)
            return take

        in_att = taker(ATT)
        XS = [in_att(D) for _ in range(4)]
        YS = [in_att(D) for _ in range(4)]
        GG = [in_att(I) for _ in range(2)]
        SILU = [in_att(I) for _ in range(2)]
        GTS = [in_att(2, P, rows=IH) for _ in range(2)]
        XTS = [in_att(KC, P) for _ in range(2)]
        SC = in_att(NT, E)
        MSK = in_att(NT, E)
        GS = in_att(NT, 4)
        GR = in_att(NT, 4)
        GA = in_att(NT, 4, 4)
        GB = in_att(NT, 4, 4)
        in_qs = taker(QS[:, SLOTS * GH * T // 4:SLOTS * GH * T // 2])
        OHJ = in_qs(NT, TOPK, E)
        TMJ = in_qs(NT, TOPK, E)
        OHLO = in_qs(CH * TOPK, P)
        OHHI = in_qs(CH * TOPK, HI)
        RH = in_qs(CH * TOPK, 2 * HI)
        POS = in_qs(NT, E)
        in_ctx = taker(CTX[:, :, :].rearrange("p q d -> p (q d)"))
        TOP = in_ctx(NT, 8)
        TOPI = in_ctx(NT, 8, dt=U32)
        TOPF = in_ctx(NT, 8)
        WJ = in_ctx(NT, TOPK)
        WSUM = in_ctx(NT)
        WREC = in_ctx(NT)
        PJ = in_ctx(TJ)
        PU = in_ctx(TJ, dt=U32)
        HU = in_ctx(TJ, dt=U32)
        LU = in_ctx(TJ, dt=U32)
        HF = in_ctx(TJ)
        LF = in_ctx(TJ)
        NEXP = in_ctx(E)
        KEXP = in_ctx(E)
        BASE = in_ctx(E)
        ENDS = in_ctx(E)
        in_pvs = taker(PVS)
        IDXF = in_pvs(HI)
        EMPTY = in_pvs(HI)
        IDX = sb("IDX", [P, HI], U32)
        WT = sb("WT", [P, HI])
        EOTF = sb("EOTF", [P, HI])
        EOT = sb("EOT", [P, HI], U32)
        MB = sb("MB", [P, NT, E], BF16)
        LOWER = sb("LOWER", [P, 4, 4])
        LOWER16 = sb("LOWER16", [P, E, E])
        IOTA = sb("IOTA", [P, P])
        TID1 = sb("TID1", [P, NT, TOPK])
        PADROW = sb("PADROW", [P, 1])
        UPPER = sb("UPPER", [P, P], BF16)
        ONES = sb("ONES", [P, P], BF16)

        S1P = [psum(f"S1P{i}", [P, T]) for i in range(2)]
        S2P = [psum(f"S2P{i}", [P, 2, T]) for i in range(2)]
        PVP = psum("PVP", [P, T])
        MIS = psum("MIS", [P, T])
        CTXP = MIS[:, 0:QT * GH * (HD + 1)].rearrange("p (q j n) -> p q j n", q=QT, j=GH)
        MRP = MIS[:, T // 2:T].bitcast(BF16)
        S1P6 = [S1P[0][:, :], S1P[1][:, :]] + [S2P[i][:, j, :] for i in range(2) for j in range(2)]
        HP = [S2P[0][:, i, :] for i in range(2)]
        TGP = [S2P[1][:, i, :] for i in range(2)]
        YP = [S1P[i] for i in range(2)]
        TXP = [PVP, MIS]

        ld_x = [sem(f"ld_x{b}") for b in range(NB)]; ld_wq = sem("ld_wq"); ld_w = sem("ld_w"); ld_tab = sem("ld_tab")
        ld_res = sem("ld_res"); ld_w13 = sem("ld_w13"); ld_w2 = sem("ld_w2")
        consts_ready = sem("consts_ready")
        ones_ready = sem("ones_ready")
        proj_ready = sem("proj_ready")
        proj_used = sem("proj_used")
        v_ready = sem("v_ready"); v_used = sem("v_used")
        rot_ready = sem("rot_ready")
        hi_ready = sem("hi_ready")
        rest1_ready = sem("rest1_ready")
        mid_ready = sem("mid_ready")
        lo_ready = sem("lo_ready")
        scr_done = [sem(f"scr_done{i}") for i in range(UB)]
        stack = [[sem(f"stack{p}{h}") for h in range(2)] for p in range(2)]
        s1_ready = sem("s1_ready"); s1_free = sem("s1_free")
        s2_ready = sem("s2_ready"); exp_done = sem("exp_done")
        vc_ready = sem("vc_ready"); vc_init = sem("vc_init")
        pv_done = sem("pv_done"); pvs_ready = sem("pvs_ready")
        ctxT_ready = sem("ctxT_ready"); norm_done = sem("norm_done")
        dve_step = sem("dve_step")
        ns_ready = sem("ns_ready"); mrT_ready = sem("mrT_ready"); mr_ready = sem("mr_ready")
        mrow = [[sem(f"mrow{p}{h}") for h in range(2)] for p in range(2)]
        sel_done = sem("sel_done")
        oproj_ready = sem("oproj_ready"); oproj_used = sem("oproj_used")
        var_ready = sem("var_ready"); std_ready = sem("std_ready")
        x1_ready = sem("x1_ready")
        zero_ready = sem("zero_ready"); zeroed = sem("zeroed")
        x1T_ready = sem("x1T_ready"); x1T_copied = sem("x1T_copied")
        x1_out = [sem(f"x1_out{b}") for b in range(NB)]; res_out = sem("res_out")
        logits_ready = sem("logits_ready"); score_ready = sem("score_ready")
        mb_ready = sem("mb_ready"); pre_ready = sem("pre_ready")
        onehot_ready = sem("onehot_ready"); tab_used = sem("tab_used"); tab_ready = sem("tab_ready")
        wprod_ready = sem("wprod_ready"); hi_made = sem("hi_made")
        idx_ready = sem("idx_ready")
        sh_h = sem("sh_h"); sh_silu = sem("sh_silu"); sh_g = sem("sh_g")
        sh_gT = sem("sh_gT"); sh_gts = sem("sh_gts"); sh_y = sem("sh_y"); sh_yused = sem("sh_yused")
        xs_in = [sem(f"xs_in{i}") for i in range(4)]
        xT_ready = sem("xT_ready"); xts_ready = sem("xts_ready")
        h_ready = sem("h_ready"); silu_ready = sem("silu_ready"); g_ready = sem("g_ready")
        gT_ready = sem("gT_ready"); gts_ready = sem("gts_ready")
        y_ready = sem("y_ready"); ys_ready = sem("ys_ready")
        acc_done = [sem(f"acc_done{i}") for i in range(2)]
        acc_in = [sem(f"acc_in{i}") for i in range(4)]
        out_ready = sem("out_ready"); out_done = sem("out_done")

        FIN = [W13[:, i * NT * D:(i + 1) * NT * D].rearrange("p (n d) -> p n d", n=NT) for i in range(2)]

        block = ctx.enter_context(nc.Block())

        x_tiles = x.rearrange("(n p q) d -> p n (q d)", p=P, q=2)
        out_tiles = out.rearrange("(n p q) d -> p n q d", p=P, q=2)

        def load_stacks(eng, b, half):
            p, g0, n = b % 2, half * 4, 4
            s0 = p * G + g0
            for a in range(PARTS):
                src = q_scr[b, a].rearrange("d h t -> d (h t)")[:, g0 * GH * T:(g0 + n) * GH * T]
                src = bass.AP(tensor=src.tensor, offset=src.offset, ap=[[0, PARTS]] + list(src.ap))
                dst = qs[a * 24:(a + 1) * 24, s0:s0 + n, :, :].rearrange("p s h t -> p (s h t)")
                eng.dma_start(dst, src).then_inc(stack[p][half], 16)
            src = k_scr[b].rearrange("c d g t -> (c d) (g t)")[:, g0 * T:(g0 + n) * T]
            src = bass.AP(tensor=src.tensor, offset=src.offset, ap=[[0, PARTS]] + list(src.ap))
            eng.dma_start(KS[0:ROWS, s0:s0 + n, :].rearrange("p s t -> p (s t)"), src).then_inc(
                stack[p][half], 16)

        def stacks_here(eng, b, half):
            eng.wait_ge(stack[b % 2][half], 64 * (b // 2 + 1))

        @block.sync
        def _(sp):
            sp.dma_start(WQ, wqkv.rearrange("(c p) n -> p c n", p=P)).then_inc(ld_wq, 16)
            xT_rows = xT.rearrange("(c p) t -> p c t", p=P)
            sp.dma_start(xT_sb[:, :, 0:T], xT_rows[:, :, 0:T]).then_inc(ld_x[0], 16)
            sp.dma_start(COS, cos).then_inc(ld_tab, 16)
            sp.dma_start(SIN, sin).then_inc(ld_tab, 16)
            for b in range(1, NB):
                sp.dma_start(xT_sb[:, :, b * T:(b + 1) * T], xT_rows[:, :, b * T:(b + 1) * T]).then_inc(
                    ld_x[b], 16)
            sp.dma_start(WO[:, :, :], wo.rearrange("(c p) n -> p c n", p=P)).then_inc(ld_w, 16)
            sp.dma_start(GT[:, :, :], gateT.rearrange("(c p) n -> p c n", p=P)).then_inc(ld_w, 16)
            sp.wait_ge(zero_ready, 1)
            ctx0 = CTX[:, 0, :]
            zero = bass.AP(tensor=ctx0.tensor, offset=ctx0.offset, ap=[ctx0.ap[0], [0, NT + 1], ctx0.ap[1]])
            sp.dma_start(acc[1].rearrange("(t p) d -> p t d", p=P), zero).then_inc(zeroed, 16)
            for rows in (acc[0], x1_scr):
                sp.dma_start(rows[PAD:PAD + P, :], CTX[:, 0, :]).then_inc(zeroed, 16)
            for b in range(NB):
                for m in range(3):
                    u = 3 * b + m
                    sp.wait_ge(lo_ready, u + 1)
                    for a in range(PARTS):
                        if m < 2:
                            sp.dma_start(q_scr[b, a, :, m * 16:(m + 1) * 16, :].rearrange("d h t -> h d t"),
                                         parts[:, u % UB, a, :]).then_inc(scr_done[u % UB], 16)
                        else:
                            sp.dma_start(k_scr[b, a].rearrange("d h t -> h d t"),
                                         parts[0:64, u % UB, a, :]).then_inc(scr_done[u % UB], 16)
                if b == 0:
                    sp.wait_ge(ones_ready, 1)
                if b < 2:
                    for i in range(3):
                        u = 3 * b + i
                        sp.wait_ge(scr_done[u % UB], 48 * (u // UB + 1))
                    load_stacks(sp, b, 0)
                    load_stacks(sp, b, 1)
            for i in range(UB):
                sp.wait_ge(scr_done[i], 48 * 3 * NB // UB)
            sp.wait_ge(v_ready, NB)
            sp.dma_start(XT[:, :].rearrange("p (n d) -> p n d", n=NT // 2), x_tiles).then_inc(ld_res, 16)
            sp.dma_start(w13_sb, w13.rearrange("(c p) e n -> p c e n", p=P)).then_inc(ld_w13, 16)

            def maxima_out(b, half):
                sp.wait_ge(mr_ready, 2 * b + half + 1)
                s0 = (b % 2) * G + half * G // 2
                for a in range(PARTS):
                    sp.dma_start(qs[ROWS + a:ROWS + a + 1, s0:s0 + G // 2, :, :].rearrange(
                        "p s h t -> p (s h) t"), MR[a * H // 2:(a + 1) * H // 2, half, :]).then_inc(
                            mrow[b % 2][half], 16)

            for half in range(2):
                maxima_out(0, half)
            for b in range(NB - 1):
                for half in range(2):
                    if b < 2:
                        sp.wait_ge(s2_ready, S2_TILES * (8 * b + 4 * (half + 1)))
                        load_stacks(sp, b + 2, half)
                    maxima_out(b + 1, half)
            sp.wait_ge(s2_ready, S2_TILES * 3 * G)
            sp.dma_start(w2_sb, w2[:, 0:E, :, :]).then_inc(ld_w2, 16)
            sp.dma_start(w2s_sb, w2[:, E:NE, :, :]).then_inc(ld_w2, 16)
            for b in range(NB - 1):
                sp.wait_ge(x1_ready, b + 1)
                sp.dma_start(x1_scr[b * T:(b + 1) * T, :].rearrange("(t p) d -> p t d", p=P),
                             X1[:, 4 * b:4 * b + 4, :]).then_inc(x1_out[b], 16)
            sp.wait_ge(x1_ready, NB)
            sp.dma_start(x1_scr[3 * T:4 * T, :].rearrange("(t p) d -> p t d", p=P),
                         X1[:, 12:16, :]).then_inc(x1_out[3], 16)
            sp.wait_ge(sh_yused, NT)
            sp.dma_start(acc[0][0:TOKENS, :].rearrange("(t p) d -> p t d", p=P), X1[:, :, :]).then_inc(
                res_out, 16)
            sp.wait_ge(acc_done[0], 16 * ((TILES + 1) // 2))
            sp.wait_ge(acc_done[1], 16 * (TILES // 2))
            sp.wait_ge(res_out, 16)
            for q in range(4):
                for a in range(2):
                    sp.dma_start(FIN[a][:, 4 * q:4 * q + 4, :],
                                 acc[a][q * T:(q + 1) * T, :].rearrange("(t p) d -> p t d", p=P)).then_inc(
                                     acc_in[q], 16)
            for b in range(NB):
                sp.wait_ge(out_ready, b + 1)
                for q in range(2):
                    sp.dma_start(out_tiles[:, 2 * b:2 * b + 2, q, :], X1[:, 4 * b + q:4 * b + 4:2, :]).then_inc(
                        out_done, 16)
            sp.wait_ge(out_done, 16 * 2 * NB)

        @block.gpsimd
        def _(pool):
            nc.gpsimd.memset(IDF[:, :], 0.0).then_inc(consts_ready, 1)
            nc.gpsimd.memset(IDB[:, :], 0.0).then_inc(consts_ready, 1)
            nc.gpsimd.memset(MQ[:, :, :], 0.0).then_inc(consts_ready, 1)
            nc.gpsimd.memset(EPSC[:, :], EPS).then_inc(consts_ready, 1)
            nc.gpsimd.memset(LOWER[:, :, :], 0.0).then_inc(consts_ready, 1)
            nc.gpsimd.iota(IOTA[:, :], pattern=[[1, P]], base=0, channel_multiplier=0,
                           allow_small_or_imprecise_dtypes=True).then_inc(consts_ready, 1)
            nc.gpsimd.iota(TID1[:, :, :], pattern=[[P, NT], [0, TOPK]], base=1, channel_multiplier=1,
                           allow_small_or_imprecise_dtypes=True).then_inc(consts_ready, 1)
            nc.gpsimd.iota(PADROW[:, :], pattern=[[0, 1]], base=PAD + 1, channel_multiplier=1,
                           allow_small_or_imprecise_dtypes=True).then_inc(consts_ready, 1)
            nc.gpsimd.memset(LOWER16[:, :, :], 0.0).then_inc(consts_ready, 1)
            nc.gpsimd.memset(UPPER[:, :], 0.0).then_inc(consts_ready, 1)
            nc.gpsimd.memset(ONES[:, :], 1.0).then_inc(consts_ready, 1)
            nc.gpsimd.memset(VC[:, :, HD + 1:32], 0.0).then_inc(vc_init, 1)
            nc.gpsimd.memset(VC[:, :, HD:HD + 1], 1.0).then_inc(vc_init, 1)
            pool.wait_ge(consts_ready, 11)
            for m in (IDF, IDB):
                nc.gpsimd.affine_select(out=m[:, :], in_=m[:, :], compare_op=ALU.not_equal, fill=1.0, base=0,
                                        pattern=[[-1, P]], channel_multiplier=1).then_inc(consts_ready, 1)
            nc.gpsimd.affine_select(out=MQ[:, :, :], in_=MQ[:, :, :], compare_op=ALU.is_ge, fill=NEG, base=0,
                                    pattern=[[0, GH], [-1, P]], channel_multiplier=1).then_inc(consts_ready, 1)
            nc.gpsimd.affine_select(out=LOWER[:, :, :], in_=LOWER[:, :, :], compare_op=ALU.is_ge, fill=1.0,
                                    base=0, pattern=[[-1, 4], [1, 4]], channel_multiplier=0).then_inc(
                                        consts_ready, 1)
            nc.gpsimd.affine_select(out=LOWER16[:, :, :], in_=LOWER16[:, :, :], compare_op=ALU.is_ge, fill=1.0,
                                    base=0, pattern=[[-1, E], [1, E]], channel_multiplier=0).then_inc(
                                        consts_ready, 1)
            nc.gpsimd.affine_select(out=UPPER[:, :], in_=UPPER[:, :], compare_op=ALU.is_ge, fill=1.0, base=0,
                                    pattern=[[-1, P]], channel_multiplier=1).then_inc(consts_ready, 1)
            pool.wait_ge(consts_ready, 17)
            nc.gpsimd.tensor_copy(SEL[:, :, :], IDF[:, :].rearrange("p (j n) -> p j n", j=GH)[:, :, 0:HD + 1]
                                  ).then_inc(consts_ready, 1)
            pool.wait_ge(consts_ready, 18)
            nc.gpsimd.memset(KS[64:96, :, :], 1.0).then_inc(ones_ready, 1)
            pool.wait_ge(ones_ready, 1)
            for u in range(3 * NB):
                n = P if u % 3 < 2 else 64
                pool.wait_ge(mid_ready, u + 1)
                nc.gpsimd.tensor_tensor(parts[0:n, u % UB, 2, :], rope_t[0:n, u % UB, 3, :],
                                        parts[0:n, u % UB, 1, :], ALU.subtract).then_inc(lo_ready, 1)
            pool.wait_ge(vc_init, 2)
            for b in range(NB):
                pool.wait_ge(v_used, b + 1)
                with pool.Fori(0, G) as g:
                    for kt in range(QT):
                        pool.wait_ge(exp_done, (g + 8 * b) * S2_TILES + 2 + EXPS[kt])
                        nc.gpsimd.tensor_copy(VC[:, kt, 0:HD], VA[:, b * QT + kt, ds(g * HD, HD)]).then_inc(
                            vc_ready, 1)
                        nc.gpsimd.affine_select(out=PT[kt][:, :, 0:P], in_=PT[kt][:, :, 0:P],
                                                compare_op=ALU.is_ge, fill=0.0, base=0,
                                                pattern=[[0, GH], [1, P]], channel_multiplier=-1).then_inc(
                                                    sel_done, 1)
            for c in range(NT // CH):
                pool.wait_ge(hi_made, c + 1)
                nc.gpsimd.tensor_tensor(RH[:, :, HI:2 * HI], OHHI,
                                        WJ.rearrange("p t j -> p (t j)")[:, c * CH * TOPK:(c + 1) * CH * TOPK]
                                        .unsqueeze(2).broadcast_to([P, CH * TOPK, HI]),
                                        ALU.mult).then_inc(wprod_ready, 1)
            pool.wait_ge(idx_ready, 1)
            for b in range(NB):
                pool.wait_ge(x1_out[b], 16)
            pool.wait_ge(res_out, 16)
            pool.wait_ge(zeroed, 48)
            AHEAD = 5
            for n in range(TILES + AHEAD):
                if n < TILES:
                    if n >= 4:
                        pool.wait_ge(xT_ready, n - 3)
                    nc.gpsimd.indirect_dma_start(XS[n % 4], None, x1_scr,
                                                 bass.IndirectOffsetOnAxis(IDX[:, n:n + 1], 0)).then_inc(
                                                     xs_in[n % 4], 16)
                m = n - AHEAD
                if m >= 0:
                    if m >= 2:
                        pool.wait_ge(acc_done[m % 2], 16 * (m // 2))
                    pool.wait_ge(ys_ready, m + 3)
                    nc.gpsimd.indirect_dma_start(acc[m % 2], bass.IndirectOffsetOnAxis(IDX[:, m:m + 1], 0),
                                                 YS[m % 4], None, compute_op=ALU.add).then_inc(
                                                     acc_done[m % 2], 16)

        @block.scalar
        def _(act):
            act.sem_inc(exp_done, 2)
            def second(u):
                act.wait_ge(rest1_ready, u + 1)
                n = P if u % 3 < 2 else 64
                nc.scalar.activation(parts[0:n, u % UB, 1, :], rope_t[0:n, u % UB, 3, :], ACT.Copy).then_inc(
                    mid_ready, 1)

            for b in range(NB):
                for m in range(3):
                    u = 3 * b + m
                    n = P if m < 2 else 64
                    act.wait_ge(rot_ready, u + 1)
                    if u >= UB:
                        act.wait_ge(scr_done[u % UB], 48 * (u // UB))
                    nc.scalar.activation(parts[0:n, u % UB, 0, :], rope_t[0:n, u % UB, 2, :], ACT.Copy).then_inc(
                        hi_ready, 1)
                    if u >= 1:
                        second(u - 1)
                act.wait_ge(v_ready, b + 1)
                nc.scalar.activation(VA[:, b * QT:(b + 1) * QT, :],
                                     PVP[:, 0:QT * G * HD].rearrange("p (q n) -> p q n", q=QT),
                                     ACT.Copy).then_inc(v_used, 1)
            second(3 * NB - 1)

            def maxima_rows(b, half):
                act.wait_ge(mrT_ready, 2 * b + half + 1)
                if b >= 1:
                    act.wait_ge(mrow[(b - 1) % 2][half], 48 * ((b - 1) // 2 + 1))
                nc.scalar.activation(MR[:, half, :], MRP[0:PARTS * H // 2, :], ACT.Copy).then_inc(mr_ready, 1)

            def copy_x1T(b, banks):
                act.wait_ge(x1T_ready, b + 1)
                for i in range(2):
                    t = (4 * b + 2 * i) * P
                    nc.scalar.activation(x1T[:, :, t:t + 2 * P].rearrange("p c (t n) -> p t c n", n=P),
                                         banks[i][:, :].rearrange("p (t c n) -> p t c n", t=2, c=KC),
                                         ACT.Copy).then_inc(x1T_copied, 1)

            def exps(s, k):
                kt, h0, nh = S2[k]
                act.wait_ge(s2_ready, s * S2_TILES + k + 1)
                act.wait_ge(pv_done, s * 4 + kt + 1)
                w = T - P * kt
                tile = S2P[k % 2][:, :, :]
                if nh == 2:
                    src = tile[:, :, 0:w]
                    dst = PT[kt][:, h0:h0 + 2, :]
                else:
                    src = tile.rearrange("p a t -> p (a t)")[:, 0:GH * w]
                    dst = PT[kt].rearrange("p h t -> p (h t)")
                nc.scalar.activation(dst, src, ACT.Exp, scale=SCALE).then_inc(exp_done, 1)

            def group(s, last=False):
                for k in range(2, S2_TILES):
                    exps(s, k)
                if not last:
                    exps(s + 1, 0)
                act.wait_ge(pv_done, s * 4 + 8)
                act.wait_ge(ctxT_ready, s + 1)
                nc.scalar.activation(PVS[:, :], PVP[:, :], ACT.Copy).then_inc(pvs_ready, 1)
                if not last:
                    exps(s + 1, 1)

            for half in range(2):
                maxima_rows(0, half)
            nc.scalar.preload_act_table(ACT.Exp)
            exps(0, 0)
            exps(0, 1)
            for b in range(NB - 1):
                with act.Fori(8 * b, 8 * b + 6) as s:
                    group(s)
                maxima_rows(b + 1, 0)
                with act.Fori(8 * b + 6, 8 * b + 8) as s:
                    group(s)
                maxima_rows(b + 1, 1)
            last = 8 * (NB - 1)
            with act.Fori(last, last + 2) as s:
                group(s)
            act.wait_ge(var_ready, NB - 1)
            nc.scalar.activation(SD[:, 0:4 * NB - 4], MV[:, 0:4 * NB - 4, 1], ACT.Sqrt,
                                 bias=EPSC[:, 0:1]).then_inc(std_ready, 1)
            nc.scalar.preload_act_table(ACT.Exp)
            with act.Fori(last + 2, last + 7) as s:
                group(s)
            group(last + 7, last=True)
            act.wait_ge(var_ready, NB)
            nc.scalar.activation(SD[:, 4 * NB - 4:4 * NB], MV[:, 4 * NB - 4:4 * NB, 1], ACT.Sqrt,
                                 bias=EPSC[:, 0:1]).then_inc(std_ready, 1)

            def unit(u):
                act.wait_ge(sh_h, u + 1)
                if u >= 2:
                    act.wait_ge(sh_g, u - 1)
                nc.scalar.activation(SILU[u % 2], HP[u % 2][:, 0:I], ACT.Silu).then_inc(sh_silu, 1)
                if u >= 1:
                    unit_gT(u - 1)

            def unit_gT(u):
                act.wait_ge(sh_gT, u + 1)
                if u >= 2:
                    act.wait_ge(sh_y, u - 1)
                nc.scalar.activation(GTS[u % 2], TGP[u % 2][0:IH, 0:2 * P].rearrange("p (c t) -> p c t", c=2),
                                     ACT.Copy).then_inc(sh_gts, 1)

            for u in range(2):
                unit(u)
            copy_x1T(NB - 1, TXP)
            act.wait_ge(logits_ready, 1)
            nc.scalar.activation(SC, MIS[:, 0:NT * E].rearrange("p (t e) -> p t e", t=NT),
                                 ACT.Sigmoid).then_inc(score_ready, 1)
            for u in range(2, UNITS):
                unit(u)
            unit_gT(UNITS - 1)

            def silu(n, p):
                act.wait_ge(h_ready, n + 3)
                act.wait_ge(g_ready, n + 1)
                nc.scalar.activation(SILU[p], HP[p][:, 0:I], ACT.Silu).then_inc(silu_ready, 1)

            def copy_gT(n, p):
                act.wait_ge(gT_ready, n + 3)
                act.wait_ge(y_ready, n + 1)
                nc.scalar.activation(GTS[p], TGP[p][0:IH, 0:2 * P].rearrange("p (c t) -> p c t", c=2),
                                     ACT.Copy).then_inc(gts_ready, 1)

            act.wait_ge(sh_y, UNITS)
            act.sem_inc(gts_ready, 2)
            silu(0, 0)
            with act.Fori(0, TILES // 2) as i:
                for p in range(2):
                    silu(2 * i + (p + 1), (p + 1) % 2)
                    copy_gT(2 * i + p, p)
            copy_gT(TILES - 1, (TILES - 1) % 2)
            for b in range(NB):
                act.wait_ge(var_ready, NB + b + 1)
                nc.scalar.activation(SD[:, 4 * b:4 * b + 4], MV[:, 4 * b:4 * b + 4, 1], ACT.Sqrt,
                                     bias=EPSC[:, 0:1]).then_inc(std_ready, 1)

        @block.tensor
        def _(pe):
            pe.sem_inc(pv_done, 4)
            pe.sem_inc(ctxT_ready, 1)
            pe.wait_ge(ld_wq, 16)
            for b in range(NB):
                pe.wait_ge(ld_x[b], 16)
                toks = slice(b * T, (b + 1) * T)
                for m in range(3):
                    if b >= 1:
                        pe.wait_ge(proj_used, 3 * (b - 1) + m + 1)
                    outs = ([(S2P[m][:, 0, :], m * P), (S2P[m][:, 1, :], D + m * P)] if m < 2
                            else [(S1P[0][:, :], 2 * D)])
                    for dst, col in outs:
                        for c in range(KC):
                            last = nc.tensor.matmul(dst, WQ[:, c, col:col + P], xT_sb[:, c, toks],
                                                    start=(c == 0), stop=(c == KC - 1))
                    last.then_inc(proj_ready, 1)
                if b >= 1:
                    pe.wait_ge(v_used, b)
                for q in range(QT):
                    for c in range(KC):
                        last = nc.tensor.matmul(PVP[:, q * 64:(q + 1) * 64],
                                                xT_sb[:, c, b * T + q * P:b * T + (q + 1) * P],
                                                WQ[:, c, 640:704], start=(c == 0), stop=(c == KC - 1))
                last.then_inc(v_ready, 1)
            pe.wait_ge(proj_used, 3 * NB)
            pe.wait_ge(v_used, NB)
            pe.wait_ge(consts_ready, 18)
            pe.wait_ge(ones_ready, 1)
            pe.wait_ge(ld_w, 32)

            def s1_tile(s, slot, k, banks=S1P):
                q, h0, nh = S1[k]
                w = P * (q + 1)
                pe.wait_ge(s1_free, s * S1_TILES + (k + 7 - len(banks)))
                dst = banks[k % len(banks)][:, 0:nh * w].rearrange("p (h k) -> p h k", h=nh)
                for h in range(nh):
                    nc.tensor.matmul(dst[:, h, :], qs[0:ROWS, ds(slot, 1), h0 + h, q * P:(q + 1) * P],
                                     KS[0:ROWS, ds(slot, 1), 0:w], start=(h == 0), stop=True,
                                     skip_group_check=True)
                nc.tensor.matmul(dst[:, :, w - P:w], IDB[:, :], MQ[:, 0:nh, :], start=False, stop=True,
                                 skip_group_check=True).then_inc(s1_ready, 1)

            def s2_tile(s, slot, k):
                kt, h0, nh = S2[k]
                w = T - P * kt
                pe.wait_ge(exp_done, s * S2_TILES + k + 1)
                per = T // w if kt >= 2 else 1
                for a in range(max(1, nh // per)):
                    hs = slice(h0 + a * per, h0 + (a + 1) * per)
                    dst = S2P[k % 2][:, a, 0:per * w].rearrange("p (h q) -> p h q", h=per)
                    last = nc.tensor.matmul(dst, KS[0:KROWS, ds(slot, 1), kt * P:(kt + 1) * P],
                                            qs[0:KROWS, ds(slot, 1), hs, kt * P:T], start=True, stop=True)
                last.then_inc(s2_ready, 1)

            def pv(s, kt):
                pe.wait_ge(sel_done, s * 4 + kt + 1)
                pe.wait_ge(vc_ready, s * 4 + kt + 1)
                for j in range(GH):
                    last = nc.tensor.matmul(PVP[32 * j:32 * j + 32, kt * P:T], VC[:, kt, :], PT[kt][:, j, :],
                                            start=(kt == 0), stop=(kt == QT - 1))
                last.then_inc(pv_done, 1)

            def group(b, g, with_next=True, with_maxima=False):
                s = g + 8 * b
                slot = g + 8 * (b % 2)
                nxt = g + 8 * ((b + 1) % 2)

                def fill(*ks):
                    if b < NB - 1:
                        for k in ks:
                            s1_tile(s + 8, nxt, k)

                def ahead(k):
                    if with_next:
                        s2_tile(s + 1, slot + 1 if not (isinstance(g, int) and g == G - 1)
                                else 8 * ((b + 1) % 2), k)

                fill(0)
                s2_tile(s, slot, 2)
                fill(1)
                s2_tile(s, slot, 3)
                fill(2)
                pv(s, 0)
                if with_maxima:
                    maxima(b + 1, 0)
                fill(3)
                s2_tile(s, slot, 4)
                fill(4)
                pv(s, 1)
                fill(5)
                s2_tile(s, slot, 5)
                fill(6)
                ahead(0)
                fill(7)
                pv(s, 2)
                fill(8, 9)
                pv(s, 3)
                fill(10)
                ahead(1)
                fill(11)
                pe.wait_ge(pvs_ready, s + 1)
                pe.wait_ge(norm_done, s + 1)
                if with_maxima:
                    pe.wait_ge(mr_ready, 2 * b + 3)
                for q in range(QT):
                    last = nc.tensor.matmul(CTXP[:, q, :, :].rearrange("p j n -> p (j n)"),
                                            PVS[:, q * P:(q + 1) * P],
                                            SEL[:, :, :].rearrange("p j n -> p (j n)"), start=True, stop=True,
                                            skip_group_check=True)
                last.then_inc(ctxT_ready, 1)

            def maxima(b, half):
                pe.wait_ge(ns_ready, 2 * b + half + 1)
                if b:
                    pe.wait_ge(norm_done, 8 * b + (1 if half else -1))
                elif half:
                    pe.wait_ge(mr_ready, 1)
                for q in range(QT):
                    last = nc.tensor.transpose(
                        MRP[0:PARTS * H // 2, q * P:(q + 1) * P],
                        NS[:, half, q, :, :].rearrange("p a h -> p (a h)"), IDB[:, :])
                last.then_inc(mrT_ready, 1)

            def rows_here(b, half):
                pe.wait_ge(mrow[b % 2][half], 48 * (b // 2 + 1))

            def transpose_x1(b, banks):
                for i in range(2):
                    for t in range(2):
                        for c in range(KC):
                            last = nc.tensor.matmul(banks[i][:, (2 * t + c) * P:(2 * t + c + 1) * P],
                                                    X1[:, 4 * b + 2 * i + t, c * P:(c + 1) * P], IDF[:, :],
                                                    is_transpose=True, start=True, stop=True)
                last.then_inc(x1T_ready, 1)

            for g0, n in ((0, 4), (4, 2), (6, 2)):
                if g0 != 6:
                    stacks_here(pe, 0, g0 // 4)
                else:
                    maxima(0, 0)
                with pe.Fori(g0, g0 + n) as g:
                    for k in range(S1_TILES):
                        s1_tile(g, g, k, S1P6)
            maxima(0, 1)
            rows_here(0, 0)
            s2_tile(0, 0, 0)
            s2_tile(0, 0, 1)
            for b in range(NB):
                more = b < NB - 1
                if more:
                    stacks_here(pe, b + 1, 0)
                with pe.Fori(0, 2) as g:
                    group(b, g)
                rows_here(b, 1)
                with pe.Fori(2, 4) as g:
                    group(b, g)
                if more:
                    stacks_here(pe, b + 1, 1)
                else:
                    pe.wait_ge(x1_ready, NB - 1)
                    transpose_x1(0, S1P)
                with pe.Fori(4, 6) as g:
                    group(b, g)
                if not more:
                    pe.wait_ge(x1T_copied, 2)
                    transpose_x1(1, S1P)
                group(b, 6, with_maxima=more)
                if more:
                    rows_here(b + 1, 0)
                else:
                    pe.wait_ge(x1T_copied, 4)
                    transpose_x1(2, S1P)
                group(b, 7, with_next=more)
                if not more:
                    pe.wait_ge(x1T_copied, 6)
                pe.wait_ge(s1_free, S1_TILES * G * min(b + 2, NB) + 6)
                pe.wait_ge(norm_done, 8 * b + 9)
                for hd in range(KC):
                    for q in range(2):
                        for c in range(KC):
                            last = nc.tensor.matmul(S1P[hd][:, q * D:(q + 1) * D],
                                                    CTX[:, 2 * q + c, hd * P:(hd + 1) * P], WO[:, c, :],
                                                    start=(c == 0), stop=(c == KC - 1))
                    last.then_inc(oproj_ready, 1)
                    if hd == 0 and more:
                        maxima(b + 1, 1)
                if more:
                    pe.wait_ge(mr_ready, 2 * b + 4)
                pe.wait_ge(oproj_used, 2 * b + 2)

            pe.wait_ge(ld_w13, 16)
            pe.wait_ge(ld_w2, 32)

            def unit_h(u):
                t, e = divmod(u, 2)
                if u >= 2:
                    pe.wait_ge(sh_g, u - 1)
                for c in range(KC):
                    last = nc.tensor.matmul(HP[u % 2][:, 0:2 * I], x1T[:, c, t * P:(t + 1) * P],
                                            w13_sb[:, c, E + e, :], start=(c == 0), stop=(c == KC - 1))
                last.then_inc(sh_h, 1)

            def transpose_g(dst, g, done):
                for c in range(2):
                    last = nc.tensor.matmul(dst[0:IH, c * P:(c + 1) * P], g[:, c * IH:(c + 1) * IH],
                                            IDF[:, :], is_transpose=True, start=True, stop=True)
                last.then_inc(done, 1)

            def unit_y(u):
                t, e = divmod(u, 2)
                pe.wait_ge(sh_gts, u + 1)
                if e == 0 and t >= 2:
                    pe.wait_ge(sh_yused, t - 1)
                for c in range(2):
                    last = nc.tensor.matmul(YP[t % 2][:, 0:D], GTS[u % 2][:, c, :], w2s_sb[:, e, c, :],
                                            start=(e == 0 and c == 0), stop=(e == 1 and c == 1))
                last.then_inc(sh_y, 1)

            def units(u0, u1):
                for u in range(u0, u1):
                    if u + 1 < UNITS:
                        unit_h(u + 1)
                    pe.wait_ge(sh_g, u + 1)
                    if u >= 2:
                        pe.wait_ge(sh_gts, u - 1)
                    transpose_g(TGP[u % 2], GG[u % 2], sh_gT)
                    if u >= 1:
                        unit_y(u - 1)

            unit_h(0)
            units(0, 1)
            pe.wait_ge(x1_ready, NB)
            transpose_x1(NB - 1, TXP)
            units(1, 2)
            pe.wait_ge(x1T_copied, 2 * NB)
            for t in range(NT):
                for c in range(KC):
                    last = nc.tensor.matmul(MIS[:, t * E:(t + 1) * E], x1T[:, c, t * P:(t + 1) * P], GT[:, c, :],
                                            start=(c == 0), stop=(c == KC - 1))
            last.then_inc(logits_ready, 1)
            units(2, 12)
            pe.wait_ge(mb_ready, 1)
            nc.tensor.matmul(MIS[:, 0:NT * E], UPPER[:, :], MB[:, :, :], start=True, stop=True)
            for t in range(NT - 1):
                later = MB[:, t, :].unsqueeze(1).broadcast_to([P, NT - 1 - t, E])
                nc.tensor.matmul(MIS[:, (t + 1) * E:NT * E].rearrange("p (t e) -> p t e", e=E), ONES[:, :],
                                 later, start=False, stop=True, skip_group_check=True)
            for t in range(NT):
                last = nc.tensor.matmul(PVP[:, 0:E], ONES[:, :], MB[:, t, :], start=(t == 0), stop=(t == NT - 1))
            last.then_inc(pre_ready, 1)
            units(12, 22)

            def place_tables(c):
                pe.wait_ge(onehot_ready, c + 1)
                pe.wait_ge(wprod_ready, c + 1)
                for k in range(CH * TOPK):
                    last = nc.tensor.matmul(PVP[:, 0:2 * HI], OHLO[:, k, :], RH[:, k, :],
                                            start=(c == 0 and k == 0),
                                            stop=(c == NT // CH - 1 and k == CH * TOPK - 1))
                last.then_inc(tab_ready, 1)

            for c, (u0, u1) in enumerate(((22, 24), (24, 26), (26, 28), (28, 30))):
                place_tables(c)
                units(u0, u1)
            units(30, UNITS)
            unit_y(UNITS - 1)

            def expert(n):
                return pe.value_load(EOT[0:1, n], min_val=0, max_val=E - 1)

            def tile_x(n, p, k):
                pe.wait_ge(xts_ready, n + 1)
                for c in range(KC):
                    last = nc.tensor.matmul(TXP[p][:, c * P:(c + 1) * P], XS[k][:, c * P:(c + 1) * P], IDF[:, :],
                                            is_transpose=True, start=True, stop=True)
                last.then_inc(xT_ready, 1)

            def tile_h(n, p, e):
                pe.wait_ge(xts_ready, n + 3)
                pe.wait_ge(g_ready, n + 1)
                for c in range(KC):
                    last = nc.tensor.matmul(HP[p][:, 0:2 * I], XTS[p][:, c, :], w13_sb[:, c, ds(e, 1), :],
                                            start=(c == 0), stop=(c == KC - 1))
                last.then_inc(h_ready, 1)

            def tile_g(n, p):
                pe.wait_ge(g_ready, n + 3)
                pe.wait_ge(gts_ready, n + 1)
                transpose_g(TGP[p], GG[p], gT_ready)

            def tile_y(n, p, e):
                pe.wait_ge(gts_ready, n + 3)
                pe.wait_ge(ys_ready, n + 1)
                for c in range(2):
                    last = nc.tensor.matmul(YP[p][:, 0:D], GTS[p][:, c, :], w2_sb[:, ds(e, 1), c, :],
                                            start=(c == 0), stop=(c == 1))
                last.then_inc(y_ready, 1)

            def one(n):
                return slice(n, n + 1)

            pe.wait_ge(idx_ready, 1)
            pe.sem_inc(y_ready, 2)
            pe.sem_inc(h_ready, 2)
            pe.sem_inc(gT_ready, 2)
            for n in range(2):
                pe.wait_ge(xs_in[n], 16)
                tile_x(n, n, n)
            tile_h(0, 0, expert(one(0)))
            tile_h(1, 1, expert(one(1)))
            pe.wait_ge(xs_in[2], 16)
            tile_x(2, 0, 2)
            tile_g(0, 0)
            LOOPED = (TILES - 3) // 4 * 4
            with pe.Fori(0, LOOPED // 4) as i:
                for k in range(4):
                    n = 4 * i + (k + 1)
                    p = (k + 1) % 2
                    tile_h(n + 1, 1 - p, expert(ds(n + 1, 1)))
                    pe.wait_ge(xs_in[(k + 3) % 4], 16 * i + 16 * ((k + 3) // 4 + 1))
                    tile_x(n + 2, p, (k + 3) % 4)
                    tile_g(n, p)
                    tile_y(n - 1, 1 - p, expert(ds(n - 1, 1)))
            for n in range(LOOPED + 1, TILES):
                p = n % 2
                if n + 1 < TILES:
                    tile_h(n + 1, 1 - p, expert(one(n + 1)))
                if n + 2 < TILES:
                    pe.wait_ge(xs_in[(n + 2) % 4], 16 * ((n + 2) // 4 + 1))
                    tile_x(n + 2, p, (n + 2) % 4)
                tile_g(n, p)
                tile_y(n - 1, 1 - p, expert(one(n - 1)))
            tile_y(TILES - 1, (TILES - 1) % 2, expert(one(TILES - 1)))

        @block.vector
        def _(dve):
            steps = [0]

            def link(ins, wait=True):
                steps[0] += 1
                ins.then_inc(dve_step, 1)
                if wait:
                    dve.wait_ge(dve_step, steps[0])

            dve.sem_inc(s1_free, 6)
            dve.sem_inc(norm_done, 1)
            nc.vector.memset(CTX[:, 0, :], 0.0).then_inc(zero_ready, 1)
            dve.wait_ge(ld_tab, 32)

            def rest(u):
                n = P if u % 3 < 2 else 64
                dve.wait_ge(hi_ready, u + 1)
                nc.vector.tensor_tensor(rope_t[0:n, u % UB, 3, :], rope_t[0:n, u % UB, 2, :],
                                        parts[0:n, u % UB, 0, :], ALU.subtract).then_inc(rest1_ready, 1)

            for u in range(3 * NB):
                m = u % 3
                dve.wait_ge(proj_ready, u + 1)
                if u >= UB:
                    dve.wait_ge(lo_ready, u - UB + 1)
                n = P if m < 2 else 64
                t1, t2, rot = (rope_t[0:n, u % UB, k, :] for k in range(3))
                if m < 2:
                    straight, swapped, sn = S2P[m][:, 0, :], S2P[m][:, 1, :], SIN
                else:
                    straight, swapped, sn = S1P[0][0:64, :], S1P[0][64:128, :], SIN[64:128, :]
                link(nc.vector.tensor_tensor(t1, straight, COS[0:n, :], ALU.mult), False)
                link(nc.vector.tensor_tensor(t2, swapped, sn, ALU.mult))
                dve.sem_inc(proj_used, 1)
                nc.vector.tensor_tensor(rot, t1, t2, ALU.add).then_inc(rot_ready, 1)
                if u >= 1:
                    rest(u - 1)
            rest(3 * NB - 1)

            def s1_max(s, g, k, banks=S1P):
                q, h0, nh = S1[k]
                w = P * (q + 1)
                dve.wait_ge(s1_ready, s * S1_TILES + k + 1)
                nc.vector.tensor_reduce(NM[:, q, ds(g * GH + h0, nh)],
                                        banks[k % len(banks)][:, 0:nh * w].rearrange("p (h k) -> p h k", h=nh),
                                        AXX, ALU.max, negate=True).then_inc(s1_free, 1)

            def split_maxima(b, half):
                dve.wait_ge(s1_free, S1_TILES * (8 * b + 4 * half + 4) + 6)
                if b >= 1:
                    dve.wait_ge(mrT_ready, 2 * (b - 1) + half + 1)
                nm = NM[:, :, half * H // 2:(half + 1) * H // 2]
                ns = NS[:, half, :, :, :]
                link(nc.vector.tensor_copy(ns[:, :, 0, :], nm))
                link(nc.vector.tensor_tensor(NR[:, 0, :, :], nm, ns[:, :, 0, :], ALU.subtract))
                link(nc.vector.tensor_copy(ns[:, :, 1, :], NR[:, 0, :, :]))
                link(nc.vector.tensor_tensor(NR[:, 1, :, :], NR[:, 0, :, :], ns[:, :, 1, :], ALU.subtract))
                nc.vector.tensor_copy(ns[:, :, 2, :], NR[:, 1, :, :]).then_inc(ns_ready, 1)

            for half in range(2):
                with dve.Fori(4 * half, 4 * half + 4) as g:
                    for k in range(S1_TILES):
                        s1_max(g, g, k, S1P6)
                split_maxima(0, half)
            dve.wait_ge(ld_res, 16)
            dve.wait_ge(zeroed, 48)
            ctx_v = CTX[:, :, :].rearrange("p q (g j d) -> p q g j d", g=G, j=GH)

            def groups(b, g0, n):
                with dve.Fori(g0, g0 + n) as g:
                    s = g + 8 * b
                    if b < NB - 1:
                        for k in range(S1_TILES):
                            s1_max(s + 8, g, k)
                    dve.wait_ge(ctxT_ready, s + 2)
                    nc.vector.reciprocal(RC[:, :, :], CTXP[:, :, :, HD]).then_inc(dve_step, 1)
                    dve.wait_ge(dve_step, g + (steps[0] + 1 - g0))
                    nc.vector.tensor_tensor(ctx_v[:, :, ds(g, 1), :, :].rearrange("p q g j d -> p q (g j) d"),
                                            CTXP[:, :, :, 0:HD],
                                            RC[:, :, :].unsqueeze(3).broadcast_to([P, QT, GH, HD]),
                                            ALU.mult).then_inc(norm_done, 1)
                steps[0] += n

            def residual(b):
                for hd in range(KC):
                    dve.wait_ge(oproj_ready, 2 * b + hd + 1)
                    t = 4 * b + 2 * hd
                    nc.vector.tensor_tensor(X1[:, t:t + 2, :], S1P[hd][:, :].rearrange("p (q d) -> p q d", q=2),
                                            X1[:, t:t + 2, :], ALU.add).then_inc(oproj_used, 1)
                dve.wait_ge(oproj_used, 2 * b + 2)
                for k in range(4):
                    link(nc.vector.bn_stats(ST[:, k, :], X1[:, 4 * b + k, :]), False)
                dve.wait_ge(dve_step, steps[0])
                for k in range(4):
                    link(nc.vector.bn_aggr(MV[:, 4 * b + k, :], ST[:, k, :]), False)
                dve.wait_ge(dve_step, steps[0])
                dve.sem_inc(var_ready, 1)

            def normalise(b):
                for t in range(4 * b, 4 * b + 4):
                    link(nc.vector.tensor_scalar(X1[:, t, :], X1[:, t, :], MV[:, t, 0:1], RSTD[:, t:t + 1],
                                                 ALU.subtract, ALU.mult), False)
                dve.wait_ge(dve_step, steps[0])
                dve.sem_inc(x1_ready, 1)

            def copy_x1T(b):
                dve.wait_ge(x1T_ready, b + 1)
                for i in range(2):
                    t = (4 * b + 2 * i) * P
                    nc.vector.tensor_copy(x1T[:, :, t:t + 2 * P].rearrange("p c (t n) -> p t c n", n=P),
                                          S1P[i][:, :].rearrange("p (t c n) -> p t c n", t=2, c=KC)).then_inc(
                                              x1T_copied, 1)

            for b in range(NB - 1):
                for half in range(2):
                    groups(b, 4 * half, 4)
                    split_maxima(b + 1, half)
                residual(b)
            b = NB - 1
            groups(b, 0, 2)
            dve.wait_ge(std_ready, 1)
            link(nc.vector.reciprocal(RSTD[:, 0:4 * b], SD[:, 0:4 * b]))
            for i in range(b):
                normalise(i)
            groups(b, 2, 2)
            copy_x1T(0)
            groups(b, 4, 2)
            copy_x1T(1)
            groups(b, 6, 1)
            copy_x1T(2)
            groups(b, 7, 1)
            residual(b)
            dve.wait_ge(std_ready, 2)
            link(nc.vector.reciprocal(RSTD[:, 4 * b:4 * b + 4], SD[:, 4 * b:4 * b + 4]))
            normalise(b)

            def units(u0, u1):
                for u in range(u0, u1):
                    dve.wait_ge(sh_silu, u + 1)
                    if u >= 2:
                        dve.wait_ge(sh_gT, u - 1)
                    nc.vector.tensor_tensor(GG[u % 2], SILU[u % 2], HP[u % 2][:, I:2 * I],
                                            ALU.mult).then_inc(sh_g, 1)
                    if u % 2 and u >= 3:
                        unit_out(u // 2 - 1)

            def unit_out(t):
                dve.wait_ge(sh_y, 2 * t + 2)
                dve.wait_ge(x1_out[t // 4], 16)
                nc.vector.tensor_tensor(X1[:, t, :], YP[t % 2][:, 0:D], X1[:, t, :], ALU.add).then_inc(
                    sh_yused, 1)

            dve.wait_ge(pv_done, 4 * NB * G + 4)
            units(0, 2)
            dve.wait_ge(score_ready, 1)
            dve.wait_ge(consts_ready, 18)
            sg = SC.rearrange("p t (g k) -> p t g k", g=4)
            link(nc.vector.tensor_reduce(GS, sg, AXX, ALU.max))
            other = GS.unsqueeze(2).broadcast_to([P, NT, 4, 4])
            own = GS.unsqueeze(3).broadcast_to([P, NT, 4, 4])
            low = LOWER[:, :, :].unsqueeze(1).broadcast_to([P, NT, 4, 4])
            link(nc.vector.tensor_tensor(GA, other, own, ALU.is_gt), False)
            link(nc.vector.tensor_tensor(GB, other, own, ALU.is_equal))
            link(nc.vector.tensor_tensor(GB, GB, low, ALU.mult))
            link(nc.vector.tensor_tensor(GA, GA, GB, ALU.add))
            link(nc.vector.tensor_reduce(GR, GA, AXX, ALU.add))
            link(nc.vector.tensor_scalar(GR, GR, 2.0, None, ALU.is_lt))
            link(nc.vector.tensor_tensor(MSK.rearrange("p t (g k) -> p t g k", g=4), sg,
                                         GR.unsqueeze(3).broadcast_to([P, NT, 4, 4]), ALU.mult))
            units(2, 4)
            for t in range(NT):
                link(nc.vector.max(TOP[:, t, :], MSK[:, t, :]), False)
            dve.wait_ge(dve_step, steps[0])
            for t in range(NT):
                link(nc.vector.max_index(TOPI[:, t, :], TOP[:, t, :], MSK[:, t, :]), False)
            dve.wait_ge(dve_step, steps[0])
            units(4, 7)
            link(nc.vector.tensor_copy(TOPF, TOPI))
            by_t = [P, NT, TOPK, E]
            link(nc.vector.tensor_tensor(OHJ, TOPF[:, :, 0:TOPK].unsqueeze(3).broadcast_to(by_t),
                                         IOTA[:, 0:E].unsqueeze(1).unsqueeze(1).broadcast_to(by_t),
                                         ALU.is_equal))
            with nc.allow_low_precision("zeros and ones"):
                nc.vector.tensor_reduce(MB[:, :, :], OHJ.rearrange("p t j e -> p t e j"), AXX,
                                        ALU.add).then_inc(mb_ready, 1)
            link(nc.vector.tensor_tensor(TMJ, OHJ, SC.unsqueeze(2).broadcast_to(by_t), ALU.mult))
            link(nc.vector.tensor_reduce(WJ, TMJ, AXX, ALU.add))
            units(7, 9)
            link(nc.vector.tensor_reduce(WSUM, WJ, AXX, ALU.add))
            link(nc.vector.reciprocal(WREC, WSUM))
            link(nc.vector.tensor_tensor(WJ, WJ, WREC.unsqueeze(2).broadcast_to([P, NT, TOPK]), ALU.mult))
            units(9, 12)
            dve.wait_ge(pre_ready, 1)
            sq = [P, E, E]
            cmp = MSK.rearrange("p a b -> p (a b)").rearrange("p (a b) -> p a b", a=E)
            link(nc.vector.tensor_scalar(EMPTY[:, 0:E], IOTA[:, 0:E], float(P), None, ALU.mult), False)
            link(nc.vector.tensor_copy(NEXP, PVP[:, 0:E]))
            link(nc.vector.tensor_tensor(cmp, NEXP.unsqueeze(2).broadcast_to(sq),
                                         EMPTY[:, 0:E].unsqueeze(1).broadcast_to(sq), ALU.is_gt))
            link(nc.vector.tensor_reduce(KEXP, cmp, AXX, ALU.add))
            link(nc.vector.tensor_tensor(cmp, KEXP.unsqueeze(1).broadcast_to(sq), LOWER16[:, :, :], ALU.mult))
            link(nc.vector.tensor_reduce(BASE, cmp, AXX, ALU.add))
            link(nc.vector.tensor_tensor(ENDS, BASE, KEXP, ALU.add), False)
            link(nc.vector.scalar_tensor_tensor(out=POS, in0=BASE.unsqueeze(1).broadcast_to([P, NT, E]),
                                                scalar=float(P),
                                                in1=MIS[:, 0:NT * E].rearrange("p (t e) -> p t e", t=NT),
                                                op0=ALU.mult, op1=ALU.add))
            link(nc.vector.tensor_tensor(TMJ, OHJ, POS.unsqueeze(2).broadcast_to(by_t), ALU.mult))
            link(nc.vector.tensor_reduce(PJ.rearrange("p (t j) -> p t j", j=TOPK), TMJ, AXX, ALU.add))
            units(12, 14)
            link(nc.vector.tensor_copy(PU, PJ))
            link(nc.vector.tensor_scalar(HU, PU, 7, None, ALU.logical_shift_right), False)
            link(nc.vector.tensor_scalar(LU, PU, P - 1, None, ALU.bitwise_and))
            link(nc.vector.tensor_copy(HF, HU), False)
            link(nc.vector.tensor_copy(LF, LU))

            def onehots(c):
                n = CH * TOPK
                ch = slice(c * n, (c + 1) * n)
                if c:
                    dve.wait_ge(tab_ready, c)
                nc.vector.tensor_tensor(OHHI, HF[:, ch].unsqueeze(2).broadcast_to([P, n, HI]),
                                        IOTA[:, 0:HI].unsqueeze(1).broadcast_to([P, n, HI]),
                                        ALU.is_equal).then_inc(hi_made, 1)
                link(nc.vector.tensor_tensor(OHLO, LF[:, ch].unsqueeze(2).broadcast_to([P, n, P]),
                                             IOTA[:, :].unsqueeze(1).broadcast_to([P, n, P]), ALU.is_equal))
                dve.wait_ge(hi_made, c + 1)
                nc.vector.tensor_tensor(RH[:, :, 0:HI], OHHI,
                                        TID1[:, :, :].rearrange("p t j -> p (t j)")[:, ch].unsqueeze(2)
                                        .broadcast_to([P, n, HI]), ALU.mult).then_inc(onehot_ready, 1)

            onehots(0)
            units(14, 22)
            for c, (u0, u1) in enumerate(((22, 24), (24, 26), (26, 28), (28, 30))):
                if c < 3:
                    onehots(c + 1)
                units(u0, u1)
            dve.wait_ge(tab_ready, 4)
            dve.wait_ge(wprod_ready, 4)
            ends = RH.rearrange("p a b -> p (a b)")[:, 0:HI * E].rearrange("p (n e) -> p n e", e=E)
            link(nc.vector.tensor_tensor(ends, ENDS.unsqueeze(1).broadcast_to([P, HI, E]),
                                         IOTA[:, 0:HI].unsqueeze(2).broadcast_to([P, HI, E]), ALU.is_le))
            link(nc.vector.tensor_reduce(EOTF[:, :], ends, AXX, ALU.add))
            link(nc.vector.tensor_scalar(EOTF[:, :], EOTF[:, :], float(E - 1), None, ALU.min))
            link(nc.vector.tensor_copy(EOT[:, :], EOTF[:, :]), False)
            link(nc.vector.tensor_scalar(IDXF, PVP[:, 0:HI], -1.0, None, ALU.add), False)
            link(nc.vector.tensor_scalar(EMPTY, PVP[:, 0:HI], 0.0, PADROW[:, 0:1], ALU.is_equal, ALU.mult), False)
            link(nc.vector.tensor_copy(WT[:, :], PVP[:, HI:2 * HI]))
            link(nc.vector.tensor_tensor(IDXF, IDXF, EMPTY, ALU.add))
            link(nc.vector.tensor_copy(IDX[:, :], IDXF))
            dve.sem_inc(idx_ready, 1)
            units(30, UNITS)
            unit_out(NT - 1)

            dve.wait_ge(sh_yused, NT)
            dve.sem_inc(xts_ready, 2)
            dve.sem_inc(g_ready, 2)
            dve.sem_inc(ys_ready, 2)

            def copy_xT(n, p):
                dve.wait_ge(xT_ready, n + 1)
                dve.wait_ge(h_ready, n + 1)
                nc.vector.tensor_copy(XTS[p], TXP[p][:, 0:D].rearrange("p (c t) -> p c t", c=KC)).then_inc(
                    xts_ready, 1)

            def product(n, p):
                dve.wait_ge(silu_ready, n + 1)
                dve.wait_ge(gT_ready, n + 1)
                weight = WT[:, n:n + 1] if isinstance(n, int) else WT[:, ds(n, 1)]
                nc.vector.scalar_tensor_tensor(out=GG[p], in0=SILU[p], scalar=weight, in1=HP[p][:, I:2 * I],
                                               op0=ALU.mult, op1=ALU.mult).then_inc(g_ready, 1)

            def result(n, k):
                dve.wait_ge(y_ready, n + 3)
                nc.vector.tensor_copy(YS[k], YP[k % 2][:, 0:D]).then_inc(ys_ready, 1)

            def tile(n):
                if n + 2 < TILES:
                    copy_xT(n + 2, n % 2)
                if n + 1 < TILES:
                    product(n + 1, (n + 1) % 2)
                if n >= 1:
                    if n >= 5:
                        dve.wait_ge(acc_done[(n - 1) % 2], 16 * ((n - 1) // 2 - 1))
                    result(n - 1, (n - 1) % 4)

            copy_xT(0, 0)
            copy_xT(1, 1)
            product(0, 0)
            for n in range(5):
                tile(n)
            rounds = (TILES - 2 - 5) // 4
            with dve.Fori(0, rounds) as i:
                for k in range(4):
                    n = 4 * i + (k + 5)
                    copy_xT(n + 2, (k + 1) % 2)
                    product(n + 1, k % 2)
                    dve.wait_ge(acc_done[k % 2], 32 * i + 16 * (1 + k // 2))
                    result(n - 1, k)
            for n in range(5 + 4 * rounds, TILES):
                tile(n)
            dve.wait_ge(acc_done[(TILES - 1) % 2], 16 * ((TILES - 1) // 2 - 1))
            result(TILES - 1, (TILES - 1) % 4)

            for b in range(NB):
                dve.wait_ge(acc_in[b], 32)
                ts = slice(4 * b, 4 * b + 4)
                link(nc.vector.tensor_tensor(X1[:, ts, :], FIN[0][:, ts, :], FIN[1][:, ts, :], ALU.add))
                for k in range(4):
                    link(nc.vector.bn_stats(ST[:, k, :], X1[:, 4 * b + k, :]), False)
                dve.wait_ge(dve_step, steps[0])
                for k in range(4):
                    link(nc.vector.bn_aggr(MV[:, 4 * b + k, :], ST[:, k, :]), False)
                dve.wait_ge(dve_step, steps[0])
                dve.sem_inc(var_ready, 1)
                dve.wait_ge(std_ready, 3 + b)
                link(nc.vector.reciprocal(RSTD[:, ts], SD[:, ts]))
                for k in range(4):
                    t = 4 * b + k
                    link(nc.vector.tensor_scalar(X1[:, t, :], X1[:, t, :], MV[:, t, 0:1], RSTD[:, t:t + 1],
                                                 ALU.subtract, ALU.mult), False)
                dve.wait_ge(dve_step, steps[0])
                dve.sem_inc(out_ready, 1)


def tables():
    import numpy as np
    half = HD // 2
    inv = (np.float32(1.0) / np.float32(10000.0) ** (np.arange(half, dtype=np.float32) * np.float32(2.0) /
                                                      np.float32(HD))).astype(np.float32)
    ang = np.arange(T, dtype=np.float32)[:, None] * inv[None, :]
    c, s = np.cos(ang).astype(np.float32).T, np.sin(ang).astype(np.float32).T
    cos = np.tile(np.concatenate([c, c]), (P // HD, 1))
    sin = np.tile(np.concatenate([-s, s]), (P // HD, 1))
    return np.ascontiguousarray(cos), np.ascontiguousarray(sin)


def kernel(L0_attn_x, L0_attn_Wq, L0_attn_Wk, L0_attn_Wv, L0_attn_Wo, L0_ffn_gate_w, L0_ffn_W1, L0_ffn_W2,
           L0_ffn_W3, L0_ffn_Ws1, L0_ffn_Ws2, L0_ffn_Ws3):
    import numpy as np
    import concourse.bacc as bacc
    from concourse.bass_utils import run_bass_kernel_spmd

    def halves_swapped(w):
        return w.reshape(D, -1, 2, HD // 2)[:, :, ::-1].reshape(D, -1)

    x = np.asarray(L0_attn_x).reshape(NB * T, D)
    wq, wk, wv = (np.asarray(w) for w in (L0_attn_Wq, L0_attn_Wk, L0_attn_Wv))
    wqkv = np.concatenate([wq, halves_swapped(wq), wk, halves_swapped(wk), wv], axis=1)
    w1 = np.concatenate([np.asarray(L0_ffn_W1), np.asarray(L0_ffn_Ws1).reshape(2, I, D)])
    w3 = np.concatenate([np.asarray(L0_ffn_W3), np.asarray(L0_ffn_Ws3).reshape(2, I, D)])
    w13 = np.concatenate([w1, w3], axis=1).transpose(2, 0, 1)
    w2 = np.concatenate([np.asarray(L0_ffn_W2), np.asarray(L0_ffn_Ws2).reshape(D, 2, I).transpose(1, 0, 2)])
    w2 = w2.transpose(2, 0, 1).reshape(2, IH, NE, D).transpose(1, 2, 0, 3)
    cos, sin = tables()
    ins = {"x": x, "xT": x.T, "wqkv": wqkv, "wo": np.asarray(L0_attn_Wo), "cos": cos, "sin": sin,
           "gateT": np.asarray(L0_ffn_gate_w).T, "w13": w13, "w2": w2}
    nc = bacc.Bacc("TRN2", target_bir_lowering=False, num_devices=1)
    arrays, args = {}, []
    for name, a in ins.items():
        arrays[f"in_{name}"] = np.ascontiguousarray(a)
        args.append(nc.dram_tensor(f"in_{name}", a.shape, mybir.dt.from_np(a.dtype), kind="ExternalInput").ap())
    args.append(nc.dram_tensor("out_x", (NB * T, D), F32, kind="ExternalOutput").ap())
    program(nc, *args)
    r = run_bass_kernel_spmd(nc, [arrays], core_ids=[0])
    return r.results[0]["out_x"].reshape(NB, T, D)
```

```python
from contextlib import ExitStack

import concourse.bass as bass
from concourse import mybir

F32 = mybir.dt.float32
BF16 = mybir.dt.bfloat16
U32 = mybir.dt.uint32
ALU = mybir.AluOpType
ACT = mybir.ActivationFunctionType
AXX = mybir.AxisListType.X
ds = bass.ds

P = 128
NB, T, D = 4, 512, 256
H, G, HD = 32, 8, 8
GH = H // G
QT = T // P
KC = D // P
NT = NB * T // P
E, I = 16, 176
NE = E + 2
IH = I // 2
PARTS = 3
ROWS = PARTS * PARTS * HD
KROWS = ROWS + PARTS
SLOTS = 2 * G
NEG = -3.0e38
EPS = 1e-5
SCALE = float(HD) ** -0.5
TOPK = 4
TJ = NT * TOPK
TOKENS = NB * T
TILES = (TOKENS * TOPK + E * (P - 1)) // P
HI = TILES + 1
PAD = TOKENS
CW = (P, P, 2 * I - 2 * P)
SB = 2 * P
UNITS = NT * P // SB * len(CW)
PIECES = NT // 2
CH = 4

PAIRS = ("q0", "k", "q1", "q2", "q3")
SCR = {"q": 16 * PARTS, "k": 32 * PARTS}
WC = 2 * P + 2 * HD // 2 * G + G * HD
V0 = WC - G * HD
S1_TILES = 12
S2_TILES = 6
S1 = [(1, 0, 2), (1, 2, 2)] + [(q, h, 1) for q in (3, 2) for h in range(GH)] + [(0, 0, 2), (0, 2, 2)]
EXPS = (2, 4, 5, 6)
S2 = [(0, 0, 2), (0, 2, 2), (1, 0, 2), (1, 2, 2), (2, 0, 4), (3, 0, 4)]


def program(nc, x, xT, wqkv, wo, cos, sin, gateT, w13, w2, ws2, out):
    q_scr = nc.dram_tensor("q_parts", (NB, PARTS, HD, H, T), BF16, kind="Internal").ap()
    k_scr = nc.dram_tensor("k_parts", (NB, PARTS, HD, G, T), BF16, kind="Internal").ap()
    x1_scr = nc.dram_tensor("x1_rows", (TOKENS + P, D), F32, kind="Internal").ap()
    acc = [nc.dram_tensor(f"acc{i}", (TOKENS + P, D), F32, kind="Internal").ap() for i in range(2)]
    with ExitStack() as ctx:
        def sb(name, shape, dt=F32):
            return ctx.enter_context(nc.sbuf_tensor(name, shape, dt))

        def psum(name, shape):
            return ctx.enter_context(nc.psum_tensor(name, shape, F32))

        def sem(name):
            return ctx.enter_context(nc.semaphore(name))

        def taker(region):
            at = [0]

            def take(*shape, dt=F32, rows=P):
                n = 1
                for d in shape:
                    n *= d
                view = region[0:rows, at[0]:at[0] + n]
                at[0] += n
                names = [f"x{i}" for i in range(len(shape))]
                if len(shape) > 1:
                    view = view.rearrange(f"p ({' '.join(names)}) -> p {' '.join(names)}",
                                          **{m: d for m, d in zip(names[1:], shape[1:])})
                return view if dt == F32 else view.bitcast(dt)
            return take

        EARLY = sb("EARLY", [P, KC * TOKENS])
        WQ = EARLY[:, 0:KC * WC].rearrange("p (c n) -> p c n", c=KC)
        COS = [EARLY[:, KC * WC + 2 * i * T:KC * WC + (2 * i + 1) * T] for i in range(2)]
        SIN = [EARLY[:, KC * WC + (2 * i + 1) * T:KC * WC + (2 * i + 2) * T] for i in range(2)]
        x1T = EARLY[:, :].rearrange("p (c t) -> p c t", c=KC)
        WO = sb("WO", [P, KC, D])
        GT = sb("GT", [P, KC, E])
        XT = sb("XT", [P, KC * NB * T])
        xT_sb = XT[:, :].rearrange("p (c t) -> p c t", c=KC)
        X1 = XT[:, :].rearrange("p (n d) -> p n d", n=NT)
        QS = sb("QS", [P, SLOTS * GH * T // 2])
        qs = QS[:, :].bitcast(BF16).rearrange("p (s h t) -> p s h t", s=SLOTS, h=GH)
        w2_sb = QS[0:IH, 0:E * 2 * D].rearrange("p (e c d) -> p e c d", e=E, c=2)
        KS = sb("KS", [P, SLOTS, T], BF16)
        w2s_sb = KS[:, 0:3, :].rearrange("p s t -> p (s t)").bitcast(F32).rearrange("p (c d) -> p c d", c=3)
        W13 = sb("W13", [P, KC * NE * 2 * I])
        w13_sb = W13[:, :].rearrange("p (c e n) -> p c e n", c=KC, e=NE)
        in_w13 = taker(W13)
        COSP, SINP = in_w13(2, T), in_w13(2, T)
        ROT = [in_w13(2, T) for _ in range(2)]
        REST = [in_w13(2, T) for _ in range(2)]
        parts = [in_w13(PARTS, T).bitcast(BF16).rearrange("p a (h t) -> p a h t", h=2) for _ in range(4)]
        VA = sb("VA", [P, NT, G * HD])
        VC = sb("VC", [P, QT, 32])
        ATT = sb("ATT", [P, GH * sum(T - P * k for k in range(QT))])
        PT, at = [], 0
        for k in range(QT):
            PT.append(ATT[:, at:at + GH * (T - P * k)].rearrange("p (h t) -> p h t", h=GH))
            at += GH * (T - P * k)
        PVS = sb("PVS", [P, T])
        RC = sb("RC", [P, QT, GH])
        CTX = sb("CTX", [P, QT, D])
        NM = sb("NM", [P, QT, H])
        NR = sb("NR", [P, 2, QT, H // 2])
        NS = sb("NS", [P, 2, QT, PARTS, H // 2], BF16)
        MR = sb("MR", [PARTS * H // 2, 2, T], BF16)
        IDF = sb("IDF", [P, P])
        IDB = sb("IDB", [P, P], BF16)
        MQ = sb("MQ", [P, GH, P], BF16)
        EPSC = sb("EPSC", [P, 1])
        ST = sb("ST", [P, QT, 6])
        MV = sb("MV", [P, NT, 2])
        SD = sb("SD", [P, NT])
        RSTD = sb("RSTD", [P, NT])
        SHIFT = sb("SHIFT", [P, NT])
        in_att = taker(ATT)
        in_gt = taker(ATT[:, 8 * D:])
        SG = [in_gt(len(CW), SB) for _ in range(2)]
        XS = [in_att(D) for _ in range(4)]
        YS = [in_att(D) for _ in range(4)]
        GG = [in_att(I) for _ in range(2)]
        SILU = [in_att(I) for _ in range(2)]
        GTS = [in_att(2, P, rows=IH) for _ in range(2)]
        XTS = [in_att(KC, P) for _ in range(2)]
        SC = in_att(NT, E)
        MSK = in_att(NT, E)
        GS = in_att(NT, 4)
        GR = in_att(NT, 4)
        GA = in_att(NT, 4, 4)
        GB = in_att(NT, 4, 4)
        in_qs = taker(QS[:, SLOTS * GH * T // 4:SLOTS * GH * T // 2])
        OHJ = in_qs(NT, TOPK, E)
        TMJ = in_qs(NT, TOPK, E)
        in_ks = taker(KS[:, 3:SLOTS, :].rearrange("p s t -> p (s t)").bitcast(F32))
        in_tiles = taker(ATT)
        in_va = taker(VA[:, :, :].rearrange("p n v -> p (n v)"))
        SILS = [in_va(SB) for _ in range(2)]
        OHLO = [in_qs(CH * TOPK, P), in_tiles(CH * TOPK, P)]
        OHHI = [in_qs(CH * TOPK, HI // 2).rearrange("p a b -> p (a b)").bitcast(BF16).rearrange(
            "p (a b) -> p a b", a=CH * TOPK) for _ in range(2)]
        RH = [take(CH * TOPK, 2 * HI) for take in (in_qs, in_ks)]
        POS = in_qs(NT, E)
        in_ctx = taker(CTX[:, :, :].rearrange("p q d -> p (q d)"))
        TOP = in_ctx(NT, 8)
        TOPI = in_ctx(NT, 8, dt=U32)
        TOPF = in_ctx(NT, 8)
        WJ = in_ctx(NT, TOPK)
        WSUM = in_ctx(NT)
        WREC = in_ctx(NT)
        PJ = in_ctx(TJ)
        PU = in_ctx(TJ, dt=U32)
        HU = in_ctx(TJ, dt=U32)
        LU = in_ctx(TJ, dt=U32)
        HF = in_ctx(TJ)
        LF = in_ctx(TJ)
        NEXP = in_ctx(E)
        KEXP = in_ctx(E)
        BASE = in_ctx(E)
        ENDS = in_ctx(E)
        in_pvs = taker(PVS)
        IDXF = in_pvs(HI)
        EMPTY = in_pvs(HI)
        IDX = sb("IDX", [P, HI], U32)
        WT = sb("WT", [P, HI])
        EOTF = sb("EOTF", [P, HI])
        EOT = sb("EOT", [P, HI], U32)
        MB = sb("MB", [P, NT, E], BF16)
        LOWER = sb("LOWER", [P, 4, 4])
        LOWER16 = sb("LOWER16", [P, E, E])
        IOTA = sb("IOTA", [P, P])
        TID1 = sb("TID1", [P, NT, TOPK])
        PADROW = sb("PADROW", [P, 1])
        UPPER = sb("UPPER", [P, P], BF16)
        ONES = sb("ONES", [P, P], BF16)

        S1P = [psum(f"S1P{i}", [P, T]) for i in range(2)]
        S2P = [psum(f"S2P{i}", [P, 2, T]) for i in range(2)]
        PVP = psum("PVP", [P, T])
        MIS = psum("MIS", [P, T])
        CTXP = MIS[:, :].rearrange("p (q j n) -> p q j n", q=QT, j=GH)
        MRP = MIS[:, T // 2:T].bitcast(BF16)
        S1P6 = [S1P[0][:, :], S1P[1][:, :]] + [S2P[i][:, j, :] for i in range(2) for j in range(2)]
        VP = [PVP, MIS, S1P[0], S1P[1]]
        HP = [S2P[0][:, i, :] for i in range(2)]
        TGP = [S2P[1][:, i, :] for i in range(2)]
        YP = [S1P[i] for i in range(2)]
        TXP = [PVP, MIS]

        ld_x = [sem(f"ld_x{b}") for b in range(NB)]; ld_wq = sem("ld_wq"); ld_w = sem("ld_w"); ld_tab = [sem(f"ld_tab{i}") for i in range(2)]
        ld_res = sem("ld_res"); ld_w13 = sem("ld_w13"); ld_w2 = sem("ld_w2")
        consts_ready = sem("consts_ready")
        ones_ready = sem("ones_ready")
        proj_ready = sem("proj_ready")
        proj_used = sem("proj_used")
        v_ready = sem("v_ready"); v_used = sem("v_used")
        rot_ready = sem("rot_ready")
        hi_ready = sem("hi_ready")
        rest1_ready = sem("rest1_ready")
        mid_ready = sem("mid_ready")
        lo_ready = sem("lo_ready")
        scr_done = [sem(f"scr_done_{v}") for v in PAIRS]
        stack = [[sem(f"stack{p}{h}") for h in range(2)] for p in range(2)]
        s1_ready = sem("s1_ready"); s1_free = sem("s1_free")
        s2_ready = sem("s2_ready"); exp_done = sem("exp_done")
        vc_ready = sem("vc_ready"); vc_init = sem("vc_init")
        pv_done = sem("pv_done"); pvs_ready = sem("pvs_ready")
        ctxT_ready = sem("ctxT_ready"); norm_done = sem("norm_done")
        dve_step = sem("dve_step")
        ns_ready = sem("ns_ready"); mrT_ready = sem("mrT_ready"); mr_ready = sem("mr_ready")
        mrow = [[sem(f"mrow{p}{h}") for h in range(2)] for p in range(2)]
        sel_done = sem("sel_done")
        oproj_ready = sem("oproj_ready"); oproj_used = sem("oproj_used")
        var_ready = sem("var_ready"); std_ready = sem("std_ready")
        x1_ready = sem("x1_ready")
        zero_ready = sem("zero_ready"); zeroed = sem("zeroed")
        x1T_ready = sem("x1T_ready"); x1T_copied = sem("x1T_copied")
        x1_out = [sem(f"x1_out{b}") for b in range(NB)]; res_out = sem("res_out")
        logits_ready = sem("logits_ready"); score_ready = sem("score_ready")
        mb_ready = sem("mb_ready"); pre_ready = sem("pre_ready")
        onehot_ready = sem("onehot_ready"); tab_used = sem("tab_used"); tab_ready = sem("tab_ready")
        wprod_ready = sem("wprod_ready"); hi_made = sem("hi_made")
        idx_ready = sem("idx_ready")
        sh_h = sem("sh_h"); sh_silu = sem("sh_silu"); sh_g = sem("sh_g")
        sh_y = sem("sh_y"); sh_yused = sem("sh_yused")
        xs_in = [sem(f"xs_in{i}") for i in range(4)]
        xT_ready = sem("xT_ready"); xts_ready = sem("xts_ready")
        h_ready = sem("h_ready"); silu_ready = sem("silu_ready"); g_ready = sem("g_ready")
        gT_ready = sem("gT_ready"); gts_ready = sem("gts_ready")
        y_ready = sem("y_ready"); ys_ready = sem("ys_ready")
        acc_done = [sem(f"acc_done{i}") for i in range(2)]
        sum_ready = sem("sum_ready")
        acc_in = [sem(f"acc_in{i}") for i in range(PIECES)]
        shift_ready = sem("shift_ready"); out_ready = sem("out_ready"); out_done = sem("out_done")

        FIN = [W13[:, i * NT * D:(i + 1) * NT * D].rearrange("p (n d) -> p n d", n=NT) for i in range(2)]

        block = ctx.enter_context(nc.Block())

        x_tiles = x.rearrange("(n p q) d -> p n (q d)", p=P, q=2)
        out_tiles = out.rearrange("(n p q) d -> p n q d", p=P, q=2)

        def load_stacks(eng, b, half):
            p, g0, n = b % 2, half * 4, 4
            s0 = p * G + g0
            for a in range(PARTS):
                src = q_scr[b, a].rearrange("d h t -> d (h t)")[:, g0 * GH * T:(g0 + n) * GH * T]
                src = bass.AP(tensor=src.tensor, offset=src.offset, ap=[[0, PARTS]] + list(src.ap))
                dst = qs[a * 24:(a + 1) * 24, s0:s0 + n, :, :].rearrange("p s h t -> p (s h t)")
                eng.dma_start(dst, src).then_inc(stack[p][half], 16)
            src = k_scr[b].rearrange("c d g t -> (c d) (g t)")[:, g0 * T:(g0 + n) * T]
            src = bass.AP(tensor=src.tensor, offset=src.offset, ap=[[0, PARTS]] + list(src.ap))
            eng.dma_start(KS[0:ROWS, s0:s0 + n, :].rearrange("p s t -> p (s t)"), src).then_inc(
                stack[p][half], 16)

        def stacks_here(eng, b, half):
            eng.wait_ge(stack[b % 2][half], 64 * (b // 2 + 1))

        @block.sync
        def _(sp):
            sp.dma_start(WQ, wqkv.rearrange("(c p) n -> p c n", p=P)).then_inc(ld_wq, 16)
            xT_rows = xT.rearrange("(c p) t -> p c t", p=P)
            sp.dma_start(xT_sb[:, :, 0:T], xT_rows[:, :, 0:T]).then_inc(ld_x[0], 16)
            for i in range(2):
                sp.dma_start(COS[i], cos[i]).then_inc(ld_tab[i], 16)
                sp.dma_start(SIN[i], sin[i]).then_inc(ld_tab[i], 16)
            for b in range(1, NB):
                sp.dma_start(xT_sb[:, :, b * T:(b + 1) * T], xT_rows[:, :, b * T:(b + 1) * T]).then_inc(
                    ld_x[b], 16)
            sp.dma_start(WO[:, :, :], wo.rearrange("(c p) n -> p c n", p=P)).then_inc(ld_w, 16)
            sp.dma_start(GT[:, :, :], gateT.rearrange("(c p) n -> p c n", p=P)).then_inc(ld_w, 16)
            sp.wait_ge(zero_ready, 1)
            ctx0 = CTX[:, 0, :]
            zero = bass.AP(tensor=ctx0.tensor, offset=ctx0.offset, ap=[ctx0.ap[0], [0, NT + 1], ctx0.ap[1]])
            sp.dma_start(acc[1].rearrange("(t p) d -> p t d", p=P), zero).then_inc(zeroed, 16)
            for rows in (acc[0], x1_scr):
                sp.dma_start(rows[PAD:PAD + P, :], CTX[:, 0, :]).then_inc(zeroed, 16)
            def parts_out(v):
                sp.wait_ge(lo_ready, v + 1)
                for a in range(PARTS):
                    if PAIRS[v] == "k":
                        for h in range(2):
                            sp.dma_start(k_scr[:, a, h * HD // 2:(h + 1) * HD // 2, :, :].rearrange(
                                "b d g t -> b (d g) t"), parts[v % 4][:, a, h, :]).then_inc(scr_done[v], 16)
                    else:
                        sp.dma_start(q_scr[int(PAIRS[v][1]), a].rearrange("(a d) h t -> (d h) a t", a=2),
                                     parts[v % 4][:, a, :, :]).then_inc(scr_done[v], 16)

            parts_out(0)
            parts_out(1)
            sp.wait_ge(ones_ready, 1)
            for b in range(2):
                if b:
                    parts_out(2)
                for v in (0, 1) if b == 0 else (2,):
                    sp.wait_ge(scr_done[v], SCR[PAIRS[v][0]])
                load_stacks(sp, b, 0)
                load_stacks(sp, b, 1)
            for v in (3, 4):
                parts_out(v)
            for v in (3, 4):
                sp.wait_ge(scr_done[v], SCR["q"])
            sp.wait_ge(v_ready, NB)
            sp.dma_start(XT[:, :].rearrange("p (n d) -> p n d", n=NT // 2), x_tiles).then_inc(ld_res, 16)
            sp.dma_start(w13_sb, w13.rearrange("(c p) e n -> p c e n", p=P)).then_inc(ld_w13, 16)

            def maxima_out(b, half):
                sp.wait_ge(mr_ready, 2 * b + half + 1)
                s0 = (b % 2) * G + half * G // 2
                for a in range(PARTS):
                    sp.dma_start(qs[ROWS + a:ROWS + a + 1, s0:s0 + G // 2, :, :].rearrange(
                        "p s h t -> p (s h) t"), MR[a * H // 2:(a + 1) * H // 2, half, :]).then_inc(
                            mrow[b % 2][half], 16)

            def w2_in():
                sp.wait_ge(s2_ready, S2_TILES * 3 * G)
                sp.dma_start(w2_sb, w2).then_inc(ld_w2, 16)
                sp.dma_start(w2s_sb[:, 0:2, :], ws2[0:2 * P, :].rearrange("(c p) d -> p c d", p=P)).then_inc(
                    ld_w2, 16)
                sp.dma_start(w2s_sb[0:CW[2], 2, :], ws2[2 * P:2 * I, :]).then_inc(ld_w2, 16)

            def next_stacks(b, half):
                sp.wait_ge(s2_ready, S2_TILES * (8 * b + 4 * (half + 1)))
                load_stacks(sp, b + 2, half)

            maxima_out(0, 0)
            for b in range(NB):
                maxima_out(b, 1)
                if b < NB - 2:
                    next_stacks(b, 0)
                if b < NB - 1:
                    maxima_out(b + 1, 0)
                if b < NB - 2:
                    next_stacks(b, 1)
                if b == NB - 2:
                    w2_in()
            for b in range(NB - 1):
                sp.wait_ge(x1_ready, b + 1)
                sp.dma_start(x1_scr[b * T:(b + 1) * T, :].rearrange("(t p) d -> p t d", p=P),
                             X1[:, 4 * b:4 * b + 4, :]).then_inc(x1_out[b], 16)
            sp.wait_ge(x1_ready, NB)
            sp.dma_start(x1_scr[3 * T:4 * T, :].rearrange("(t p) d -> p t d", p=P),
                         X1[:, 12:16, :]).then_inc(x1_out[3], 16)
            sp.wait_ge(sh_yused, NT)
            sp.dma_start(acc[0][0:TOKENS, :].rearrange("(t p) d -> p t d", p=P), X1[:, :, :]).then_inc(
                res_out, 16)
            sp.wait_ge(acc_done[0], 16 * ((TILES + 1) // 2))
            sp.wait_ge(acc_done[1], 16 * (TILES // 2))
            sp.wait_ge(res_out, 16)
            for i in range(PIECES):
                for a in range(2):
                    sp.dma_start(FIN[a][:, 2 * i:2 * i + 2, :],
                                 acc[a][2 * i * P:(2 * i + 2) * P, :].rearrange("(t p) d -> p t d", p=P)).then_inc(
                                     acc_in[i], 16)
            for i in range(PIECES):
                sp.wait_ge(out_ready, 2 * i + 2)
                sp.dma_start(out_tiles[:, i, :, :], X1[:, 2 * i:2 * i + 2, :]).then_inc(out_done, 16)
            sp.wait_ge(out_done, 16 * PIECES)

        @block.gpsimd
        def _(pool):
            nc.gpsimd.memset(IDF[:, :], 0.0).then_inc(consts_ready, 1)
            nc.gpsimd.memset(IDB[:, :], 0.0).then_inc(consts_ready, 1)
            nc.gpsimd.memset(MQ[:, :, :], 0.0).then_inc(consts_ready, 1)
            nc.gpsimd.memset(EPSC[:, :], EPS).then_inc(consts_ready, 1)
            nc.gpsimd.memset(LOWER[:, :, :], 0.0).then_inc(consts_ready, 1)
            nc.gpsimd.iota(IOTA[:, :], pattern=[[1, P]], base=0, channel_multiplier=0,
                           allow_small_or_imprecise_dtypes=True).then_inc(consts_ready, 1)
            nc.gpsimd.iota(TID1[:, :, :], pattern=[[P, NT], [0, TOPK]], base=1, channel_multiplier=1,
                           allow_small_or_imprecise_dtypes=True).then_inc(consts_ready, 1)
            nc.gpsimd.iota(PADROW[:, :], pattern=[[0, 1]], base=PAD + 1, channel_multiplier=1,
                           allow_small_or_imprecise_dtypes=True).then_inc(consts_ready, 1)
            nc.gpsimd.memset(LOWER16[:, :, :], 0.0).then_inc(consts_ready, 1)
            nc.gpsimd.memset(UPPER[:, :], 0.0).then_inc(consts_ready, 1)
            nc.gpsimd.memset(ONES[:, :], 1.0).then_inc(consts_ready, 1)
            nc.gpsimd.memset(VC[:, :, HD + 1:32], 0.0).then_inc(vc_init, 1)
            nc.gpsimd.memset(VC[:, :, HD:HD + 1], 1.0).then_inc(vc_init, 1)
            pool.wait_ge(consts_ready, 11)
            for m in (IDF, IDB):
                nc.gpsimd.affine_select(out=m[:, :], in_=m[:, :], compare_op=ALU.not_equal, fill=1.0, base=0,
                                        pattern=[[-1, P]], channel_multiplier=1).then_inc(consts_ready, 1)
            nc.gpsimd.affine_select(out=MQ[:, :, :], in_=MQ[:, :, :], compare_op=ALU.is_ge, fill=NEG, base=0,
                                    pattern=[[0, GH], [-1, P]], channel_multiplier=1).then_inc(consts_ready, 1)
            nc.gpsimd.affine_select(out=LOWER[:, :, :], in_=LOWER[:, :, :], compare_op=ALU.is_ge, fill=1.0,
                                    base=0, pattern=[[-1, 4], [1, 4]], channel_multiplier=0).then_inc(
                                        consts_ready, 1)
            nc.gpsimd.affine_select(out=LOWER16[:, :, :], in_=LOWER16[:, :, :], compare_op=ALU.is_ge, fill=1.0,
                                    base=0, pattern=[[-1, E], [1, E]], channel_multiplier=0).then_inc(
                                        consts_ready, 1)
            nc.gpsimd.affine_select(out=UPPER[:, :], in_=UPPER[:, :], compare_op=ALU.is_ge, fill=1.0, base=0,
                                    pattern=[[-1, P]], channel_multiplier=1).then_inc(consts_ready, 1)
            pool.wait_ge(consts_ready, 17)
            nc.gpsimd.memset(KS[64:96, :, :], 1.0).then_inc(ones_ready, 1)
            pool.wait_ge(ones_ready, 1)
            for v in range(len(PAIRS)):
                pool.wait_ge(mid_ready, v + 1)
                nc.gpsimd.tensor_tensor(parts[v % 4][:, 2, :, :], REST[v % 2], parts[v % 4][:, 1, :, :],
                                        ALU.subtract).then_inc(lo_ready, 1)
            pool.wait_ge(vc_init, 2)
            for b in range(NB):
                pool.wait_ge(v_used, b + 1)
                with pool.Fori(0, G) as g:
                    for kt in range(QT):
                        pool.wait_ge(exp_done, (g + 8 * b) * S2_TILES + 2 + EXPS[kt])
                        nc.gpsimd.tensor_copy(VC[:, kt, 0:HD], VA[:, b * QT + kt, ds(g * HD, HD)]).then_inc(
                            vc_ready, 1)
                        nc.gpsimd.affine_select(out=PT[kt][:, :, 0:P], in_=PT[kt][:, :, 0:P],
                                                compare_op=ALU.is_ge, fill=0.0, base=0,
                                                pattern=[[0, GH], [1, P]], channel_multiplier=-1).then_inc(
                                                    sel_done, 1)
            for c in range(NT // CH):
                pool.wait_ge(hi_made, c + 1)
                nc.gpsimd.tensor_tensor(RH[c % 2][:, :, HI:2 * HI], OHHI[c % 2],
                                        WJ.rearrange("p t j -> p (t j)")[:, c * CH * TOPK:(c + 1) * CH * TOPK]
                                        .unsqueeze(2).broadcast_to([P, CH * TOPK, HI]),
                                        ALU.mult).then_inc(wprod_ready, 1)
            pool.wait_ge(idx_ready, 1)
            for b in range(NB):
                pool.wait_ge(x1_out[b], 16)
            AHEAD = 5
            for n in range(TILES + AHEAD):
                if n < TILES:
                    if n >= 4:
                        pool.wait_ge(xT_ready, n - 3)
                    nc.gpsimd.indirect_dma_start(XS[n % 4], None, x1_scr,
                                                 bass.IndirectOffsetOnAxis(IDX[:, n:n + 1], 0)).then_inc(
                                                     xs_in[n % 4], 16)
                m = n - AHEAD
                if m == 0:
                    pool.wait_ge(res_out, 16)
                    pool.wait_ge(zeroed, 48)
                if m >= 0:
                    if m >= 2:
                        pool.wait_ge(acc_done[m % 2], 16 * (m // 2))
                    pool.wait_ge(ys_ready, m + 3)
                    nc.gpsimd.indirect_dma_start(acc[m % 2], bass.IndirectOffsetOnAxis(IDX[:, m:m + 1], 0),
                                                 YS[m % 4], None, compute_op=ALU.add).then_inc(
                                                     acc_done[m % 2], 16)
            for i in range(PIECES):
                pool.wait_ge(acc_in[i], 32)
                ts = slice(2 * i, 2 * i + 2)
                nc.gpsimd.tensor_tensor(X1[:, ts, :], FIN[0][:, ts, :], FIN[1][:, ts, :], ALU.add).then_inc(
                    sum_ready, 1)

        @block.scalar
        def _(act):
            act.sem_inc(exp_done, 2)
            def second(v):
                act.wait_ge(rest1_ready, v + 1)
                nc.scalar.activation(parts[v % 4][:, 1, :, :], REST[v % 2], ACT.Copy).then_inc(mid_ready, 1)

            for v, pair in enumerate(PAIRS):
                act.wait_ge(rot_ready, v + 1)
                if v >= 4:
                    act.wait_ge(scr_done[v - 4], SCR[PAIRS[v - 4][0]])
                nc.scalar.activation(parts[v % 4][:, 0, :, :], ROT[v % 2], ACT.Copy).then_inc(hi_ready, 1)
                if pair != "k":
                    b = int(pair[1])
                    act.wait_ge(v_ready, b + 1)
                    nc.scalar.activation(VA[:, b * QT:(b + 1) * QT, :],
                                         VP[b][:, 0:QT * G * HD].rearrange("p (q n) -> p q n", q=QT),
                                         ACT.Copy).then_inc(v_used, 1)
                second(v)

            def maxima_rows(b, half):
                act.wait_ge(mrT_ready, 2 * b + half + 1)
                if b >= 1:
                    act.wait_ge(mrow[(b - 1) % 2][half], 48 * ((b - 1) // 2 + 1))
                nc.scalar.activation(MR[:, half, :], MRP[0:PARTS * H // 2, :], ACT.Copy).then_inc(mr_ready, 1)

            def copy_x1T(b, banks):
                act.wait_ge(x1T_ready, b + 1)
                for i in range(2):
                    t = (4 * b + 2 * i) * P
                    nc.scalar.activation(x1T[:, :, t:t + 2 * P].rearrange("p c (t n) -> p t c n", n=P),
                                         banks[i][:, :].rearrange("p (t c n) -> p t c n", t=2, c=KC),
                                         ACT.Copy).then_inc(x1T_copied, 1)

            def exps(s, k):
                kt, h0, nh = S2[k]
                act.wait_ge(s2_ready, s * S2_TILES + k + 1)
                act.wait_ge(pv_done, s * 4 + kt + 1)
                w = T - P * kt
                tile = S2P[k % 2][:, :, :]
                if nh == 2:
                    src = tile[:, :, 0:w]
                    dst = PT[kt][:, h0:h0 + 2, :]
                else:
                    src = tile.rearrange("p a t -> p (a t)")[:, 0:GH * w]
                    dst = PT[kt].rearrange("p h t -> p (h t)")
                nc.scalar.activation(dst, src, ACT.Exp, scale=SCALE).then_inc(exp_done, 1)

            def group(s, last=False, rows=None):
                for k in range(2, S2_TILES):
                    exps(s, k)
                    if rows and k == 3:
                        maxima_rows(*rows)
                if not last:
                    exps(s + 1, 0)
                act.wait_ge(pv_done, s * 4 + 8)
                act.wait_ge(ctxT_ready, s + 1)
                nc.scalar.activation(PVS[:, :], PVP[:, :], ACT.Copy).then_inc(pvs_ready, 1)
                if not last:
                    exps(s + 1, 1)

            def groups(s0, n):
                with act.Fori(0, n // 2) as i:
                    for j in range(2):
                        group(2 * i + (s0 + j))
                if n % 2:
                    group(s0 + n - 1)

            maxima_rows(0, 0)
            nc.scalar.preload_act_table(ACT.Exp)
            exps(0, 0)
            exps(0, 1)
            for b in range(NB):
                s0 = 8 * b
                group(s0)
                group(s0 + 1, rows=(b, 1))
                groups(s0 + 2, 2)
                if b == NB - 1:
                    act.wait_ge(var_ready, NB - 1)
                    nc.scalar.activation(SD[:, 0:4 * NB - 4], MV[:, 0:4 * NB - 4, 1], ACT.Sqrt,
                                         bias=EPSC[:, 0:1]).then_inc(std_ready, 1)
                    nc.scalar.preload_act_table(ACT.Exp)
                groups(s0 + 4, 2)
                group(s0 + 6, rows=(b + 1, 0) if b < NB - 1 else None)
                group(s0 + 7, last=(b == NB - 1))
            act.wait_ge(var_ready, NB)
            nc.scalar.activation(SD[:, 4 * NB - 4:4 * NB], MV[:, 4 * NB - 4:4 * NB, 1], ACT.Sqrt,
                                 bias=EPSC[:, 0:1]).then_inc(std_ready, 1)

            def unit(u):
                w = CW[u % 3]
                act.wait_ge(sh_h, u + 1)
                if u >= 2:
                    act.wait_ge(sh_g, u - 1)
                nc.scalar.activation(SILS[u % 2][0:w, :], HP[u % 2][0:w, 0:SB], ACT.Silu).then_inc(sh_silu, 1)

            unit(0)
            copy_x1T(NB - 1, (PVP, TGP[0]))
            unit(1)
            act.wait_ge(logits_ready, 1)
            nc.scalar.activation(SC, MIS[:, 0:NT * E].rearrange("p (t e) -> p t e", t=NT),
                                 ACT.Sigmoid).then_inc(score_ready, 1)
            for u in range(2, UNITS):
                unit(u)

            def silu(n, p):
                act.wait_ge(h_ready, n + 3)
                act.wait_ge(g_ready, n + 1)
                nc.scalar.activation(SILU[p], HP[p][:, 0:I], ACT.Silu).then_inc(silu_ready, 1)

            def copy_gT(n, p):
                act.wait_ge(gT_ready, n + 3)
                act.wait_ge(y_ready, n + 1)
                nc.scalar.activation(GTS[p], TGP[p][0:IH, 0:2 * P].rearrange("p (c t) -> p c t", c=2),
                                     ACT.Copy).then_inc(gts_ready, 1)

            def normalise(i):
                act.wait_ge(shift_ready, i + 1)
                for t in range(2 * i, 2 * i + 2):
                    nc.scalar.activation(X1[:, t, :], X1[:, t, :], ACT.Identity, bias=SHIFT[:, t:t + 1],
                                         scale=RSTD[:, t:t + 1]).then_inc(out_ready, 1)

            act.wait_ge(sh_y, NT)
            act.sem_inc(gts_ready, 2)
            silu(0, 0)
            with act.Fori(0, TILES // 2) as i:
                for p in range(2):
                    silu(2 * i + (p + 1), (p + 1) % 2)
                    copy_gT(2 * i + p, p)
            copy_gT(TILES - 1, (TILES - 1) % 2)
            for i in range(PIECES):
                ts = slice(2 * i, 2 * i + 2)
                act.wait_ge(var_ready, NB + i + 1)
                nc.scalar.activation(SD[:, ts], MV[:, ts, 1], ACT.Sqrt, bias=EPSC[:, 0:1]).then_inc(std_ready, 1)
                if i >= 1:
                    normalise(i - 1)
            normalise(PIECES - 1)

        @block.tensor
        def _(pe):
            pe.sem_inc(pv_done, 4)
            pe.sem_inc(ctxT_ready, 1)
            pe.wait_ge(ld_wq, 16)
            for v, pair in enumerate(PAIRS):
                if v >= 2:
                    pe.wait_ge(proj_used, v - 1)
                if pair == "k":
                    for b in range(1, NB):
                        pe.wait_ge(ld_x[b], 16)
                    for h in range(2):
                        for b in range(NB):
                            for c in range(KC):
                                last = nc.tensor.matmul(S2P[v % 2][32 * b:32 * b + 32, h, :],
                                                        WQ[:, c, 2 * P + 32 * h:2 * P + 32 * h + 32],
                                                        xT_sb[:, c, b * T:(b + 1) * T],
                                                        start=(c == 0), stop=(c == KC - 1))
                    last.then_inc(proj_ready, 1)
                    continue
                b = int(pair[1])
                pe.wait_ge(ld_x[b], 16)
                for h in range(2):
                    for c in range(KC):
                        last = nc.tensor.matmul(S2P[v % 2][:, h, :], WQ[:, c, h * P:(h + 1) * P],
                                                xT_sb[:, c, b * T:(b + 1) * T],
                                                start=(c == 0), stop=(c == KC - 1))
                last.then_inc(proj_ready, 1)
                for q in range(QT):
                    for c in range(KC):
                        last = nc.tensor.matmul(VP[b][:, q * 64:(q + 1) * 64],
                                                xT_sb[:, c, b * T + q * P:b * T + (q + 1) * P],
                                                WQ[:, c, V0:WC], start=(c == 0), stop=(c == KC - 1))
                last.then_inc(v_ready, 1)
            pe.wait_ge(proj_used, len(PAIRS))
            pe.wait_ge(v_used, NB)
            pe.wait_ge(consts_ready, 17)
            pe.wait_ge(ones_ready, 1)
            pe.wait_ge(ld_w, 32)

            def s1_tile(s, slot, k, banks=S1P):
                q, h0, nh = S1[k]
                w = P * (q + 1)
                pe.wait_ge(s1_free, s * S1_TILES + (k + 7 - len(banks)))
                dst = banks[k % len(banks)][:, 0:nh * w].rearrange("p (h k) -> p h k", h=nh)
                for h in range(nh):
                    nc.tensor.matmul(dst[:, h, :], qs[0:ROWS, ds(slot, 1), h0 + h, q * P:(q + 1) * P],
                                     KS[0:ROWS, ds(slot, 1), 0:w], start=(h == 0), stop=True,
                                     skip_group_check=True)
                nc.tensor.matmul(dst[:, :, w - P:w], IDB[:, :], MQ[:, 0:nh, :], start=False, stop=True,
                                 skip_group_check=True).then_inc(s1_ready, 1)

            def s2_tile(s, slot, k):
                kt, h0, nh = S2[k]
                w = T - P * kt
                pe.wait_ge(exp_done, s * S2_TILES + k + 1)
                per = T // w if kt >= 2 else 1
                for a in range(max(1, nh // per)):
                    hs = slice(h0 + a * per, h0 + (a + 1) * per)
                    dst = S2P[k % 2][:, a, 0:per * w].rearrange("p (h q) -> p h q", h=per)
                    last = nc.tensor.matmul(dst, KS[0:KROWS, ds(slot, 1), kt * P:(kt + 1) * P],
                                            qs[0:KROWS, ds(slot, 1), hs, kt * P:T], start=True, stop=True)
                last.then_inc(s2_ready, 1)

            def pv(s, kt):
                pe.wait_ge(sel_done, s * 4 + kt + 1)
                pe.wait_ge(vc_ready, s * 4 + kt + 1)
                for j in range(GH):
                    last = nc.tensor.matmul(PVP[32 * j:32 * j + 32, kt * P:T], VC[:, kt, :], PT[kt][:, j, :],
                                            start=(kt == 0), stop=(kt == QT - 1))
                last.then_inc(pv_done, 1)

            def group(b, g, with_next=True, maxima_of=None, output_of=None):
                s = g + 8 * b
                slot = g + 8 * (b % 2)
                nxt = g + 8 * ((b + 1) % 2)

                def fill(*ks):
                    if b < NB - 1:
                        for k in ks:
                            s1_tile(s + 8, nxt, k)

                def ahead(k):
                    if with_next:
                        s2_tile(s + 1, slot + 1 if not (isinstance(g, int) and g == G - 1)
                                else 8 * ((b + 1) % 2), k)

                def output(piece):
                    if output_of is not None:
                        oproj(output_of, piece, MIS)

                if b == NB - 1:
                    s2_tile(s, slot, 3)
                    s2_tile(s, slot, 4)
                    pv(s, 0)
                    if maxima_of:
                        maxima(*maxima_of, s)
                    output(0)
                    output(1)
                    s2_tile(s, slot, 5)
                    ahead(0)
                    pv(s, 1)
                    pv(s, 2)
                    pv(s, 3)
                    ahead(1)
                    output(2)
                    output(3)
                    ahead(2)
                else:
                    fill(0)
                    s2_tile(s, slot, 3)
                    fill(1)
                    pv(s, 0)
                    if maxima_of:
                        maxima(*maxima_of, s)
                    output(0)
                    fill(2)
                    output(1)
                    s2_tile(s, slot, 4)
                    fill(3)
                    pv(s, 1)
                    fill(4)
                    s2_tile(s, slot, 5)
                    fill(5)
                    ahead(0)
                    fill(6)
                    output(2)
                    pv(s, 2)
                    fill(7)
                    output(3)
                    ahead(1)
                    fill(8)
                    pv(s, 3)
                    fill(9)
                    ahead(2)
                    fill(10)
                pe.wait_ge(pvs_ready, s + 1)
                pe.wait_ge(norm_done, s + 1)
                if maxima_of:
                    pe.wait_ge(mr_ready, 2 * maxima_of[0] + maxima_of[1] + 1)
                if output_of is not None:
                    pe.wait_ge(oproj_used, 2 * output_of + 2)
                for q in range(QT):
                    last = nc.tensor.matmul(MIS[:, q * P:(q + 1) * P], PVS[:, q * P:(q + 1) * P], IDF[:, :],
                                            is_transpose=True, start=True, stop=True)
                last.then_inc(ctxT_ready, 1)
                fill(11)

            def maxima(b, half, s=None):
                pe.wait_ge(ns_ready, 2 * b + half + 1)
                if s is not None:
                    pe.wait_ge(norm_done, s + 1)
                for q in range(QT):
                    last = nc.tensor.transpose(
                        MRP[0:PARTS * H // 2, q * P:(q + 1) * P],
                        NS[:, half, q, :, :].rearrange("p a h -> p (a h)"), IDB[:, :])
                last.then_inc(mrT_ready, 1)

            def oproj(b, piece, bank):
                hd, q = divmod(piece, 2)
                if piece == 0:
                    pe.wait_ge(norm_done, 8 * b + 9)
                if q == 0 and bank is MIS and hd:
                    pe.wait_ge(oproj_used, 2 * b + hd)
                for c in range(KC):
                    last = nc.tensor.matmul(bank[:, q * D:(q + 1) * D],
                                            CTX[:, 2 * q + c, hd * P:(hd + 1) * P], WO[:, c, :],
                                            start=(c == 0), stop=(c == KC - 1))
                if q == 1:
                    last.then_inc(oproj_ready, 1)

            def rows_here(b, half):
                pe.wait_ge(mrow[b % 2][half], 48 * (b // 2 + 1))

            def transpose_x1(b, banks):
                for i in range(2):
                    for t in range(2):
                        for c in range(KC):
                            last = nc.tensor.matmul(banks[i][:, (2 * t + c) * P:(2 * t + c + 1) * P],
                                                    X1[:, 4 * b + 2 * i + t, c * P:(c + 1) * P], IDF[:, :],
                                                    is_transpose=True, start=True, stop=True)
                last.then_inc(x1T_ready, 1)

            for g0, n in ((0, 4), (4, 2), (6, 2)):
                if g0 != 6:
                    stacks_here(pe, 0, g0 // 4)
                else:
                    maxima(0, 0)
                with pe.Fori(g0, g0 + n) as g:
                    for k in range(S1_TILES):
                        s1_tile(g, g, k, S1P6)
            rows_here(0, 0)
            pe.wait_ge(s1_free, S1_TILES * G + 6)
            s2_tile(0, 0, 0)
            s2_tile(0, 0, 1)
            s2_tile(0, 0, 2)
            for b in range(NB):
                more = b < NB - 1
                if more:
                    stacks_here(pe, b + 1, 0)
                group(b, 0, output_of=b - 1 if b else None)
                group(b, 1, maxima_of=(b, 1))
                rows_here(b, 1)
                if more:
                    stacks_here(pe, b + 1, 1)
                with pe.Fori(2, 6) as g:
                    group(b, g)
                if more:
                    group(b, 6, maxima_of=(b + 1, 0))
                    rows_here(b + 1, 0)
                    group(b, 7)
                else:
                    pe.wait_ge(x1_ready, 1)
                    transpose_x1(0, S1P)
                    group(b, 6)
                    pe.wait_ge(x1T_copied, 2)
                    pe.wait_ge(x1_ready, NB - 1)
                    transpose_x1(1, S1P)
                    group(b, 7, with_next=False)
                    pe.wait_ge(x1T_copied, 4)
                    transpose_x1(2, S1P)
            pe.wait_ge(x1T_copied, 6)
            for piece in range(4):
                oproj(NB - 1, piece, S1P[piece // 2])
            pe.wait_ge(oproj_used, 2 * NB)

            pe.wait_ge(ld_w13, 16)
            pe.wait_ge(ld_w2, 48)

            def unit_h(u):
                blk, i = divmod(u, 3)
                w = CW[i]
                if u >= 2:
                    pe.wait_ge(sh_g, u - 1)
                for j in range(2):
                    for c in range(KC):
                        last = nc.tensor.matmul(HP[u % 2][0:w, j * SB:(j + 1) * SB],
                                                w13_sb[:, c, E + j, i * P:i * P + w],
                                                x1T[:, c, blk * SB:(blk + 1) * SB],
                                                start=(c == 0), stop=(c == KC - 1))
                last.then_inc(sh_h, 1)

            def transpose_g(dst, g, done):
                for c in range(2):
                    last = nc.tensor.matmul(dst[0:IH, c * P:(c + 1) * P], g[:, c * IH:(c + 1) * IH],
                                            IDF[:, :], is_transpose=True, start=True, stop=True)
                last.then_inc(done, 1)

            def unit_y(t):
                blk = t // 2
                pe.wait_ge(sh_g, 3 * blk + 3)
                if t >= 2:
                    pe.wait_ge(sh_yused, t - 1)
                for i, w in enumerate(CW):
                    last = nc.tensor.matmul(YP[t % 2][:, 0:D], SG[blk % 2][0:w, i, (t % 2) * P:(t % 2 + 1) * P],
                                            w2s_sb[0:w, i, :], start=(i == 0), stop=(i == 2))
                last.then_inc(sh_y, 1)

            def units(u0, u1):
                for u in range(u0, u1):
                    if u + 1 < UNITS:
                        unit_h(u + 1)
                    blk, i = divmod(u, 3)
                    if blk >= 1 and i < 2:
                        unit_y(2 * (blk - 1) + i)

            def logits(t0, t1):
                for t in range(t0, t1):
                    for c in range(KC):
                        last = nc.tensor.matmul(MIS[:, t * E:(t + 1) * E], x1T[:, c, t * P:(t + 1) * P],
                                                GT[:, c, :], start=(c == 0), stop=(c == KC - 1))
                return last

            unit_h(0)
            logits(0, NT - QT)
            pe.wait_ge(x1_ready, NB)
            transpose_x1(NB - 1, (PVP, TGP[0]))
            units(0, 1)
            pe.wait_ge(x1T_copied, 2 * NB)
            logits(NT - QT, NT).then_inc(logits_ready, 1)
            units(1, 7)
            pe.wait_ge(mb_ready, 1)
            nc.tensor.matmul(MIS[:, 0:NT * E], UPPER[:, :], MB[:, :, :], start=True, stop=True)
            for t in range(NT - 1):
                later = MB[:, t, :].unsqueeze(1).broadcast_to([P, NT - 1 - t, E])
                nc.tensor.matmul(MIS[:, (t + 1) * E:NT * E].rearrange("p (t e) -> p t e", e=E), ONES[:, :],
                                 later, start=False, stop=True, skip_group_check=True)
            for t in range(NT):
                last = nc.tensor.matmul(PVP[:, 0:E], ONES[:, :], MB[:, t, :], start=(t == 0), stop=(t == NT - 1))
            last.then_inc(pre_ready, 1)
            units(7, 12)

            def place_tables(c):
                pe.wait_ge(onehot_ready, c + 1)
                pe.wait_ge(wprod_ready, c + 1)
                for k in range(CH * TOPK):
                    last = nc.tensor.matmul(PVP[:, 0:2 * HI], OHLO[c % 2][:, k, :], RH[c % 2][:, k, :],
                                            start=(c == 0 and k == 0),
                                            stop=(c == NT // CH - 1 and k == CH * TOPK - 1))
                last.then_inc(tab_ready, 1)

            for c in range(NT // CH):
                place_tables(c)
                units(12 + c, 13 + c)
            units(16, UNITS)
            unit_y(NT - 2)
            unit_y(NT - 1)

            def expert(n):
                return pe.value_load(EOT[0:1, n], min_val=0, max_val=E - 1)

            def tile_x(n, p, k):
                pe.wait_ge(xts_ready, n + 1)
                for c in range(KC):
                    last = nc.tensor.matmul(TXP[p][:, c * P:(c + 1) * P], XS[k][:, c * P:(c + 1) * P], IDF[:, :],
                                            is_transpose=True, start=True, stop=True)
                last.then_inc(xT_ready, 1)

            def tile_h(n, p, e):
                pe.wait_ge(xts_ready, n + 3)
                pe.wait_ge(g_ready, n + 1)
                for c in range(KC):
                    last = nc.tensor.matmul(HP[p][:, 0:2 * I], XTS[p][:, c, :], w13_sb[:, c, ds(e, 1), :],
                                            start=(c == 0), stop=(c == KC - 1))
                last.then_inc(h_ready, 1)

            def tile_g(n, p):
                pe.wait_ge(g_ready, n + 3)
                pe.wait_ge(gts_ready, n + 1)
                transpose_g(TGP[p], GG[p], gT_ready)

            def tile_y(n, p, e):
                pe.wait_ge(gts_ready, n + 3)
                pe.wait_ge(ys_ready, n + 1)
                for c in range(2):
                    last = nc.tensor.matmul(YP[p][:, 0:D], GTS[p][:, c, :], w2_sb[:, ds(e, 1), c, :],
                                            start=(c == 0), stop=(c == 1))
                last.then_inc(y_ready, 1)

            def one(n):
                return slice(n, n + 1)

            pe.wait_ge(idx_ready, 1)
            pe.sem_inc(y_ready, 2)
            pe.sem_inc(h_ready, 2)
            pe.sem_inc(gT_ready, 2)
            for n in range(2):
                pe.wait_ge(xs_in[n], 16)
                tile_x(n, n, n)
            tile_h(0, 0, expert(one(0)))
            tile_h(1, 1, expert(one(1)))
            pe.wait_ge(xs_in[2], 16)
            tile_x(2, 0, 2)
            tile_g(0, 0)
            LOOPED = (TILES - 3) // 4 * 4
            with pe.Fori(0, LOOPED // 4) as i:
                for k in range(4):
                    n = 4 * i + (k + 1)
                    p = (k + 1) % 2
                    tile_h(n + 1, 1 - p, expert(ds(n + 1, 1)))
                    pe.wait_ge(xs_in[(k + 3) % 4], 16 * i + 16 * ((k + 3) // 4 + 1))
                    tile_x(n + 2, p, (k + 3) % 4)
                    tile_g(n, p)
                    tile_y(n - 1, 1 - p, expert(ds(n - 1, 1)))
            for n in range(LOOPED + 1, TILES):
                p = n % 2
                if n + 1 < TILES:
                    tile_h(n + 1, 1 - p, expert(one(n + 1)))
                if n + 2 < TILES:
                    pe.wait_ge(xs_in[(n + 2) % 4], 16 * ((n + 2) // 4 + 1))
                    tile_x(n + 2, p, (n + 2) % 4)
                tile_g(n, p)
                tile_y(n - 1, 1 - p, expert(one(n - 1)))
            tile_y(TILES - 1, (TILES - 1) % 2, expert(one(TILES - 1)))

        @block.vector
        def _(dve):
            steps = [0]

            def link(ins, wait=True):
                steps[0] += 1
                ins.then_inc(dve_step, 1)
                if wait:
                    dve.wait_ge(dve_step, steps[0])

            dve.sem_inc(s1_free, 6)
            dve.sem_inc(norm_done, 1)
            nc.vector.memset(CTX[:, 0, :], 0.0).then_inc(zero_ready, 1)

            def rest(v):
                dve.wait_ge(hi_ready, v + 1)
                if v >= 2:
                    dve.wait_ge(lo_ready, v - 1)
                nc.vector.tensor_tensor(REST[v % 2], ROT[v % 2], parts[v % 4][:, 0, :, :],
                                        ALU.subtract).then_inc(rest1_ready, 1)

            both = [P, 2, T]
            for v in range(len(PAIRS)):
                tab = int(PAIRS[v] == "k")
                dve.wait_ge(ld_tab[tab], 32)
                dve.wait_ge(proj_ready, v + 1)
                link(nc.vector.tensor_tensor(COSP, S2P[v % 2][:, :, :], COS[tab].unsqueeze(1).broadcast_to(both),
                                             ALU.mult), False)
                if v >= 1:
                    rest(v - 1)
                link(nc.vector.tensor_tensor(SINP, S2P[v % 2][:, :, :], SIN[tab].unsqueeze(1).broadcast_to(both),
                                             ALU.mult))
                dve.sem_inc(proj_used, 1)
                link(nc.vector.tensor_tensor(ROT[v % 2][:, 0, :], COSP[:, 0, :], SINP[:, 1, :], ALU.subtract),
                     False)
                link(nc.vector.tensor_tensor(ROT[v % 2][:, 1, :], COSP[:, 1, :], SINP[:, 0, :], ALU.add))
                dve.sem_inc(rot_ready, 1)
            rest(len(PAIRS) - 1)

            def s1_max(s, g, k, banks=S1P):
                q, h0, nh = S1[k]
                w = P * (q + 1)
                dve.wait_ge(s1_ready, s * S1_TILES + k + 1)
                nc.vector.tensor_reduce(NM[:, q, ds(g * GH + h0, nh)],
                                        banks[k % len(banks)][:, 0:nh * w].rearrange("p (h k) -> p h k", h=nh),
                                        AXX, ALU.max, negate=True).then_inc(s1_free, 1)

            def split_maxima(b, half, step=None):
                if not step:
                    dve.wait_ge(s1_free, S1_TILES * (8 * b + 4 * half + 4) + 6)
                    if b >= 1:
                        dve.wait_ge(mrT_ready, 2 * (b - 1) + half + 1)
                nm = NM[:, :, half * H // 2:(half + 1) * H // 2]
                ns = NS[:, half, :, :, :]
                for k in range(5) if step is None else (step,):
                    if k == 0:
                        link(nc.vector.tensor_copy(ns[:, :, 0, :], nm))
                    elif k == 1:
                        link(nc.vector.tensor_tensor(NR[:, 0, :, :], nm, ns[:, :, 0, :], ALU.subtract))
                    elif k == 2:
                        link(nc.vector.tensor_copy(ns[:, :, 1, :], NR[:, 0, :, :]))
                    elif k == 3:
                        link(nc.vector.tensor_tensor(NR[:, 1, :, :], NR[:, 0, :, :], ns[:, :, 1, :],
                                                     ALU.subtract))
                    else:
                        nc.vector.tensor_copy(ns[:, :, 2, :], NR[:, 1, :, :]).then_inc(ns_ready, 1)

            for half in range(2):
                with dve.Fori(4 * half, 4 * half + 4) as g:
                    for k in range(S1_TILES):
                        s1_max(g, g, k, S1P6)
                if half == 0:
                    split_maxima(0, 0)
            dve.wait_ge(ld_res, 16)
            dve.wait_ge(zeroed, 48)
            ctx_v = CTX[:, :, :].rearrange("p q (g j d) -> p q g j d", g=G, j=GH)

            def group(b, g, step, split=None, output_of=None):
                s = g + 8 * b
                for k in range(S1_TILES):
                    if b < NB - 1:
                        s1_max(s + 8, g, k)
                    if split and k < 5:
                        split_maxima(*split, k)
                    if output_of is not None and k in (5, 9):
                        residual(output_of, int(k == 9), MIS)
                dve.wait_ge(ctxT_ready, s + 2)
                nc.vector.reciprocal(RC[:, :, :], CTXP[:, :, :, HD]).then_inc(dve_step, 1)
                dve.wait_ge(dve_step, step)
                nc.vector.tensor_tensor(ctx_v[:, :, ds(g, 1), :, :].rearrange("p q g j d -> p q (g j) d"),
                                        CTXP[:, :, :, 0:HD],
                                        RC[:, :, :].unsqueeze(3).broadcast_to([P, QT, GH, HD]),
                                        ALU.mult).then_inc(norm_done, 1)

            def groups(b, g0, n):
                with dve.Fori(0, n // 2) as i:
                    for j in range(2):
                        group(b, 2 * i + (g0 + j), 2 * i + (steps[0] + j + 1))
                steps[0] += n

            def one_group(b, g, split=None, output_of=None):
                n = 4 if split else 0
                group(b, g, steps[0] + n + 1, split, output_of)
                steps[0] += 1

            def residual(b, hd, bank):
                dve.wait_ge(oproj_ready, 2 * b + hd + 1)
                t = 4 * b + 2 * hd
                nc.vector.tensor_tensor(X1[:, t:t + 2, :], bank[:, :].rearrange("p (q d) -> p q d", q=2),
                                        X1[:, t:t + 2, :], ALU.add).then_inc(oproj_used, 1)

            def statistics(b):
                dve.wait_ge(oproj_used, 2 * b + 2)
                for k in range(4):
                    link(nc.vector.bn_stats(ST[:, k, :], X1[:, 4 * b + k, :]), False)
                dve.wait_ge(dve_step, steps[0])
                for k in range(4):
                    link(nc.vector.bn_aggr(MV[:, 4 * b + k, :], ST[:, k, :]), False)
                dve.wait_ge(dve_step, steps[0])
                dve.sem_inc(var_ready, 1)

            def normalise(b):
                for t in range(4 * b, 4 * b + 4):
                    link(nc.vector.tensor_scalar(X1[:, t, :], X1[:, t, :], MV[:, t, 0:1], RSTD[:, t:t + 1],
                                                 ALU.subtract, ALU.mult), False)
                dve.wait_ge(dve_step, steps[0])
                dve.sem_inc(x1_ready, 1)

            def copy_x1T(b):
                dve.wait_ge(x1T_ready, b + 1)
                for i in range(2):
                    t = (4 * b + 2 * i) * P
                    nc.vector.tensor_copy(x1T[:, :, t:t + 2 * P].rearrange("p c (t n) -> p t c n", n=P),
                                          S1P[i][:, :].rearrange("p (t c n) -> p t c n", t=2, c=KC)).then_inc(
                                              x1T_copied, 1)

            for b in range(NB):
                one_group(b, 0, split=(b, 1), output_of=b - 1 if b else None)
                if b < NB - 1:
                    groups(b, 1, 4)
                    one_group(b, 5, split=(b + 1, 0))
                    groups(b, 6, 2)
            b = NB - 1
            for i in range(b):
                statistics(i)
                one_group(b, i + 1)
            dve.wait_ge(std_ready, 1)
            link(nc.vector.reciprocal(RSTD[:, 0:4 * b], SD[:, 0:4 * b]))
            normalise(0)
            one_group(b, 4)
            normalise(1)
            one_group(b, 5)
            normalise(2)
            copy_x1T(0)
            one_group(b, 6)
            copy_x1T(1)
            one_group(b, 7)
            copy_x1T(2)
            for hd in range(2):
                residual(b, hd, S1P[hd])
            statistics(b)
            dve.wait_ge(std_ready, 2)
            link(nc.vector.reciprocal(RSTD[:, 4 * b:4 * b + 4], SD[:, 4 * b:4 * b + 4]))
            normalise(b)

            def units(u0, u1):
                for u in range(u0, u1):
                    blk, i = divmod(u, 3)
                    w = CW[i]
                    dve.wait_ge(sh_silu, u + 1)
                    if blk >= 2:
                        dve.wait_ge(sh_y, 2 * blk - 2)
                    nc.vector.tensor_tensor(SG[blk % 2][0:w, i, :], SILS[u % 2][0:w, :],
                                            HP[u % 2][0:w, SB:2 * SB], ALU.mult).then_inc(sh_g, 1)
                    if blk >= 1 and i >= 1:
                        unit_out(2 * (blk - 1) + i - 1)

            def unit_out(t):
                dve.wait_ge(sh_y, t + 1)
                dve.wait_ge(x1_out[t // 4], 16)
                nc.vector.tensor_tensor(X1[:, t, :], YP[t % 2][:, 0:D], X1[:, t, :], ALU.add).then_inc(
                    sh_yused, 1)

            dve.wait_ge(pv_done, 4 * NB * G + 4)
            units(0, 2)
            dve.wait_ge(score_ready, 1)
            dve.wait_ge(consts_ready, 17)
            sg = SC.rearrange("p t (g k) -> p t g k", g=4)
            link(nc.vector.tensor_reduce(GS, sg, AXX, ALU.max))
            other = GS.unsqueeze(2).broadcast_to([P, NT, 4, 4])
            own = GS.unsqueeze(3).broadcast_to([P, NT, 4, 4])
            low = LOWER[:, :, :].unsqueeze(1).broadcast_to([P, NT, 4, 4])
            link(nc.vector.tensor_tensor(GA, other, own, ALU.is_gt), False)
            link(nc.vector.tensor_tensor(GB, other, own, ALU.is_equal))
            link(nc.vector.tensor_tensor(GB, GB, low, ALU.mult))
            link(nc.vector.tensor_tensor(GA, GA, GB, ALU.add))
            link(nc.vector.tensor_reduce(GR, GA, AXX, ALU.add))
            link(nc.vector.tensor_scalar(GR, GR, 2.0, None, ALU.is_lt))
            link(nc.vector.tensor_tensor(MSK.rearrange("p t (g k) -> p t g k", g=4), sg,
                                         GR.unsqueeze(3).broadcast_to([P, NT, 4, 4]), ALU.mult))
            units(2, 3)
            for t in range(NT):
                link(nc.vector.max(TOP[:, t, :], MSK[:, t, :]), False)
            dve.wait_ge(dve_step, steps[0])
            for t in range(NT):
                link(nc.vector.max_index(TOPI[:, t, :], TOP[:, t, :], MSK[:, t, :]), False)
            dve.wait_ge(dve_step, steps[0])
            units(3, 5)
            link(nc.vector.tensor_copy(TOPF, TOPI))
            by_t = [P, NT, TOPK, E]
            link(nc.vector.tensor_tensor(OHJ, TOPF[:, :, 0:TOPK].unsqueeze(3).broadcast_to(by_t),
                                         IOTA[:, 0:E].unsqueeze(1).unsqueeze(1).broadcast_to(by_t),
                                         ALU.is_equal))
            with nc.allow_low_precision("zeros and ones"):
                nc.vector.tensor_reduce(MB[:, :, :], OHJ.rearrange("p t j e -> p t e j"), AXX,
                                        ALU.add).then_inc(mb_ready, 1)
            link(nc.vector.tensor_tensor(TMJ, OHJ, SC.unsqueeze(2).broadcast_to(by_t), ALU.mult))
            link(nc.vector.tensor_reduce(WJ, TMJ, AXX, ALU.add))
            units(5, 6)
            link(nc.vector.tensor_reduce(WSUM, WJ, AXX, ALU.add))
            link(nc.vector.reciprocal(WREC, WSUM))
            link(nc.vector.tensor_tensor(WJ, WJ, WREC.unsqueeze(2).broadcast_to([P, NT, TOPK]), ALU.mult))
            units(6, 7)
            dve.wait_ge(pre_ready, 1)
            sq = [P, E, E]
            cmp = MSK.rearrange("p a b -> p (a b)").rearrange("p (a b) -> p a b", a=E)
            link(nc.vector.tensor_scalar(EMPTY[:, 0:E], IOTA[:, 0:E], float(P), None, ALU.mult), False)
            link(nc.vector.tensor_copy(NEXP, PVP[:, 0:E]))
            link(nc.vector.tensor_tensor(cmp, NEXP.unsqueeze(2).broadcast_to(sq),
                                         EMPTY[:, 0:E].unsqueeze(1).broadcast_to(sq), ALU.is_gt))
            link(nc.vector.tensor_reduce(KEXP, cmp, AXX, ALU.add))
            units(7, 8)
            link(nc.vector.tensor_tensor(cmp, KEXP.unsqueeze(1).broadcast_to(sq), LOWER16[:, :, :], ALU.mult))
            link(nc.vector.tensor_reduce(BASE, cmp, AXX, ALU.add))
            link(nc.vector.tensor_tensor(ENDS, BASE, KEXP, ALU.add), False)
            link(nc.vector.scalar_tensor_tensor(out=POS, in0=BASE.unsqueeze(1).broadcast_to([P, NT, E]),
                                                scalar=float(P),
                                                in1=MIS[:, 0:NT * E].rearrange("p (t e) -> p t e", t=NT),
                                                op0=ALU.mult, op1=ALU.add))
            link(nc.vector.tensor_tensor(TMJ, OHJ, POS.unsqueeze(2).broadcast_to(by_t), ALU.mult))
            link(nc.vector.tensor_reduce(PJ.rearrange("p (t j) -> p t j", j=TOPK), TMJ, AXX, ALU.add))
            units(8, 9)
            link(nc.vector.tensor_copy(PU, PJ))
            link(nc.vector.tensor_scalar(HU, PU, 7, None, ALU.logical_shift_right), False)
            link(nc.vector.tensor_scalar(LU, PU, P - 1, None, ALU.bitwise_and))
            link(nc.vector.tensor_copy(HF, HU), False)
            link(nc.vector.tensor_copy(LF, LU))

            def onehots(c):
                n = CH * TOPK
                ch = slice(c * n, (c + 1) * n)
                if c >= 2:
                    dve.wait_ge(tab_ready, c - 1)
                nc.vector.tensor_tensor(OHHI[c % 2], HF[:, ch].unsqueeze(2).broadcast_to([P, n, HI]),
                                        IOTA[:, 0:HI].unsqueeze(1).broadcast_to([P, n, HI]),
                                        ALU.is_equal).then_inc(hi_made, 1)
                link(nc.vector.tensor_tensor(OHLO[c % 2], LF[:, ch].unsqueeze(2).broadcast_to([P, n, P]),
                                             IOTA[:, :].unsqueeze(1).broadcast_to([P, n, P]), ALU.is_equal))
                units(10 + c, 11 + c)
                dve.wait_ge(hi_made, c + 1)
                nc.vector.tensor_tensor(RH[c % 2][:, :, 0:HI], OHHI[c % 2],
                                        TID1[:, :, :].rearrange("p t j -> p (t j)")[:, ch].unsqueeze(2)
                                        .broadcast_to([P, n, HI]), ALU.mult).then_inc(onehot_ready, 1)

            units(9, 10)
            for c in range(NT // CH):
                onehots(c)
            units(14, 16)
            dve.wait_ge(tab_ready, 4)
            dve.wait_ge(wprod_ready, 4)
            ends = RH[0].rearrange("p a b -> p (a b)")[:, 0:HI * E].rearrange("p (n e) -> p n e", e=E)
            link(nc.vector.tensor_tensor(ends, ENDS.unsqueeze(1).broadcast_to([P, HI, E]),
                                         IOTA[:, 0:HI].unsqueeze(2).broadcast_to([P, HI, E]), ALU.is_le))
            link(nc.vector.tensor_reduce(EOTF[:, :], ends, AXX, ALU.add))
            link(nc.vector.tensor_scalar(EOTF[:, :], EOTF[:, :], float(E - 1), None, ALU.min))
            link(nc.vector.tensor_copy(EOT[:, :], EOTF[:, :]), False)
            link(nc.vector.tensor_scalar(IDXF, PVP[:, 0:HI], -1.0, None, ALU.add), False)
            link(nc.vector.tensor_scalar(EMPTY, PVP[:, 0:HI], 0.0, PADROW[:, 0:1], ALU.is_equal, ALU.mult), False)
            link(nc.vector.tensor_copy(WT[:, :], PVP[:, HI:2 * HI]))
            link(nc.vector.tensor_tensor(IDXF, IDXF, EMPTY, ALU.add))
            link(nc.vector.tensor_copy(IDX[:, :], IDXF))
            dve.sem_inc(idx_ready, 1)
            units(16, UNITS)
            unit_out(NT - 2)
            unit_out(NT - 1)

            dve.wait_ge(sh_yused, NT)
            dve.sem_inc(xts_ready, 2)
            dve.sem_inc(g_ready, 2)
            dve.sem_inc(ys_ready, 2)

            def copy_xT(n, p):
                dve.wait_ge(xT_ready, n + 1)
                dve.wait_ge(h_ready, n + 1)
                nc.vector.tensor_copy(XTS[p], TXP[p][:, 0:D].rearrange("p (c t) -> p c t", c=KC)).then_inc(
                    xts_ready, 1)

            def product(n, p):
                dve.wait_ge(silu_ready, n + 1)
                dve.wait_ge(gT_ready, n + 1)
                weight = WT[:, n:n + 1] if isinstance(n, int) else WT[:, ds(n, 1)]
                nc.vector.scalar_tensor_tensor(out=GG[p], in0=SILU[p], scalar=weight, in1=HP[p][:, I:2 * I],
                                               op0=ALU.mult, op1=ALU.mult).then_inc(g_ready, 1)

            def result(n, k):
                dve.wait_ge(y_ready, n + 3)
                nc.vector.tensor_copy(YS[k], YP[k % 2][:, 0:D]).then_inc(ys_ready, 1)

            def tile(n):
                if n + 2 < TILES:
                    copy_xT(n + 2, n % 2)
                if n + 1 < TILES:
                    product(n + 1, (n + 1) % 2)
                if n >= 1:
                    if n >= 5:
                        dve.wait_ge(acc_done[(n - 1) % 2], 16 * ((n - 1) // 2 - 1))
                    result(n - 1, (n - 1) % 4)

            copy_xT(0, 0)
            copy_xT(1, 1)
            product(0, 0)
            for n in range(5):
                tile(n)
            rounds = (TILES - 2 - 5) // 4
            with dve.Fori(0, rounds) as i:
                for k in range(4):
                    n = 4 * i + (k + 5)
                    copy_xT(n + 2, (k + 1) % 2)
                    product(n + 1, k % 2)
                    dve.wait_ge(acc_done[k % 2], 32 * i + 16 * (1 + k // 2))
                    result(n - 1, k)
            for n in range(5 + 4 * rounds, TILES):
                tile(n)
            dve.wait_ge(acc_done[(TILES - 1) % 2], 16 * ((TILES - 1) // 2 - 1))
            result(TILES - 1, (TILES - 1) % 4)

            def shift(i):
                ts = slice(2 * i, 2 * i + 2)
                dve.wait_ge(std_ready, 3 + i)
                link(nc.vector.reciprocal(RSTD[:, ts], SD[:, ts]))
                nc.vector.scalar_tensor_tensor(out=SHIFT[:, ts], in0=MV[:, ts, 0], scalar=-1.0,
                                               in1=RSTD[:, ts], op0=ALU.mult, op1=ALU.mult).then_inc(
                                                   shift_ready, 1)

            for i in range(PIECES):
                dve.wait_ge(sum_ready, i + 1)
                for t in range(2):
                    link(nc.vector.bn_stats(ST[:, t, :], X1[:, 2 * i + t, :]), False)
                if i >= 1:
                    shift(i - 1)
                dve.wait_ge(dve_step, steps[0])
                for t in range(2):
                    link(nc.vector.bn_aggr(MV[:, 2 * i + t, :], ST[:, t, :]), False)
                dve.wait_ge(dve_step, steps[0])
                dve.sem_inc(var_ready, 1)
            shift(PIECES - 1)


def tables():
    import numpy as np
    half = HD // 2
    inv = (np.float32(1.0) / np.float32(10000.0) ** (np.arange(half, dtype=np.float32) * np.float32(2.0) /
                                                      np.float32(HD))).astype(np.float32)
    ang = np.arange(T, dtype=np.float32)[:, None] * inv[None, :]
    c, s = np.cos(ang).astype(np.float32).T, np.sin(ang).astype(np.float32).T
    cos, sin = (np.stack([np.repeat(a, H, axis=0), np.tile(np.repeat(a, G, axis=0), (NB, 1))]) for a in (c, s))
    return np.ascontiguousarray(cos), np.ascontiguousarray(sin)


def kernel(L0_attn_x, L0_attn_Wq, L0_attn_Wk, L0_attn_Wv, L0_attn_Wo, L0_ffn_gate_w, L0_ffn_W1, L0_ffn_W2,
           L0_ffn_W3, L0_ffn_Ws1, L0_ffn_Ws2, L0_ffn_Ws3):
    import numpy as np
    import concourse.bacc as bacc
    from concourse.bass_utils import run_bass_kernel_spmd

    x = np.asarray(L0_attn_x).reshape(NB * T, D)
    wq, wk, wv = (np.asarray(w) for w in (L0_attn_Wq, L0_attn_Wk, L0_attn_Wv))
    wq = wq.reshape(D, H, 2, HD // 2).transpose(0, 2, 3, 1).reshape(D, -1)
    wk = wk.reshape(D, G, 2, HD // 2).transpose(0, 2, 3, 1).reshape(D, -1)
    wqkv = np.concatenate([wq, wk, wv], axis=1)
    w13 = np.concatenate([np.asarray(L0_ffn_W1), np.asarray(L0_ffn_W3)], axis=1)
    w13 = np.concatenate([w13, np.asarray(L0_ffn_Ws1)[None], np.asarray(L0_ffn_Ws3)[None]]).transpose(2, 0, 1)
    w2 = np.asarray(L0_ffn_W2).transpose(2, 0, 1).reshape(2, IH, E, D).transpose(1, 2, 0, 3)
    cos, sin = tables()
    ins = {"x": x, "xT": x.T, "wqkv": wqkv, "wo": np.asarray(L0_attn_Wo), "cos": cos, "sin": sin,
           "gateT": np.asarray(L0_ffn_gate_w).T, "w13": w13, "w2": w2,
           "ws2": np.asarray(L0_ffn_Ws2).T}
    nc = bacc.Bacc("TRN2", target_bir_lowering=False, num_devices=1)
    arrays, args = {}, []
    for name, a in ins.items():
        arrays[f"in_{name}"] = np.ascontiguousarray(a)
        args.append(nc.dram_tensor(f"in_{name}", a.shape, mybir.dt.from_np(a.dtype), kind="ExternalInput").ap())
    args.append(nc.dram_tensor("out_x", (NB * T, D), F32, kind="ExternalOutput").ap())
    program(nc, *args)
    r = run_bass_kernel_spmd(nc, [arrays], core_ids=[0])
    return r.results[0]["out_x"].reshape(NB, T, D)
```
